# Optimizing a Trainium2 kernel written in Bass

```python
import numpy as np
import jax
import jax.numpy as jnp

def _softmax(x, axis=-1):
    return jax.nn.softmax(x, axis=axis)

def _gelu(x):
    return jax.nn.gelu(x, approximate=True)

def _silu(x):
    return jax.nn.silu(x)

def _sigmoid(x):
    return jax.nn.sigmoid(x)

def _layernorm(x, axis=-1, eps=1e-05):
    m = jnp.mean(x, axis=axis, keepdims=True)
    v = jnp.var(x, axis=axis, keepdims=True)
    return (x - m) / jnp.sqrt(v + eps)

def _scatter_add(tgt, idx, src, axis=0):
    return tgt.at[idx].add(src)

def _segment_sum(src, seg, n):
    return jax.ops.segment_sum(src, seg, n)
kernel_name = 'mk_gps_d1_gnn_r32_85af66'

def setup_inputs(seed: int=0):
    np.random.seed(seed)
    _w = jnp.asarray

    def _rec_inputs():
        import jax
        import jax.numpy as jnp
        _gk = jax.random.key(seed)
        x = -0.0002117 + 1 * jax.random.normal(jax.random.fold_in(_gk, 1), (3125, 256), jnp.float32)
        src = jax.random.randint(jax.random.fold_in(_gk, 2), (50000,), 0, 3125, jnp.int32)
        dst = jax.random.randint(jax.random.fold_in(_gk, 3), (50000,), 0, 3125, jnp.int32)
        _o = jnp.argsort(dst, stable=True)
        src = src[_o]
        dst = dst[_o]
        return (x, src, dst)
    x, src, dst = _rec_inputs()

    def _L0_gnn_setup():
        import jax, jax.numpy as jnp
        import numpy as np
        N_NODES = 3125
        N_EDGES = 50000
        NUM_CLASSES = 256
        HIDDEN = 128

        def _gcn_norm(edge_index, num_nodes):
            src, dst = (edge_index[0], edge_index[1])
            loop = jnp.arange(num_nodes, dtype=src.dtype)
            src = jnp.concatenate([src, loop])
            dst = jnp.concatenate([dst, loop])
            deg = jax.ops.segment_sum(jnp.ones_like(dst, dtype=jnp.float32), dst, num_segments=num_nodes)
            deg_inv_sqrt = jnp.where(deg > 0, jax.lax.rsqrt(deg), 0.0)
            norm = deg_inv_sqrt[src] * deg_inv_sqrt[dst]
            return (src, dst, norm)

        def _gcn_conv(x, W, b, src, dst, norm, num_nodes):
            h = x @ W
            msgs = h[src] * norm[:, None]
            out = jax.ops.segment_sum(msgs, dst, num_segments=num_nodes)
            return out + b
        key = jax.random.key(seed)
        k1, k2, k3, k4 = jax.random.split(key, 4)
        x = jax.random.normal(k1, (N_NODES, NUM_CLASSES), dtype=jnp.float32)
        edge_index = jax.random.randint(k2, (2, N_EDGES), 0, N_NODES, dtype=jnp.int32)
        W1 = jax.random.normal(k3, (NUM_CLASSES, HIDDEN), dtype=jnp.float32) / np.sqrt(NUM_CLASSES)
        b1 = jnp.zeros((HIDDEN,), dtype=jnp.float32)
        W2 = jax.random.normal(k4, (HIDDEN, NUM_CLASSES), dtype=jnp.float32) / np.sqrt(HIDDEN)
        b2 = jnp.zeros((NUM_CLASSES,), dtype=jnp.float32)
        return {'x': x, 'edge_index': edge_index, 'W1': W1, 'b1': b1, 'W2': W2, 'b2': b2}
    _L0_gnn_all = _L0_gnn_setup()
    _L0_gnn_in = {k: v for k, v in _L0_gnn_all.items() if k in ('W1', 'b1', 'W2', 'b2')}
    del _L0_gnn_all

    def _L0_mix_setup():
        import jax, jax.numpy as jnp
        import numpy as np
        DIM = 256
        HEADS = 4
        DIM_HEAD = 32
        NUM_MEM = 4
        HIDDEN = HEADS * DIM_HEAD
        SCALE = DIM_HEAD ** (-0.5)

        def rmsnorm(x, g):
            n = jnp.linalg.norm(x, axis=-1, keepdims=True)
            return x / jnp.maximum(n, 1e-12) * g * x.shape[-1] ** 0.5
        key = jax.random.key(seed)
        ks = jax.random.split(key, 8)
        B, N = (4, 512)
        return {'x': jax.random.normal(ks[0], (B, N, DIM), jnp.float32), 't': jax.random.normal(ks[1], (B,), jnp.float32), 'w_qkv': jax.random.normal(ks[2], (DIM, 3 * HIDDEN), jnp.float32) * 0.02, 'mem_kv': jax.random.normal(ks[3], (2, HEADS, DIM_HEAD, NUM_MEM), jnp.float32), 'w_out': jax.random.normal(ks[4], (HIDDEN, DIM), jnp.float32) * 0.02, 'b_out': jnp.zeros((DIM,), jnp.float32), 'g_out': jnp.ones((DIM,), jnp.float32), 'g_pre': jnp.ones((DIM,), jnp.float32)}
    _L0_mix_all = _L0_mix_setup()
    _L0_mix_in = {k: v for k, v in _L0_mix_all.items() if k in ('t', 'w_qkv', 'mem_kv', 'w_out', 'b_out', 'g_out', 'g_pre')}
    del _L0_mix_all

    def _L0_ffn_setup():
        import jax, jax.numpy as jnp
        import numpy as np
        NUM_EXPERTS = 8
        TOP_K = 2
        B, S, D = (8, 256, 256)

        def _moe(tokens, router_w, w1, b1, w2, b2):
            N = tokens.shape[0]
            E = router_w.shape[0]
            logits = tokens.astype(jnp.float32) @ router_w.astype(jnp.float32).T
            probs = jax.nn.softmax(logits, axis=-1)
            rw, re = jax.lax.top_k(probs, TOP_K)
            if TOP_K > 1:
                rw = rw / jnp.maximum(rw.sum(-1, keepdims=True), 1e-12)
            rw = rw.astype(tokens.dtype)
            combine = jnp.zeros((N, E), tokens.dtype).at[jnp.arange(N)[:, None], re].set(rw)
            out = tokens
            for e in range(E):
                h = jax.nn.gelu(tokens @ w1[e] + b1[e], approximate=False)
                y = h @ w2[e] + b2[e]
                out = out + combine[:, e:e + 1] * y
            return out
        key = jax.random.key(seed)
        ks = jax.random.split(key, 4)
        scale = 1.0 / np.sqrt(D).astype(np.float32)
        return {'input_embeddings': jax.random.normal(ks[0], (B, S, D), jnp.float32), 'router_w': jax.random.normal(ks[1], (NUM_EXPERTS, D), jnp.float32) * scale, 'w1': jax.random.normal(ks[2], (NUM_EXPERTS, D, D), jnp.float32) * scale, 'b1': jnp.zeros((NUM_EXPERTS, D), jnp.float32), 'w2': jax.random.normal(ks[3], (NUM_EXPERTS, D, D), jnp.float32) * scale, 'b2': jnp.zeros((NUM_EXPERTS, D), jnp.float32)}
    _L0_ffn_all = _L0_ffn_setup()
    _L0_ffn_in = {k: v for k, v in _L0_ffn_all.items() if k in ('router_w', 'w1', 'b1', 'w2', 'b2')}
    del _L0_ffn_all
    return {'x': x, 'src': src, 'dst': dst, 'L0_gnn_W1': _L0_gnn_in['W1'], 'L0_gnn_b1': _L0_gnn_in['b1'], 'L0_gnn_W2': _L0_gnn_in['W2'], 'L0_gnn_b2': _L0_gnn_in['b2'], 'L0_mix_t': _L0_mix_in['t'], 'L0_mix_w_qkv': _L0_mix_in['w_qkv'], 'L0_mix_mem_kv': _L0_mix_in['mem_kv'], 'L0_mix_w_out': _L0_mix_in['w_out'], 'L0_mix_b_out': _L0_mix_in['b_out'], 'L0_mix_g_out': _L0_mix_in['g_out'], 'L0_mix_g_pre': _L0_mix_in['g_pre'], 'L0_ffn_router_w': _L0_ffn_in['router_w'], 'L0_ffn_w1': _L0_ffn_in['w1'], 'L0_ffn_b1': _L0_ffn_in['b1'], 'L0_ffn_w2': _L0_ffn_in['w2'], 'L0_ffn_b2': _L0_ffn_in['b2']}

def reference(x, src, dst, L0_gnn_W1, L0_gnn_b1, L0_gnn_W2, L0_gnn_b2, L0_mix_t, L0_mix_w_qkv, L0_mix_mem_kv, L0_mix_w_out, L0_mix_b_out, L0_mix_g_out, L0_mix_g_pre, L0_ffn_router_w, L0_ffn_w1, L0_ffn_b1, L0_ffn_w2, L0_ffn_b2):
    import jax
    import jax.numpy as jnp

    def _L0_gnn_ref(x, edge_index, W1, b1, W2, b2):
        import jax, jax.numpy as jnp
        import numpy as np
        N_NODES = 3125
        N_EDGES = 50000
        NUM_CLASSES = 256
        HIDDEN = 128

        def _gcn_norm(edge_index, num_nodes):
            src, dst = (edge_index[0], edge_index[1])
            loop = jnp.arange(num_nodes, dtype=src.dtype)
            src = jnp.concatenate([src, loop])
            dst = jnp.concatenate([dst, loop])
            deg = jax.ops.segment_sum(jnp.ones_like(dst, dtype=jnp.float32), dst, num_segments=num_nodes)
            deg_inv_sqrt = jnp.where(deg > 0, jax.lax.rsqrt(deg), 0.0)
            norm = deg_inv_sqrt[src] * deg_inv_sqrt[dst]
            return (src, dst, norm)

        def _gcn_conv(x, W, b, src, dst, norm, num_nodes):
            h = x @ W
            msgs = h[src] * norm[:, None]
            out = jax.ops.segment_sum(msgs, dst, num_segments=num_nodes)
            return out + b
        n = x.shape[0]
        src, dst, norm = _gcn_norm(edge_index, n)
        h = jax.nn.relu(_gcn_conv(x, W1, b1, src, dst, norm, n))
        out = _gcn_conv(h, W2, b2, src, dst, norm, n)
        return out

    def _L0_mix_ref(x, t, w_qkv, mem_kv, w_out, b_out, g_out, g_pre):
        import jax, jax.numpy as jnp
        import numpy as np
        DIM = 256
        HEADS = 4
        DIM_HEAD = 32
        NUM_MEM = 4
        HIDDEN = HEADS * DIM_HEAD
        SCALE = DIM_HEAD ** (-0.5)

        def rmsnorm(x, g):
            n = jnp.linalg.norm(x, axis=-1, keepdims=True)
            return x / jnp.maximum(n, 1e-12) * g * x.shape[-1] ** 0.5
        b, n, c = x.shape
        xn = rmsnorm(x, g_pre)
        qkv = xn @ w_qkv
        q, k, v = jnp.split(qkv, 3, axis=-1)

        def to_heads(z):
            return z.reshape(b, n, HEADS, DIM_HEAD).transpose(0, 2, 3, 1)
        q, k, v = map(to_heads, (q, k, v))
        mk = jnp.broadcast_to(mem_kv[0], (b, HEADS, DIM_HEAD, NUM_MEM))
        mv = jnp.broadcast_to(mem_kv[1], (b, HEADS, DIM_HEAD, NUM_MEM))
        k = jnp.concatenate([mk, k], axis=-1)
        v = jnp.concatenate([mv, v], axis=-1)
        q = jax.nn.softmax(q, axis=-2) * SCALE
        k = jax.nn.softmax(k, axis=-1)
        context = jnp.einsum('bhdn,bhen->bhde', k, v)
        out = jnp.einsum('bhde,bhdn->bhen', context, q)
        out = out.transpose(0, 3, 1, 2).reshape(b, n, HIDDEN)
        out = rmsnorm(out @ w_out + b_out, g_out)
        return out + x

    def _L0_ffn_ref(input_embeddings, router_w, w1, b1, w2, b2):
        import jax, jax.numpy as jnp
        import numpy as np
        NUM_EXPERTS = 8
        TOP_K = 2
        B, S, D = (8, 256, 256)

        def _moe(tokens, router_w, w1, b1, w2, b2):
            N = tokens.shape[0]
            E = router_w.shape[0]
            logits = tokens.astype(jnp.float32) @ router_w.astype(jnp.float32).T
            probs = jax.nn.softmax(logits, axis=-1)
            rw, re = jax.lax.top_k(probs, TOP_K)
            if TOP_K > 1:
                rw = rw / jnp.maximum(rw.sum(-1, keepdims=True), 1e-12)
            rw = rw.astype(tokens.dtype)
            combine = jnp.zeros((N, E), tokens.dtype).at[jnp.arange(N)[:, None], re].set(rw)
            out = tokens
            for e in range(E):
                h = jax.nn.gelu(tokens @ w1[e] + b1[e], approximate=False)
                y = h @ w2[e] + b2[e]
                out = out + combine[:, e:e + 1] * y
            return out
        b, s, d = input_embeddings.shape
        tokens = input_embeddings.reshape(b * s, d)
        return _moe(tokens, router_w, w1, b1, w2, b2).reshape(b, s, d)
    edge_index = jnp.stack([src, dst])
    xn = _layernorm(x, axis=-1)
    x = x + _L0_gnn_ref(xn, edge_index, L0_gnn_W1, L0_gnn_b1, L0_gnn_W2, L0_gnn_b2) + _L0_mix_ref(xn[None], L0_mix_t, L0_mix_w_qkv, L0_mix_mem_kv, L0_mix_w_out, L0_mix_b_out, L0_mix_g_out, L0_mix_g_pre)[0]
    x = x + _L0_ffn_ref(_layernorm(x, axis=-1)[None], L0_ffn_router_w, L0_ffn_w1, L0_ffn_b1, L0_ffn_w2, L0_ffn_b2)[0]
    return x

_drawn_inputs = setup_inputs


def setup_inputs(seed=0):
    import zlib

    import numpy as np

    out = dict(_drawn_inputs(seed))
    spreads = {'L0_gnn_b1': (0.0, 0.297),
     'L0_gnn_b2': (0.0, 0.1),
     'L0_mix_b_out': (0.0, 0.1),
     'L0_mix_g_out': (1.0, 0.2),
     'L0_mix_g_pre': (1.0, 0.6),
     'L0_ffn_b1': (0.0, 0.522),
     'L0_ffn_b2': (0.0, 0.353)}
    factors = {'L0_mix_w_qkv': 8.0, 'L0_mix_mem_kv': 8.0, 'L0_mix_w_out': 8.0}
    for name, (base, spread) in spreads.items():
        noise = np.random.default_rng([zlib.crc32(name.encode()), seed]).standard_normal(out[name].shape)
        drawn = base * np.exp(spread * noise) if base else spread * noise
        out[name] = jnp.asarray(drawn.astype(out[name].dtype))
    for name, factor in factors.items():
        out[name] = (out[name] * factor).astype(out[name].dtype)
    return out
```

```python
from contextlib import ExitStack

import concourse.bass as bass
from concourse import mybir

ALU = mybir.AluOpType
ACT = mybir.ActivationFunctionType
AX = mybir.AxisListType
F32 = mybir.dt.float32
BF16 = mybir.dt.bfloat16
F16 = mybir.dt.float16
I32 = mybir.dt.int32

P = 128
NODES, DIM, HID, EDGES = 3125, 256, 128, 50000
HEADS, HEAD_DIM, MEM = 4, 32, 4
EXPERTS = 8
W = 5
PT = 125
C = 5
SLOTS = C * W
WINDOWS = NODES // W
EDGE_TILES = -(-EDGES // P)
TCH = -(-EDGE_TILES // P)
TLAST = EDGE_TILES - (TCH - 1) * P
STEPS = 1024
CH = STEPS // P
KEYS = SLOTS * W
NO_NODE = 4000
NO_KEY = 1000.0
UNIT = 8
GROUP = 4
GROUPS = P // GROUP
QKV = 3 * HID
assert EDGE_TILES + WINDOWS - 1 <= STEPS and SLOTS * PT == NODES


class Steps:

    def __init__(self, eng, sem):
        self.eng, self.sem, self.n, self.base = eng, sem, 0, 0

    def did(self, ins):
        ins.then_inc(self.sem, 1)
        self.n += 1

    def wait(self):
        self.eng.wait_ge(self.sem, self.base + self.n)

    def enter(self, i, per):
        self.start, self.per, self.base = self.n, per, i * per

    def leave(self, count):
        assert self.n - self.start == self.per, (self.n - self.start, self.per)
        self.n, self.base = self.start + count * self.per, 0


def gps_layer(nc, x, src, dst, gnn_w1, gnn_b1, gnn_w2, gnn_b2, w_qkv, mem_kv, w_out, b_out, g_out,
              g_pre, router_w, moe_w1, moe_b1, moe_w2, moe_b2, out, dbg=None):
    ctx = ExitStack()
    with ctx:
        def sb(name, shape, dt, scope=ctx):
            return scope.enter_context(nc.sbuf_tensor(name, shape, dt))

        def sem(name):
            return ctx.enter_context(nc.semaphore(name))

        psA, psB, psC, psD = (ctx.enter_context(nc.psum_tensor(f"ps{n}", [P, 1024], F32)) for n in "ABCD")

        ident = sb("ident", [P, P], F32)
        ident_row = sb("ident_row", [P, P], F32)
        ident_col = sb("ident_col", [P, 1], F32)
        iota_j = sb("iota_j", [P, P, GROUP], BF16)
        iota_s = sb("iota_s", [P, STEPS], F16)
        t_of = sb("t_of", [P, TCH], F32)
        s_of = sb("s_of", [P, CH], F32)
        t_of16 = sb("t_of16", [P, TCH], F16)
        ones16 = sb("ones16", [P, 1], BF16)
        acc = sb("acc", [P, SLOTS, DIM], F32)
        hs = sb("hs", [P, SLOTS, HID], F32)
        dinv = sb("dinv", [P, SLOTS], F32)
        key = sb("key", [P, STEPS + P], BF16)
        brow = sb("brow", [P, STEPS + P], BF16)
        sel = sb("sel", [P, CH, WINDOWS], BF16)
        b1_all = sb("b1_all", [P, HID], F32)
        b2_all = sb("b2_all", [P, DIM], F32)
        bout_all = sb("bout_all", [P, DIM], F32)
        gout_all = sb("gout_all", [P, DIM], F32)
        w2g = sb("w2g", [P, DIM], F32)
        stats = sb("stats", [P, SLOTS, 6], F32)
        mv = sb("mv", [P, SLOTS, 2], F32)
        rstd = sb("rstd", [P, SLOTS], F32)
        small = sb("small", [P, 4, SLOTS], F32)
        wr = sb("wr", [P, 2, EXPERTS], F32)
        rw_nat = sb("rw_nat", [EXPERTS, DIM], F32)
        eb2 = sb("eb2", [EXPERTS, DIM], F32)
        eb1_nat = sb("eb1_nat", [2 * EXPERTS, P], F32)
        eb1 = sb("eb1", [P, 2 * EXPERTS], F32)
        comb = sb("comb", [P, SLOTS, EXPERTS], F32)

        with ExitStack() as st:
            e_dst = sb("e_dst", [P, TCH, P], I32, st)
            e_src = sb("e_src", [P, TCH, P], I32, st)
            prev_dst = sb("prev_dst", [P, TCH], I32, st)
            dst_w = sb("dst_w", [P, TCH, P], I32, st)
            src_w = sb("src_w", [P, TCH, P], I32, st)
            src_c = sb("src_c", [P, TCH, P], I32, st)
            prev_w = sb("prev_w", [P, TCH], I32, st)
            src_d = sb("src_d", [P, TCH, P], F32, st)
            src_slot = sb("src_slot", [P, TCH, P], F32, st)
            q_r = sb("q_r", [P, TCH, P], F16, st)
            q_wt = sb("q_wt", [P, TCH, P], F16, st)
            q_b = sb("q_b", [P, TCH, P], F16, st)
            q_key = sb("q_key", [P, TCH, P], F16, st)
            t_lo = sb("t_lo", [P, TCH], F32, st)
            t_hi = sb("t_hi", [P, TCH], F32, st)
            past = sb("past", [P, TCH, STEPS], F16, st)
            tile_at = sb("tile_at", [P, TCH, STEPS], F16, st)
            outside = sb("outside", [P, STEPS], BF16, st)
            r_in = sb("r_in", [P, STEPS], BF16, st)
            r_hot = sb("r_hot", [P, W, STEPS], BF16, st)
            w_of_s = sb("w_of_s", [P, CH], F32, st)
            cnt = sb("cnt", [P, CH * W], BF16, st)
            xn = sb("xn", [P, SLOTS, DIM], F32, st)
            qkv = sb("qkv", [P, SLOTS, QKV + 1], F32, st)
            xnT = sb("xnT", [P, 2, 2, PT], F32, st)
            wcat = sb("wcat", [P, 2, HID + QKV], F32, st)
            gpre = sb("gpre", [P, 2], F32, st)
            junk = sb("junk", [P, DIM], F32, st)
            mem_v = sb("mem_v", [P, MEM], F32, st)
            mem_k = sb("mem_k", [P, MEM], F32, st)
            memkT = sb("memkT", [MEM, P], F32, st)
            memvT = sb("memvT", [MEM, P + 1], F32, st)
            kmax = sb("kmax", [P, HID], F32, st)
            kmax_col = sb("kmax_col", [P, 2], F32, st)
            kmax_mat = sb("kmax_mat", [P, P], F32, st)
            qred = sb("qred", [P, SLOTS * HEADS], F32, st)
            ctx_sb = sb("ctx_sb", [P, P + 1], F32, st)
            ctx_m = sb("ctx_m", [P, P], F32, st)
            ctxT = sb("ctxT", [P, P], F32, st)
            wmix = sb("wmix", [P, DIM], F32, st)
            zinv = sb("zinv", [P, 1], F32, st)
            wout = sb("wout", [P, DIM], F32, st)
            qT = sb("qT", [P, 2, PT], F32, st)
            mix = qkv[:, :, HID:QKV]

        with ExitStack() as st:
            counts = sb("counts", [P, 2, KEYS, P], BF16, st)
            hs3 = sb("hs3", [P, SLOTS, 3, HID], BF16, st)
            hot_b = sb("hot_b", [P, 2, 2, P, GROUP], BF16, st)
            hot_k = sb("hot_k", [P, 2, 2, KEYS, GROUP], BF16, st)
            part3 = sb("part3", [P, 3, CH, W * HID], BF16, st)
            rest = sb("rest", [P, 2, W * HID], F32, st)
            post = sb("post", [P, W * HID], F32, st)
            aggT = sb("aggT", [P, W, P], F32, st)

        with ExitStack() as st:
            tok = sb("tok", [P, SLOTS, DIM], F32, st)
            tokT = sb("tokT", [P, 2, SLOTS * PT], F32, st)
            ew1 = sb("ew1", [P, EXPERTS, 2, DIM], F32, st)
            ew2 = sb("ew2", [P, EXPERTS, 2, DIM], F32, st)
            hT = sb("hT", [P, 2, 2, 4 * PT], F32, st)
            logit = sb("logit", [P, SLOTS, EXPERTS], F32, st)
            top = sb("top", [P, SLOTS, 8], F32, st)
            topi = sb("topi", [P, SLOTS, 8], mybir.dt.uint32, st)
            pick = sb("pick", [P, 2, SLOTS, EXPERTS], F32, st)
            prob = sb("prob", [P, SLOTS, EXPERTS], F32, st)
            combT = sb("combT", [EXPERTS, SLOTS * PT], F32, st)

        pads = sem("pads")
        consts = sem("consts")
        in_edges = sem("in_edges")
        in_x = sem("in_x")
        in_w = sem("in_w")
        in_moe = sem("in_moe")
        v_ = sem("vector_steps")
        a_ = sem("scalar_steps")
        ident_ok = sem("ident_ok")
        q_ready = sem("q_ready")
        q_spread = sem("q_spread")
        q_used = sem("q_used")
        rhot_ok = sem("rhot_ok")
        sel_ok = sem("sel_ok")
        cnt_in = sem("cnt_in")
        cnt_ok = sem("cnt_ok")
        deg_in = sem("deg_in")
        deg_ok = sem("deg_ok")
        dsq_ok = sem("dsq_ok")
        dinv_ok = sem("dinv_ok")
        var_ok = sem("var_ok")
        std_ok = sem("std_ok")
        xn_ok = sem("xn_ok")
        ss_ok = sem("ss_ok")
        g16_ok = sem("g16_ok")
        wcat_ok = sem("wcat_ok")
        xt_in = sem("xt_in")
        xt_ok = sem("xt_ok")
        proj = sem("proj")
        proj_h = sem("proj_h")
        proj_q = sem("proj_q")
        km_ok = sem("km_ok")
        mixpe = sem("mixpe")
        mixdve = sem("mixdve")
        mixact = sem("mixact")
        qs_ok = sem("qs_ok")
        qt_in = sem("qt_in")
        qt_ok = sem("qt_ok")
        mo_in = sem("mo_in")
        mo_ok = sem("mo_ok")
        mss_ok = sem("mss_ok")
        mixdone = sem("mixdone")
        xadd_ok = sem("xadd_ok")
        hs3_ok = sem("hs3_ok")
        hot_ready = sem("hot_ready")
        built = sem("built")
        counts_ok = sem("counts_ok")
        summed = sem("summed")
        hi_ok = sem("hi_ok")
        sums_free = sem("sums_free")
        mid_ok = sem("mid_ok")
        tok_ok = sem("tok_ok")
        wr_in = sem("wr_in")
        wr_ok = sem("wr_ok")
        logit_in = sem("logit_in")
        lg_ok = sem("lg_ok")
        ex_ok = sem("ex_ok")
        comb_ok = sem("comb_ok")
        eb_in = sem("eb_in")
        eb_ok = sem("eb_ok")
        tt_in = sem("tt_in")
        tt_ok = sem("tt_ok")
        ct_in = sem("ct_in")
        ct_ok = sem("ct_ok")
        upped = sem("upped")
        gelu = sem("gelu")
        down = sem("down")
        y_free = sem("y_free")
        lo_ok = sem("lo_ok")
        merged = sem("merged")
        merge_used = sem("merge_used")
        hs_ok = sem("hs_ok")
        hs_hi = sem("hs_hi")
        hs_rest = sem("hs_rest")
        post_ok = sem("post_ok")
        at_in = sem("at_in")
        at_ok = sem("at_ok")
        g2_in = sem("g2_in")
        g2_ok = sem("g2_ok")
        s_out = sem("s_out")
        s_dbg = sem("s_dbg")
        locals_ = dict(locals())

        block = ctx.enter_context(nc.Block())

        x_v = x.rearrange("(c p m) f -> p c (m f)", p=PT, m=W)
        acc_v = acc[:, :, :].rearrange("p (c m) f -> p c (m f)", m=W)

        @block.sync
        def _(sp):
            full = (TCH - 1) * P
            n_last = EDGES // P - full
            tail = EDGES - (EDGES // P) * P
            sp.wait_ge(pads, 3)
            for e_sb, e in ((e_dst, dst), (e_src, src)):
                sp.dma_start(e_sb[:, 0:TCH - 1, :], e[0:full * P].rearrange("(c p e) -> p c e", p=P, e=P)).then_inc(in_edges, 16)
                sp.dma_start(e_sb[0:n_last, TCH - 1, :], e[full * P:(full + n_last) * P].rearrange("(p e) -> p e", e=P)).then_inc(in_edges, 16)
                sp.dma_start(e_sb[n_last:n_last + 1, TCH - 1, 0:tail], e[(full + n_last) * P:EDGES].rearrange("(p e) -> p e", p=1)).then_inc(in_edges, 16)
            ends = dst[0:(EDGES // P) * P].rearrange("(t e) -> t e", e=P)[:, P - 1:P]
            sp.dma_start(prev_dst[1:P, 0:1], ends[0:P - 1, :], allow_slow_non_contiguous=True).then_inc(in_edges, 16)
            for c in range(1, TCH):
                k = P if c < TCH - 1 else TLAST
                sp.dma_start(prev_dst[0:k, c:c + 1], ends[c * P - 1:c * P - 1 + k, :],
                             allow_slow_non_contiguous=True).then_inc(in_edges, 16)
            for lo, hi in ((0, 112), (112, PT)):
                sp.dma_start(acc_v[lo:hi], x_v[lo:hi]).then_inc(in_x, 16)
            loads = [
                (wcat[:, :, 0:HID], gnn_w1.rearrange("(k p) f -> p k f", p=P)),
                (wcat[:, :, HID:HID + QKV], w_qkv.rearrange("(k p) f -> p k f", p=P)),
                (mem_k[:, :], mem_kv[0].rearrange("h d m -> (h d) m")),
                (mem_v[:, :], mem_kv[1].rearrange("h d m -> (h d) m")),
                (wout[:, :], w_out),
                (w2g[:, :], gnn_w2),
                (b1_all[:, :], gnn_b1.rearrange("(a f) -> a f", a=1).to_broadcast([P, HID])),
                (b2_all[:, :], gnn_b2.rearrange("(a f) -> a f", a=1).to_broadcast([P, DIM])),
                (bout_all[:, :], b_out.rearrange("(a f) -> a f", a=1).to_broadcast([P, DIM])),
                (gout_all[:, :], g_out.rearrange("(a f) -> a f", a=1).to_broadcast([P, DIM])),
                (gpre[:, 0:1], g_pre[0:P].rearrange("(p a) -> p a", a=1)),
                (gpre[:, 1:2], g_pre[P:DIM].rearrange("(p a) -> p a", a=1)),
                (rw_nat[:, :], router_w),
                (eb2[:, :], moe_b2),
                (eb1_nat[:, :], moe_b1.rearrange("e (h p) -> (e h) p", p=P)),
            ]
            for to, frm in loads:
                sp.dma_start(to, frm).then_inc(in_w, 16)
            assert len(loads) == 15
            sp.wait_ge(merged, 2 * C)
            sp.wait_ge(at_in, C)
            sp.wait_ge(g2_in, C)
            for to, w in ((ew1, moe_w1), (ew2, moe_w2)):
                sp.dma_start(to[:, :, :, :].rearrange("p e k f -> p (e k) f"), w.rearrange("e (k p) f -> p (e k) f", p=P)).then_inc(in_moe, 16)
            out_v = out.rearrange("(c p m) f -> p c (m f)", p=PT, m=W)
            sp.wait_ge(y_free, 2 + 7 * EXPERTS)
            for lo, hi in ((0, 112), (112, PT)):
                sp.dma_start(out_v[lo:hi], acc_v[lo:hi]).then_inc(s_out, 16)
            sp.wait_ge(s_out, 32)
            if dbg:
                for n, (wait, ap, to) in enumerate(dbg(locals_)):
                    if n == 0:
                        sp.wait_ge(*wait)
                    sp.dma_start(to, ap).then_inc(s_dbg, 16)
                sp.wait_ge(s_dbg, 16 * (n + 1))
        IN_W = 16 * 15
        IN_EDGES = 16 * 10

        @block.gpsimd
        def _(pool):
            pool.memset(e_dst[:, TCH - 1, :], NO_NODE).then_inc(pads, 1)
            pool.memset(e_src[:, TCH - 1, :], 0).then_inc(pads, 1)
            pool.memset(prev_dst[:, :], 0).then_inc(pads, 1)
            kw = dict(allow_small_or_imprecise_dtypes=True)
            pool.iota(t_of[:, :], [[P, TCH]], base=0, channel_multiplier=1, **kw).then_inc(consts, 1)
            pool.iota(iota_s[:, :], [[1, STEPS]], base=0, channel_multiplier=0, **kw).then_inc(consts, 1)
            pool.iota(t_of16[:, :], [[P, TCH]], base=0, channel_multiplier=1, **kw).then_inc(consts, 1)
            pool.iota(s_of[:, :], [[P, CH]], base=0, channel_multiplier=1, **kw).then_inc(consts, 1)
            pool.iota(ident_row[:, :], [[1, P]], base=0, channel_multiplier=0, **kw).then_inc(consts, 1)
            pool.iota(ident_col[:, :], [[0, 1]], base=0, channel_multiplier=1, **kw).then_inc(consts, 1)
            pool.iota(iota_j[:, :, :], [[1, P], [0, GROUP]], base=0, channel_multiplier=0, **kw).then_inc(consts, 1)
            pool.memset(ones16[:, :], 1.0).then_inc(consts, 1)

            pool.nop().then_inc(lo_ok, 2)

            def hs_parts(c, n, mids):
                sl = bass.ds(W * c, W)
                r = rest[0:PT, 0, :].rearrange("p (d f) -> p d f", d=W)
                pool.wait_ge(hs_rest, n + 1)
                pool.tensor_copy(hs3[0:PT, sl, 1, :], r).then_inc(mid_ok, 1)
                pool.wait_ge(mid_ok, mids + 1)
                pool.tensor_tensor(hs3[0:PT, sl, 2, :], r, hs3[0:PT, sl, 1, :], ALU.subtract).then_inc(hs3_ok, 1)

            with pool.Fori(0, C) as c:
                hs_parts(c, c, c)
            for layer in range(2):
                k0, m0 = CH * layer, C + (CH + C) * layer
                with pool.Fori(0, CH // 2) as kp:
                    for par in range(2):
                        mid, low = (part3[:, part, bass.ds(2 * kp + par, 1), :].rearrange("p a f -> p (a f)") for part in (1, 2))
                        pool.wait_ge(sums_free, 2 * kp + (k0 + par + 3))
                        pool.tensor_copy(mid, rest[:, par, :]).then_inc(mid_ok, 1)
                        pool.wait_ge(mid_ok, 2 * kp + (m0 + par + 1))
                        pool.tensor_tensor(low, rest[:, par, :], mid, ALU.subtract).then_inc(lo_ok, 1)
                if layer == 0:
                    with pool.Fori(0, C) as c:
                        hs_parts(c, c + C, c + (C + CH))

        CONSTS = 8

        @block.vector
        def _(v):
            st = Steps(v, v_)

            v.wait_ge(in_edges, IN_EDGES)
            v.wait_ge(consts, CONSTS)
            st.did(v.tensor_scalar(dst_w[:], e_dst[:], 1.0 / W, -0.4, ALU.mult, ALU.add))
            st.did(v.tensor_scalar(src_w[:], e_src[:], 1.0 / W, -0.4, ALU.mult, ALU.add))
            st.did(v.tensor_scalar(prev_w[:], prev_dst[:], 1.0 / W, -0.4, ALU.mult, ALU.add))
            v.tensor_scalar(ident[:], ident_row[:], ident_col[:], None, ALU.is_equal).then_inc(ident_ok, 1)
            st.wait()
            st.did(v.scalar_tensor_tensor(q_r[:], dst_w[:], -float(W), e_dst[:], ALU.mult, ALU.add))
            st.did(v.tensor_tensor(q_wt[:], dst_w[:], t_of[:, :].unsqueeze(2).to_broadcast([P, TCH, P]), ALU.add))
            st.did(v.scalar_tensor_tensor(src_d[:], src_w[:], -float(W), e_src[:], ALU.mult, ALU.add))
            st.did(v.tensor_scalar(src_c[:], src_w[:], 1.0 / PT, 0.5 / PT - 0.5, ALU.mult, ALU.add))
            st.did(v.tensor_tensor(t_lo[:], prev_w[:], t_of[:], ALU.add))
            st.did(v.scalar_tensor_tensor(t_hi[:], dst_w[:, :, P - 1], 1.0, t_of[:], ALU.add, ALU.add))
            st.wait()
            st.did(v.scalar_tensor_tensor(q_b[:], src_c[:], -float(PT), src_w[:], ALU.mult, ALU.add))
            st.did(v.scalar_tensor_tensor(src_slot[:], src_c[:], float(W), src_d[:], ALU.mult, ALU.add))
            for c in range(TCH):
                st.did(v.tensor_scalar(past[:, c, :], iota_s[:], t_lo[:, c:c + 1], None, ALU.is_ge))
            st.wait()
            st.did(v.scalar_tensor_tensor(q_key[:], src_slot[:], float(W), q_r[:], ALU.mult, ALU.add))
            for c in range(TCH):
                st.did(v.scalar_tensor_tensor(tile_at[:, c, :], iota_s[:], t_hi[:, c:c + 1], past[:, c, :], ALU.is_lt, ALU.mult))
            st.wait()
            v.nop().then_inc(q_ready, 1)

            v.wait_ge(q_spread, 1)
            v.tensor_tensor(outside[:], psA[:], iota_s[:], ALU.not_equal).then_inc(q_used, 1)
            v.wait_ge(q_used, 1)
            v.wait_ge(q_spread, 2)
            v.scalar_tensor_tensor(r_in[:], outside[:], NO_KEY, psB[:], ALU.mult, ALU.add).then_inc(q_used, 1)
            v.wait_ge(q_spread, 3)
            v.scalar_tensor_tensor(key[:, 0:STEPS], outside[:], NO_KEY, psC[:], ALU.mult, ALU.add).then_inc(q_used, 1)
            v.wait_ge(q_spread, 4)
            v.tensor_copy(brow[:, 0:STEPS], psD[:]).then_inc(q_used, 1)
            v.wait_ge(q_used, 4)
            st.did(v.tensor_copy(key[:, STEPS:STEPS + P], key[:, 0:P]))
            st.did(v.tensor_copy(brow[:, STEPS:STEPS + P], brow[:, 0:P]))
            for d in range(W):
                v.tensor_scalar(r_hot[:, d, :], r_in[:], float(d), None, ALU.is_equal).then_inc(rhot_ok, 1)
            v.wait_ge(q_spread, 5)
            st.did(v.tensor_tensor(w_of_s[:], s_of[:], psA[:, 0:CH], ALU.subtract))
            st.wait()
            for k in range(CH):
                v.tensor_scalar(sel[:, k, :], iota_s[:, 0:WINDOWS], w_of_s[:, k:k + 1], None, ALU.is_equal).then_inc(sel_ok, 1)
            v.wait_ge(cnt_in, 1)
            v.tensor_copy(cnt[:], psA[:, 64:64 + CH * W]).then_inc(cnt_ok, 1)
            v.wait_ge(deg_in, 1)
            v.tensor_scalar(small[0:PT, 0, :], psA[0:PT, 128:128 + SLOTS], 1.0, None, ALU.add).then_inc(deg_ok, 1)
            v.wait_ge(dsq_ok, 1)
            v.reciprocal(dinv[0:PT, :], small[0:PT, 1, :]).then_inc(dinv_ok, 1)

            v.wait_ge(in_x, 32)
            for n in range(SLOTS):
                st.did(v.bn_stats(stats[0:PT, n, :], acc[0:PT, n, :]))
            st.wait()
            for n in range(SLOTS):
                st.did(v.bn_aggr(mv[0:PT, n, :], stats[0:PT, n, :]))
            st.wait()
            v.tensor_scalar(small[0:PT, 2, :], mv[0:PT, :, 1], 1e-5, None, ALU.add).then_inc(var_ok, 1)
            v.wait_ge(std_ok, 1)
            st.did(v.reciprocal(rstd[0:PT, :], small[0:PT, 3, :]))
            st.wait()
            for n in range(SLOTS):
                v.tensor_scalar(xn[0:PT, n, :], acc[0:PT, n, :], mv[0:PT, n, 0:1], rstd[0:PT, n:n + 1],
                                ALU.subtract, ALU.mult).then_inc(xn_ok, 1)
            v.wait_ge(in_w, IN_W)
            for k in range(2):
                v.tensor_scalar(wcat[:, k, HID:HID + QKV], wcat[:, k, HID:HID + QKV], gpre[:, k:k + 1], None,
                                ALU.mult).then_inc(wcat_ok, 1)
            v.wait_ge(ss_ok, 1)
            st.did(v.tensor_scalar(small[0:PT, 1, :], small[0:PT, 1, :], 1e-12, 1.0 / DIM ** 0.5, ALU.max, ALU.mult))
            st.wait()
            v.reciprocal(small[0:PT, 0, :], small[0:PT, 1, :]).then_inc(g16_ok, 1)
            v.wait_ge(dinv_ok, 1)
            for n in range(SLOTS):
                v.wait_ge(proj, n + 1)
                v.tensor_scalar(hs[0:PT, n, :], psC[0:PT, 512 * (n % 2):512 * (n % 2) + HID], dinv[0:PT, n:n + 1], None,
                                ALU.mult).then_inc(proj_h, 1)

            v.wait_ge(proj_q, SLOTS)
            v.tensor_reduce(kmax[0:PT, :], qkv[0:PT, :, HID:2 * HID].rearrange("p n f -> p f n"), AX.X, ALU.max).then_inc(mixdve, 1)
            v.tensor_reduce(kmax_col[:, 1:2], mem_k[:], AX.X, ALU.max).then_inc(mixdve, 1)
            v.wait_ge(mixpe, 1)
            st.did(v.tensor_reduce(kmax_col[:, 0:1], psA[:, 0:PT], AX.X, ALU.max))
            v.wait_ge(mixdve, 2)
            st.wait()
            st.did(v.tensor_tensor(kmax_col[:, 0:1], kmax_col[:, 0:1], kmax_col[:, 1:2], ALU.max))
            st.wait()
            v.tensor_scalar(kmax_mat[:], ident[:], 0.0, kmax_col[:, 0:1], ALU.mult, ALU.add).then_inc(mixdve, 1)
            qv = qkv[0:PT, :, 0:HID].rearrange("p n (h d) -> p n h d", h=HEADS)
            qr = qred[0:PT, :].rearrange("p (n h) -> p n h", h=HEADS)
            qr_b = qr.unsqueeze(3).to_broadcast([PT, SLOTS, HEADS, HEAD_DIM])
            st.did(v.tensor_reduce(qr, qv, AX.X, ALU.max))
            st.wait()
            v.tensor_tensor(qv, qv, qr_b, ALU.subtract).then_inc(qs_ok, 1)
            v.wait_ge(mixpe, 2)
            kv_ = qkv[0:PT, :, HID:2 * HID]
            v.tensor_tensor(kv_, kv_, psA[0:PT, 256:256 + HID].unsqueeze(1).to_broadcast([PT, SLOTS, HID]),
                            ALU.subtract).then_inc(mixdve, 1)
            v.tensor_copy(memvT[:, 0:P], psB[0:MEM, 256:256 + P]).then_inc(mixdve, 1)
            st.did(v.tensor_copy(memkT[:], psB[0:MEM, 0:P]))
            st.wait()
            v.tensor_tensor(memkT[:], memkT[:], psA[0:MEM, 256:256 + HID], ALU.subtract).then_inc(mixdve, 1)
            v.memset(memvT[:, P:P + 1], 1.0).then_inc(mixdve, 1)
            v.memset(ctx_m[:], 0.0).then_inc(mixdve, 1)
            v.memset(qkv[0:PT, :, QKV:QKV + 1], 1.0).then_inc(mixdve, 1)
            v.wait_ge(mixact, 1)
            st.did(v.tensor_reduce(qr, qv, AX.X, ALU.add))
            st.wait()
            st.did(v.reciprocal(qred[0:PT, :], qred[0:PT, :]))
            st.wait()
            v.tensor_tensor(qv, qv, qr_b, ALU.mult).then_inc(qs_ok, 1)
            v.wait_ge(mixpe, 3)
            st.did(v.tensor_copy(ctx_sb[:], psB[:, 512:512 + P + 1]))
            st.wait()
            st.did(v.reciprocal(zinv[:], ctx_sb[:, P:P + 1]))
            st.wait()
            v.wait_ge(mixdve, 9)
            for h in range(HEADS):
                s = slice(h * HEAD_DIM, (h + 1) * HEAD_DIM)
                v.tensor_scalar(ctx_m[s, s], ctx_sb[s, s], zinv[s, :], HEAD_DIM ** -0.5, ALU.mult, ALU.mult).then_inc(mixdve, 1)
            v.wait_ge(mixpe, 4)
            v.tensor_copy(ctxT[:], psB[:, 0:P]).then_inc(mixdve, 1)
            v.wait_ge(mixpe, 5)
            v.tensor_copy(wmix[:], psB[:, 256:256 + DIM]).then_inc(mixdve, 1)
            for n in range(SLOTS):
                v.wait_ge(mo_in, n + 1)
                v.tensor_tensor(mix[0:PT, n, :], psC[0:PT, 512 * (n % 2):512 * (n % 2) + DIM], bout_all[0:PT, :], ALU.add).then_inc(mo_ok, 1)
            v.wait_ge(mss_ok, 1)
            st.did(v.tensor_scalar(small[0:PT, 3, :], small[0:PT, 3, :], 1e-12, 1.0 / DIM ** 0.5, ALU.max, ALU.mult))
            st.wait()
            st.did(v.reciprocal(small[0:PT, 2, :], small[0:PT, 3, :]))
            st.wait()
            for n in range(SLOTS):
                st.did(v.scalar_tensor_tensor(mix[0:PT, n, :], mix[0:PT, n, :], small[0:PT, 2, n:n + 1], gout_all[0:PT, :], ALU.mult, ALU.mult))
            st.did(v.tensor_tensor(acc[0:PT], acc[0:PT], xn[0:PT], ALU.add))
            st.wait()
            st.did(v.tensor_tensor(acc[0:PT], acc[0:PT], mix[0:PT], ALU.add))
            st.wait()
            v.tensor_tensor(acc[0:PT], acc[0:PT], b2_all[0:PT, :].unsqueeze(1).to_broadcast([PT, SLOTS, DIM]), ALU.add).then_inc(mixdone, 1)

            def hot_unit(slot, column):
                cols = bass.ds(column, UNIT)
                for hot, n, val in ((hot_b, P, brow), (hot_k, KEYS, key)):
                    v.tensor_tensor(hot[:, slot], iota_j[:, 0:n, :].unsqueeze(1).to_broadcast([P, 2, n, GROUP]),
                                    val[:, cols].rearrange("p (g s) -> p g s", g=2).unsqueeze(2).to_broadcast([P, 2, n, GROUP]),
                                    ALU.is_equal).then_inc(hot_ready, 1)

            def split_hs(c, n):
                v.wait_ge(hs_hi, n + 1)
                v.wait_ge(hs3_ok, n)
                v.tensor_tensor(rest[0:PT, 0, :].rearrange("p (d f) -> p d f", d=W), hs[0:PT, bass.ds(W * c, W), :],
                                hs3[0:PT, bass.ds(W * c, W), 0, :], ALU.subtract).then_inc(hs_rest, 1)

            v.nop().then_inc(sums_free, 2)
            v.wait_ge(mixdone, 1)
            v.wait_ge(proj_h, SLOTS)
            v.nop().then_inc(hs_ok, C)
            st.wait()
            with v.Fori(0, 8) as i:
                for u in range(2):
                    v.wait_ge(built, 4 * i + 2 * u)
                    hot_unit(u, 2 * UNIT * i + UNIT * u)
            with v.Fori(0, C) as c:
                split_hs(c, c)
            for layer in range(2):
                k0, g0 = CH * layer, GROUPS * (1 + CH * layer)
                with v.Fori(0, CH // 2) as kp:
                    for par in range(2):
                        with v.Fori(0, 8) as i:
                            for u in range(2):
                                v.wait_ge(built, 2 * GROUPS * kp + 4 * i + (g0 + GROUPS * par + 2 * u))
                                hot_unit(u, 2 * P * kp + 2 * UNIT * i + (P * (par + 1) + UNIT * u))
                        v.wait_ge(hi_ok, 2 * kp + (k0 + par + 1))
                        v.wait_ge(lo_ok, 2 * kp + (k0 + par + 1))
                        v.tensor_tensor(rest[:, par, :], (psB, psC)[par][:, 0:W * HID], part3[:, 0, bass.ds(2 * kp + par, 1), :].rearrange("p a f -> p (a f)"),
                                        ALU.subtract).then_inc(sums_free, 1)
                with v.Fori(0, C) as c:
                    dv = dinv[0:PT, bass.ds(W * c, W)].unsqueeze(2).to_broadcast([PT, W, HID])
                    post_v = post[0:PT, :].rearrange("p (d f) -> p d f", d=W)
                    hs_c = hs[0:PT, bass.ds(W * c, W), :]
                    st.enter(c, 2 if layer == 0 else 0)
                    v.wait_ge(merged, c + (C * layer + 1))
                    if layer:
                        v.wait_ge(at_in, c)
                    v.tensor_tensor(post_v, psD[0:PT, 0:W * HID].rearrange("p (d f) -> p d f", d=W), hs_c, ALU.add).then_inc(merge_used, 1)
                    v.wait_ge(merge_used, c + (C * layer + 1))
                    if layer == 0:
                        st.did(v.tensor_tensor(post_v, post_v, dv, ALU.mult))
                        st.wait()
                        st.did(v.tensor_tensor(post_v, post_v, b1_all[0:PT, :].unsqueeze(1).to_broadcast([PT, W, HID]), ALU.add))
                        st.wait()
                        v.scalar_tensor_tensor(hs_c, post_v, 0.0, dv, ALU.max, ALU.mult).then_inc(hs_ok, 1)
                        split_hs(c, c + C)
                    else:
                        v.tensor_tensor(post_v, post_v, dv, ALU.mult).then_inc(post_ok, 1)
                        v.wait_ge(g2_in, c + 1)
                        a4 = acc[0:PT, bass.ds(W * c, 4), :]
                        a1 = acc[0:PT, bass.ds(W * c + 4, 1), :]
                        v.tensor_tensor(a4, psB[0:PT, :].rearrange("p (d f) -> p d f", d=4), a4, ALU.add).then_inc(g2_ok, 1)
                        v.tensor_tensor(a1, psC[0:PT, 0:DIM].rearrange("p (d f) -> p d f", d=1), a1, ALU.add).then_inc(g2_ok, 1)
                    st.leave(C)

            v.wait_ge(g2_ok, 2 * C)
            for n in range(SLOTS):
                st.did(v.bn_stats(stats[0:PT, n, :], acc[0:PT, n, :]))
            st.wait()
            for n in range(SLOTS):
                st.did(v.bn_aggr(mv[0:PT, n, :], stats[0:PT, n, :]))
            st.wait()
            v.tensor_scalar(small[0:PT, 2, :], mv[0:PT, :, 1], 1e-5, None, ALU.add).then_inc(var_ok, 1)
            v.wait_ge(std_ok, 2)
            st.did(v.reciprocal(rstd[0:PT, :], small[0:PT, 3, :]))
            st.wait()
            for n in range(SLOTS):
                v.tensor_scalar(tok[0:PT, n, :], acc[0:PT, n, :], mv[0:PT, n, 0:1], rstd[0:PT, n:n + 1],
                                ALU.subtract, ALU.mult).then_inc(tok_ok, 1)
            v.wait_ge(tok_ok, SLOTS)
            st.did(v.tensor_tensor(acc[0:PT], acc[0:PT], tok[0:PT], ALU.add))
            v.wait_ge(wr_in, 1)
            v.tensor_copy(wr[:], psC[:, 0:2 * EXPERTS].rearrange("p (k e) -> p k e", k=2)).then_inc(wr_ok, 1)
            v.tensor_copy(eb1[:], psC[:, 128:128 + 2 * EXPERTS]).then_inc(wr_ok, 1)
            v.wait_ge(logit_in, 1)
            st.did(v.tensor_copy(logit[0:PT], psC[0:PT, 512:512 + SLOTS * EXPERTS].rearrange("p (n e) -> p n e", e=EXPERTS)))
            st.wait()
            for n in range(SLOTS):
                st.did(v.max(top[0:PT, n, :], logit[0:PT, n, :]))
            st.wait()
            for n in range(SLOTS):
                st.did(v.max_index(topi[0:PT, n, :], top[0:PT, n, :], logit[0:PT, n, :]))
            v.tensor_tensor(prob[0:PT], logit[0:PT], top[0:PT, :, 0:1].to_broadcast([PT, SLOTS, EXPERTS]), ALU.subtract).then_inc(lg_ok, 1)
            st.wait()
            for j in range(2):
                st.did(v.tensor_tensor(pick[0:PT, j], ident_row[0:PT, 0:EXPERTS].unsqueeze(1).to_broadcast([PT, SLOTS, EXPERTS]),
                                       topi[0:PT, :, j:j + 1].to_broadcast([PT, SLOTS, EXPERTS]), ALU.is_equal))
            st.wait()
            st.did(v.tensor_tensor(pick[0:PT, 0], pick[0:PT, 0], pick[0:PT, 1], ALU.add))
            v.wait_ge(ex_ok, 1)
            st.did(v.tensor_reduce(small[0:PT, 0, :], prob[0:PT], AX.X, ALU.add))
            st.wait()
            st.did(v.reciprocal(small[0:PT, 1, :], small[0:PT, 0, :]))
            st.wait()
            st.did(v.tensor_tensor(prob[0:PT], prob[0:PT], small[0:PT, 1, :].unsqueeze(2).to_broadcast([PT, SLOTS, EXPERTS]), ALU.mult))
            st.wait()
            st.did(v.tensor_tensor(prob[0:PT], prob[0:PT], pick[0:PT, 0], ALU.mult))
            st.wait()
            st.did(v.tensor_reduce(small[0:PT, 0, :], prob[0:PT], AX.X, ALU.add))
            st.wait()
            st.did(v.tensor_scalar(small[0:PT, 0, :], small[0:PT, 0, :], 1e-12, None, ALU.max))
            st.wait()
            st.did(v.reciprocal(small[0:PT, 1, :], small[0:PT, 0, :]))
            st.wait()
            v.tensor_tensor(comb[0:PT], prob[0:PT], small[0:PT, 1, :].unsqueeze(2).to_broadcast([PT, SLOTS, EXPERTS]), ALU.mult).then_inc(comb_ok, 1)
            for n in range(SLOTS):
                v.wait_ge(eb_in, n + 1)
                v.tensor_tensor(acc[0:PT, n, :], acc[0:PT, n, :], psB[0:PT, 512 * (n % 2):512 * (n % 2) + DIM], ALU.add).then_inc(eb_ok, 1)
            v.wait_ge(eb_ok, SLOTS)

            def take(base, n0, tiles):
                for e in range(EXPERTS):
                    v.wait_ge(down, base + (e + 3))
                    v.wait_ge(y_free, base + (e + 2))
                    for t in range(tiles):
                        a = acc[0:PT, bass.ds(n0 + t, 1), :].rearrange("p a f -> p (a f)")
                        cw = comb[0:PT, bass.ds(n0 + t, 1), e:e + 1].rearrange("p a e -> p (a e)")
                        y = v.scalar_tensor_tensor(a, (psC, psD)[e % 2][0:PT, DIM * t:DIM * t + DIM], cw, a, ALU.mult, ALU.add)
                    y.then_inc(y_free, 1)

            v.nop().then_inc(y_free, 2)
            with v.Fori(0, 6) as g:
                take(EXPERTS * g, 4 * g, 4)
            take(6 * EXPERTS, 24, 1)

        @block.tensor
        def _(pe):
            pe.wait_ge(q_ready, 1)
            for q, ps in ((q_wt, psA), (q_r, psB), (q_key, psC), (q_b, psD)):
                for half in range(2):
                    for c in range(TCH):
                        k = P if c < TCH - 1 else TLAST
                        m = pe.matmul(ps[:, 512 * half:512 * half + 512], q[0:k, c, :], tile_at[0:k, c, 512 * half:512 * half + 512],
                                      start=(c == 0), stop=(c == TCH - 1))
                m.then_inc(q_spread, 1)
            pe.wait_ge(q_used, 1)
            for k in range(CH):
                for c in range(TCH):
                    n = P if c < TCH - 1 else TLAST
                    m = pe.matmul(psA[:, k:k + 1], tile_at[0:n, c, P * k:P * k + P], t_of16[0:n, c:c + 1], start=(c == 0), stop=(c == TCH - 1))
            m.then_inc(q_spread, 1)
            pe.wait_ge(rhot_ok, W)
            pe.wait_ge(sel_ok, CH)
            for k in range(CH):
                for d in range(W):
                    m = pe.matmul(psA[:, 64 + W * k + d:65 + W * k + d], r_hot[:, d, P * k:P * k + P], ones16[:], start=True, stop=True)
            m.then_inc(cnt_in, 1)
            pe.wait_ge(cnt_ok, 1)
            for c in range(C):
                for k in range(CH):
                    m = pe.matmul(psA[0:PT, 128 + W * c:128 + W * c + W], sel[:, k, PT * c:PT * c + PT], cnt[:, W * k:W * k + W],
                                  start=(k == 0), stop=(k == CH - 1))
            m.then_inc(deg_in, 1)

            pe.wait_ge(ident_ok, 1)
            pe.wait_ge(q_used, 4)

            def transposes(n):
                pe.wait_ge(xn_ok, n + 1)
                if n >= 2:
                    pe.wait_ge(xt_ok, n - 1)
                for k in range(2):
                    m = pe.transpose(psB[:, 512 * (n % 2) + P * k:512 * (n % 2) + P * k + PT], xn[0:PT, n, P * k:P * k + P], ident[0:PT, 0:PT])
                m.then_inc(xt_in, 1)

            def project(n):
                if n == 0:
                    pe.wait_ge(wcat_ok, 2)
                pe.wait_ge(xt_ok, n + 1)
                if n >= 2:
                    pe.wait_ge(proj_h, n - 1)
                    pe.wait_ge(proj_q, n - 1)
                for k in range(2):
                    m = pe.matmul(psC[0:PT, 512 * (n % 2):512 * (n % 2) + 512], xnT[:, n % 2, k, :], wcat[:, k, :], start=(k == 0), stop=(k == 1))
                m.then_inc(proj, 1)

            transposes(0)
            for n in range(SLOTS):
                if n + 1 < SLOTS:
                    transposes(n + 1)
                project(n)

            pe.wait_ge(mixdve, 1)
            pe.wait_ge(deg_ok, 1)
            pe.transpose(psA[:, 0:PT], kmax[0:PT, :], ident[0:PT, 0:PT]).then_inc(mixpe, 1)
            pe.wait_ge(mixdve, 3)
            pe.wait_ge(proj_q, SLOTS)
            pe.transpose(psB[0:MEM, 0:P], mem_k[:], ident[:, :])
            pe.transpose(psB[0:MEM, 256:256 + P], mem_v[:], ident[:, :])
            pe.matmul(psA[:, 256:256 + P], kmax_mat[:], ident[:, :], start=True, stop=True).then_inc(mixpe, 1)
            pe.wait_ge(mixact, 3)
            pe.wait_ge(mixdve, 9)
            for n in range(SLOTS):
                pe.matmul(psB[:, 512:512 + P + 1], qkv[0:PT, n, HID:2 * HID], qkv[0:PT, n, 2 * HID:3 * HID + 1], start=(n == 0), stop=False)
            pe.matmul(psB[:, 512:512 + P + 1], memkT[:], memvT[:], start=False, stop=True).then_inc(mixpe, 1)
            pe.wait_ge(mixdve, 13)
            pe.transpose(psB[:, 0:P], ctx_m[:], ident[:, :]).then_inc(mixpe, 1)
            pe.wait_ge(mixdve, 14)
            pe.matmul(psB[:, 256:256 + DIM], ctxT[:], wout[:], start=True, stop=True).then_inc(mixpe, 1)
            pe.wait_ge(qs_ok, 2)
            pe.wait_ge(mixdve, 15)

            def q_transpose(n):
                if n >= 2:
                    pe.wait_ge(qt_ok, n - 1)
                pe.transpose(psD[:, 512 * (n % 2):512 * (n % 2) + PT], qkv[0:PT, n, 0:HID], ident[0:PT, 0:PT]).then_inc(qt_in, 1)

            q_transpose(0)
            for n in range(SLOTS):
                if n + 1 < SLOTS:
                    q_transpose(n + 1)
                pe.wait_ge(qt_ok, n + 1)
                if n >= 2:
                    pe.wait_ge(mo_ok, n - 1)
                pe.matmul(psC[0:PT, 512 * (n % 2):512 * (n % 2) + DIM], qT[:, n % 2, :], wmix[:], start=True, stop=True).then_inc(mo_in, 1)

            def build(g, j, slot):
                if j % 2 == 0:
                    pe.wait_ge(hot_ready, g + 2)
                bank = 512 * (j % 2)
                for q in range(GROUP):
                    m = pe.matmul(psA[:, bank + KEYS * q:bank + KEYS * q + KEYS], hot_b[:, slot, j % 2, :, q], hot_k[:, slot, j % 2, :, q],
                                  start=True, stop=True)
                m.then_inc(built, 1)

            def add_slot(par, a, start, stop):
                for d in range(W):
                    for part in range(3):
                        m = pe.matmul((psB, psC)[par][:, HID * d:HID * d + HID], counts[0:PT, par, W_KEY(a, d), :].rearrange("p a s -> p (a s)"),
                                      hs3[0:PT, bass.ds(a, 1), part, :].rearrange("p a f -> p (a f)"),
                                      start=start and part == 0 and d % 4 == 0, stop=stop and part == 2, skip_group_check=True)
                return m

            def W_KEY(a, d):
                return bass.ds(W * a + d, 1)

            pe.nop().then_inc(built, 2)
            pe.nop().then_inc(down, 2)
            pe.wait_ge(mo_ok, SLOTS)
            with pe.Fori(0, 8) as i:
                for j in range(4):
                    pe.wait_ge(counts_ok, 4 * i + j + 1)
                    build(4 * i + j, j, j // 2)
            for layer in range(2):
                k0, g0 = CH * layer, GROUPS * (1 + CH * layer)
                pe.wait_ge(hs3_ok, C * (layer + 1))
                with pe.Fori(0, CH // 2) as kp:
                    for par in range(2):
                        pe.wait_ge(counts_ok, 2 * GROUPS * kp + (g0 + GROUPS * par + 2))
                        pe.wait_ge(sums_free, 2 * kp + (k0 + par + 1))
                        add_slot(par, 0, True, True)
                        with pe.Fori(0, 8) as i:
                            for j in range(4):
                                g = 2 * GROUPS * kp + 4 * i + (g0 + GROUPS * par + j)
                                pe.wait_ge(counts_ok, g + 1)
                                build(g, j, j // 2)
                                if j < 3:
                                    m = add_slot(par, 3 * i + j + 1, False, True)
                                if j == 2:
                                    m.then_inc(summed, 1)
                pe.wait_ge(lo_ok, k0 + CH + 2)
                with pe.Fori(0, C) as c:
                    pe.wait_ge(merge_used, c + C * layer)
                    for lo, hi in ((0, 512), (512, W * HID)):
                        for k in range(CH):
                            for part in range(3):
                                m = pe.matmul(psD[0:PT, lo:hi], sel[:, k, bass.ds(PT * c, PT)], part3[:, part, k, lo:hi],
                                              start=(k == 0 and part == 0), stop=(k == CH - 1 and part == 2))
                    m.then_inc(merged, 1)
                    if layer:
                        pe.wait_ge(post_ok, c + 1)
                        for d in range(W):
                            m = pe.transpose(psA[:, P * d:P * d + PT], post[0:PT, HID * d:HID * d + HID], ident[0:PT, 0:PT])
                        m.then_inc(at_in, 1)
                        pe.wait_ge(at_ok, c + 1)
                        pe.wait_ge(g2_ok, 2 * c)
                        for d in range(W):
                            o = psB[0:PT, DIM * d:DIM * d + DIM] if d < 4 else psC[0:PT, 0:DIM]
                            m = pe.matmul(o, aggT[:, d, 0:PT], w2g[:], start=True, stop=True)
                        m.then_inc(g2_in, 1)

            pe.wait_ge(g2_ok, 2 * C)
            for k in range(2):
                pe.transpose(psC[:, EXPERTS * k:EXPERTS * k + EXPERTS], rw_nat[:, P * k:P * k + P], ident[0:EXPERTS, 0:EXPERTS])
            pe.transpose(psC[:, 128:128 + 2 * EXPERTS], eb1_nat[:], ident[0:2 * EXPERTS, 0:2 * EXPERTS]).then_inc(wr_in, 1)
            pe.wait_ge(wr_ok, 2)

            def logits(n):
                pe.wait_ge(tt_ok, n + 1)
                for k in range(2):
                    m = pe.matmul(psC[0:PT, 512 + EXPERTS * n:512 + EXPERTS * n + EXPERTS], tokT[:, k, PT * n:PT * n + PT], wr[:, k, :],
                                  start=(k == 0), stop=(k == 1))
                return m

            def bias2(n):
                pe.wait_ge(ct_ok, n + 1)
                if n >= 2:
                    pe.wait_ge(eb_ok, n - 1)
                pe.matmul(psB[0:PT, 512 * (n % 2):512 * (n % 2) + DIM], combT[:, PT * n:PT * n + PT], eb2[:], start=True, stop=True).then_inc(eb_in, 1)

            for n in range(SLOTS):
                pe.wait_ge(tok_ok, n + 1)
                if n >= 2:
                    pe.wait_ge(tt_ok, n - 1)
                for k in range(2):
                    m = pe.transpose(psA[:, 512 * (n % 2) + P * k:512 * (n % 2) + P * k + PT], tok[0:PT, n, P * k:P * k + P], ident[0:PT, 0:PT])
                m.then_inc(tt_in, 1)
                if n:
                    logits(n - 1)
            logits(SLOTS - 1).then_inc(logit_in, 1)
            pe.wait_ge(comb_ok, 1)
            for n in range(SLOTS):
                if n >= 2:
                    pe.wait_ge(ct_ok, n - 1)
                pe.transpose(psA[0:EXPERTS, 512 * (n % 2):512 * (n % 2) + PT], comb[0:PT, n, :], ident[0:PT, 0:PT]).then_inc(ct_in, 1)
                if n:
                    bias2(n - 1)
            bias2(SLOTS - 1)

            def up(E, n0, size, e):
                pe.wait_ge(gelu, 2 * E + 2)
                for h in range(2):
                    for k in range(2):
                        m = pe.matmul((psA, psB)[e % 2][:, 512 * h:512 * h + size], ew1[:, e, k, P * h:P * h + P], tokT[:, k, bass.ds(n0, size)],
                                      start=(k == 0), stop=(k == 1))
                    m.then_inc(upped, 1)

            def group(base, n0, tiles):
                for e in range(EXPERTS + 1):
                    if e < EXPERTS:
                        up(base + e, PT * n0, PT * tiles, e)
                    if e:
                        f = e - 1
                        pe.wait_ge(gelu, 2 * base + (2 * f + 6))
                        pe.wait_ge(y_free, base + (f + 1))
                        for t in range(tiles):
                            for k in range(2):
                                m = pe.matmul((psC, psD)[f % 2][0:PT, DIM * t:DIM * t + DIM], hT[:, f % 2, k, PT * t:PT * t + PT], ew2[:, f, k, :],
                                              start=(k == 0), stop=(k == 1))
                        m.then_inc(down, 1)

            pe.wait_ge(in_moe, 32)
            pe.wait_ge(eb_ok, SLOTS)
            with pe.Fori(0, 6) as g:
                group(EXPERTS * g, 4 * g, 4)
            group(6 * EXPERTS, 24, 1)

        @block.scalar
        def _(act):
            act.wait_ge(deg_ok, 1)
            act.activation(small[0:PT, 1, :], small[0:PT, 0, :], ACT.Sqrt).then_inc(dsq_ok, 1)
            act.wait_ge(var_ok, 1)
            act.activation(small[0:PT, 3, :], small[0:PT, 2, :], ACT.Sqrt).then_inc(std_ok, 1)
            sa = Steps(act, a_)
            for n in range(SLOTS):
                act.wait_ge(xn_ok, n + 1)
                if n:
                    sa.wait()
                sa.did(act.activation(junk[0:PT, :], xn[0:PT, n, :], ACT.Square, accum_out=small[0:PT, 2, n:n + 1]))
            act.wait_ge(dinv_ok, 1)
            sa.wait()
            act.activation(small[0:PT, 1, :], small[0:PT, 2, :], ACT.Sqrt).then_inc(ss_ok, 1)
            act.wait_ge(g16_ok, 1)
            for n in range(SLOTS):
                act.wait_ge(xt_in, n + 1)
                if n >= 2:
                    act.wait_ge(proj, n - 1)
                act.copy(xnT[:, n % 2, :, :], psB[:, 512 * (n % 2):512 * (n % 2) + 256].rearrange("p (k q) -> p k q", k=2)[:, :, 0:PT]).then_inc(xt_ok, 1)
                act.wait_ge(proj_h, n + 1)
                act.activation(qkv[0:PT, n, 0:QKV], psC[0:PT, 512 * (n % 2) + HID:512 * (n % 2) + 512], ACT.Copy,
                               scale=small[0:PT, 0, n:n + 1]).then_inc(proj_q, 1)
            act.wait_ge(qs_ok, 1)
            act.activation(qkv[0:PT, :, 0:HID], qkv[0:PT, :, 0:HID], ACT.Exp).then_inc(mixact, 1)
            act.wait_ge(mixdve, 4)
            act.activation(qkv[0:PT, :, HID:2 * HID], qkv[0:PT, :, HID:2 * HID], ACT.Exp).then_inc(mixact, 1)
            act.wait_ge(mixdve, 6)
            act.activation(memkT[:], memkT[:], ACT.Exp).then_inc(mixact, 1)
            for n in range(SLOTS):
                act.wait_ge(qt_in, n + 1)
                if n >= 2:
                    act.wait_ge(mo_in, n - 1)
                act.copy(qT[:, n % 2, :], psD[:, 512 * (n % 2):512 * (n % 2) + PT]).then_inc(qt_ok, 1)
                if n >= 1:
                    act.wait_ge(mo_ok, n)
                    if n >= 2:
                        sa.wait()
                    sa.did(act.activation(junk[0:PT, :], mix[0:PT, n - 1, :], ACT.Square, accum_out=small[0:PT, 2, n - 1:n]))
            act.wait_ge(mo_ok, SLOTS)
            sa.wait()
            sa.did(act.activation(junk[0:PT, :], mix[0:PT, SLOTS - 1, :], ACT.Square, accum_out=small[0:PT, 2, SLOTS - 1:SLOTS]))
            sa.wait()
            act.activation(small[0:PT, 3, :], small[0:PT, 2, :], ACT.Sqrt).then_inc(mss_ok, 1)

            act.nop().then_inc(counts_ok, 2)
            act.nop().then_inc(gelu, 4)
            act.preload_act_table(ACT.Copy)

            def take_counts(g, par, j, col):
                act.wait_ge(built, g + 3)
                act.copy(counts[:, par, :, bass.ds(col, GROUP)].rearrange("p j s -> p s j"),
                         psA[:, 512 * (j % 2):512 * (j % 2) + GROUP * KEYS].rearrange("p (s j) -> p s j", s=GROUP)).then_inc(counts_ok, 1)

            def hs_high(c, n):
                act.wait_ge(hs_ok, n + 1)
                act.copy(hs3[0:PT, bass.ds(W * c, W), 0, :], hs[0:PT, bass.ds(W * c, W), :]).then_inc(hs_hi, 1)

            with act.Fori(0, 8) as i:
                for j in range(4):
                    take_counts(4 * i + j, 0, j, 4 * GROUP * i + GROUP * j)
            with act.Fori(0, C) as c:
                hs_high(c, c)
            for layer in range(2):
                k0, g0 = CH * layer, GROUPS * (1 + CH * layer)
                if layer:
                    act.wait_ge(merged, C)
                with act.Fori(0, CH // 2) as kp:
                    for par in range(2):
                        act.wait_ge(summed, 16 * kp + 8 * (k0 + par))
                        with act.Fori(0, 8) as i:
                            for j in range(4):
                                take_counts(2 * GROUPS * kp + 4 * i + (g0 + GROUPS * par + j), 1 - par, j, 4 * GROUP * i + GROUP * j)
                        act.wait_ge(summed, 16 * kp + 8 * (k0 + par + 1))
                        act.copy(part3[:, 0, bass.ds(2 * kp + par, 1), :].rearrange("p a f -> p (a f)"), (psB, psC)[par][:, 0:W * HID]).then_inc(hi_ok, 1)
                if layer == 0:
                    with act.Fori(0, C) as c:
                        hs_high(c, c + C)
                else:
                    with act.Fori(0, C) as c:
                        act.wait_ge(at_in, c + 1)
                        act.wait_ge(g2_in, c)
                        act.copy(aggT[:, :, 0:PT], psA[:, 0:W * P].rearrange("p (d q) -> p d q", d=W)[:, :, 0:PT]).then_inc(at_ok, 1)

            act.wait_ge(var_ok, 2)
            act.activation(small[0:PT, 3, :], small[0:PT, 2, :], ACT.Sqrt).then_inc(std_ok, 1)
            for n in range(SLOTS):
                act.wait_ge(tt_in, n + 1)
                act.copy(tokT[:, :, PT * n:PT * n + PT], psA[:, 512 * (n % 2):512 * (n % 2) + 256].rearrange("p (k q) -> p k q", k=2)[:, :, 0:PT]).then_inc(tt_ok, 1)
            act.wait_ge(lg_ok, 1)
            act.activation(prob[0:PT], prob[0:PT], ACT.Exp).then_inc(ex_ok, 1)
            for n in range(SLOTS):
                act.wait_ge(ct_in, n + 1)
                act.copy(combT[:, PT * n:PT * n + PT], psA[0:EXPERTS, 512 * (n % 2):512 * (n % 2) + PT]).then_inc(ct_ok, 1)
            act.preload_act_table(ACT.Gelu)
            act.wait_ge(wr_ok, 2)

            def hidden(base, size):
                for e in range(EXPERTS):
                    act.wait_ge(down, base + (e + 1))
                    for h in range(2):
                        act.wait_ge(upped, 2 * base + (2 * e + h + 1))
                        act.activation(hT[:, e % 2, h, 0:size], (psA, psB)[e % 2][:, 512 * h:512 * h + size], ACT.Gelu,
                                       bias=eb1[:, 2 * e + h:2 * e + h + 1]).then_inc(gelu, 1)

            with act.Fori(0, 6) as g:
                hidden(EXPERTS * g, 4 * PT)
            hidden(6 * EXPERTS, PT)


_INS = ['x', 'src', 'dst', 'L0_gnn_W1', 'L0_gnn_b1', 'L0_gnn_W2', 'L0_gnn_b2', 'L0_mix_w_qkv', 'L0_mix_mem_kv', 'L0_mix_w_out',
        'L0_mix_b_out', 'L0_mix_g_out', 'L0_mix_g_pre', 'L0_ffn_router_w', 'L0_ffn_w1', 'L0_ffn_b1', 'L0_ffn_w2', 'L0_ffn_b2']
_OUTS = [((NODES, DIM), 'float32')]


def kernel(**inputs):
    import numpy as _np
    import concourse.bacc as _bacc
    from concourse import mybir as _mybir
    from concourse.bass_utils import run_bass_kernel_spmd as _run

    nc = _bacc.Bacc("TRN2", target_bir_lowering=False, num_devices=1)
    arrays, args = {}, []
    for name in _INS:
        a = _np.ascontiguousarray(inputs[name])
        arrays[f"in_{name}_dram"] = a
        args.append(nc.dram_tensor(f"in_{name}_dram", a.shape, _mybir.dt.from_np(a.dtype), kind="ExternalInput").ap())
    for i, (shape, dtype) in enumerate(_OUTS):
        dt = _mybir.dt.from_np(_np.dtype(dtype))
        args.append(nc.dram_tensor(f"out_{i}_dram", shape, dt, kind="ExternalOutput").ap())
    gps_layer(nc, *args)
    r = _run(nc, [arrays], core_ids=[0])
    got = tuple(r.results[0][f"out_{i}_dram"] for i in range(len(_OUTS)))
    return got[0]
```

```python
from contextlib import ExitStack

import concourse.bass as bass
from concourse import mybir

ALU = mybir.AluOpType
ACT = mybir.ActivationFunctionType
AX = mybir.AxisListType
F32 = mybir.dt.float32
BF16 = mybir.dt.bfloat16
F16 = mybir.dt.float16
F32R = mybir.dt.float32r
I32 = mybir.dt.int32

P = 128
NODES, DIM, HID, EDGES = 3125, 256, 128, 50000
HEADS, HEAD_DIM, MEM = 4, 32, 4
EXPERTS = 8
W = 5
PT = 125
C = 5
SLOTS = C * W
WINDOWS = NODES // W
EDGE_TILES = -(-EDGES // P)
TCH = -(-EDGE_TILES // P)
TLAST = EDGE_TILES - (TCH - 1) * P
STEPS = 1024
CH = STEPS // P
KEYS = SLOTS * W
NO_NODE = 4000
NO_KEY = 1000.0
UNIT = 8
GROUP = 4
GROUPS = P // GROUP
QKV = 3 * HID
assert EDGE_TILES + WINDOWS - 1 <= STEPS and SLOTS * PT == NODES


TILE_GROUPS = [(n, min(4, SLOTS - n)) for n in range(0, SLOTS, 4)]


class Steps:

    def __init__(self, eng, sem):
        self.eng, self.sem, self.n, self.base = eng, sem, 0, 0

    def did(self, ins):
        ins.then_inc(self.sem, 1)
        self.n += 1

    def wait(self):
        self.eng.wait_ge(self.sem, self.base + self.n)

    def enter(self, i, per):
        self.start, self.per, self.base = self.n, per, i * per

    def leave(self, count):
        assert self.n - self.start == self.per, (self.n - self.start, self.per)
        self.n, self.base = self.start + count * self.per, 0


def gps_layer(nc, x, src, dst, gnn_w1, gnn_b1, gnn_w2, gnn_b2, w_qkv, mem_kv, w_out, b_out, g_out,
              g_pre, router_w, moe_w1, moe_b1, moe_w2, moe_b2, out, dbg=None):
    ctx = ExitStack()
    with ctx:
        def sb(name, shape, dt, scope=ctx):
            return scope.enter_context(nc.sbuf_tensor(name, shape, dt))

        def sem(name):
            return ctx.enter_context(nc.semaphore(name))

        psA, psB, psC, psD = (ctx.enter_context(nc.psum_tensor(f"ps{n}", [P, 1024], F32)) for n in "ABCD")

        ident = sb("ident", [P, P], F32)
        ident_row = sb("ident_row", [P, P], F32)
        ident_col = sb("ident_col", [P, 1], F32)
        iota_j = sb("iota_j", [P, P, GROUP], BF16)
        acc = sb("acc", [P, SLOTS, DIM], F32)
        hs = sb("hs", [P, SLOTS, HID], F32)
        dinv = sb("dinv", [P, SLOTS], F32)
        key = sb("key", [P, STEPS + P + 2 * UNIT], BF16)
        brow = sb("brow", [P, STEPS + P + 2 * UNIT], BF16)
        ones_row = sb("ones_row", [1, P], F32)
        hs_max = sb("hs_max", [P, C + 1], F32)
        top_hs = sb("top_hs", [1, 4], F32)
        scale = sb("scale", [P, 2], F32)
        sel = sb("sel", [P, CH, WINDOWS], F16)
        b1_all = sb("b1_all", [P, HID], F32)
        w2g = sb("w2g", [P, DIM], F32)
        stats = sb("stats", [P, SLOTS, 6], F32)
        mv = sb("mv", [P, SLOTS, 2], F32)
        rstd = sb("rstd", [P, SLOTS], F32)
        small = sb("small", [P, 4, SLOTS], F32)
        mnorm = sb("mnorm", [P, SLOTS], F32)
        xnorm = sb("xnorm", [P, SLOTS], F32)
        wr = sb("wr", [P, 2, EXPERTS], F32)
        eb2 = sb("eb2", [3 * 32, DIM], F32R)
        eb1 = sb("eb1", [P, 2 * EXPERTS], F32)
        comb = sb("comb", [P, SLOTS, EXPERTS], F32)

        SUMS_BYTES = (2 * CH * W * HID * 2 + W * HID * 4 + W * P * 4)
        COUNTS_BYTES = KEYS * P * 2
        HOT_BYTES = 2 * UNIT * (P + KEYS) * 2
        LOOP_BYTES = SUMS_BYTES + 2 * COUNTS_BYTES + HOT_BYTES + SLOTS * 2 * HID * 2
        with ExitStack() as st:
            used = 0

            def early(name, shape, dt):
                nonlocal used
                size = {F32: 4, I32: 4, F16: 2, BF16: 2}[dt]
                for n in shape[1:]:
                    size *= n
                used += size
                return sb(name, shape, dt, st)

            def up_to(offset, name):
                nonlocal used
                assert used <= offset, (name, used, offset)
                if used < offset:
                    sb(f"before_{name}", [P, (offset - used) // 2], F16, st)
                used = offset

            t_of = early("t_of", [P, TCH], F32)
            s_of = early("s_of", [P, CH], F32)
            t_of16 = early("t_of16", [P, TCH], F16)
            ones16 = early("ones16", [P, 2], BF16)
            t_lo = early("t_lo", [P, TCH], F32)
            t_hi = early("t_hi", [P, TCH], F32)
            prev_dst = early("prev_dst", [P, TCH], I32)
            prev_w = early("prev_w", [P, TCH], I32)
            w_of_s = early("w_of_s", [P, CH], F32)
            cnt = early("cnt", [P, CH * W], F16)
            b2_all = early("b2_all", [P, DIM], F32)
            bout_all = early("bout_all", [P, DIM], F32)
            eb2_raw = early("eb2_raw", [3 * 32, DIM], F32)
            rw_nat = early("rw_nat", [EXPERTS, DIM], F32)
            eb1_nat = early("eb1_nat", [2 * EXPERTS, P], F32)
            xnT = early("xnT", [P, 2, 2, PT], F32)
            wcat = early("wcat", [P, 2, HID + QKV], F32)
            gpre = early("gpre", [P, 2], F32)
            mem_v = early("mem_v", [P, MEM], F32)
            mem_k = early("mem_k", [P, MEM], F32)
            memkT = early("memkT", [MEM, P], F32)
            memvT = early("memvT", [MEM, P + 1], F32)
            kmax_of = early("kmax_of", [P, C, HID], F32)
            kmax = early("kmax", [P, HID], F32)
            kmax_col = early("kmax_col", [P, 2], F32)
            kmax_mat = early("kmax_mat", [P, P], F32)
            qred = early("qred", [P, SLOTS * HEADS], F32)
            ctx_sb = early("ctx_sb", [P, P + 1], F32)
            ctx_m = early("ctx_m", [P, P], F32)
            ctxT = early("ctxT", [P, P], F32)
            wmix = early("wmix", [P, DIM], F32)
            zinv = early("zinv", [P, 1], F32)
            wout = early("wout", [P, DIM], F32)
            qT = early("qT", [P, 2, 4 * PT], F32)
            up_to(SUMS_BYTES, "counts")
            e_dst = early("e_dst", [P, TCH, P], I32)
            e_src = early("e_src", [P, TCH, P], I32)
            dst_w = early("dst_w", [P, TCH, P], I32)
            src_w = early("src_w", [P, TCH, P], I32)
            src_c = early("src_c", [P, TCH, P], I32)
            src_d = early("src_d", [P, TCH, P], F32)
            past = early("past", [P, TCH, STEPS], F16)
            r_hot = early("r_hot", [P, W, STEPS], BF16)
            up_to(SUMS_BYTES + COUNTS_BYTES, "second_counts")
            xn = early("xn", [P, SLOTS, DIM], F32)
            src_slot = early("src_slot", [P, TCH, P], F32)
            q_r = early("q_r", [P, TCH, P], F16)
            q_wt = early("q_wt", [P, TCH, P], F16)
            q_b = early("q_b", [P, TCH, P], F16)
            q_key = early("q_key", [P, TCH, P], F16)
            tile_at = early("tile_at", [P, TCH, STEPS], F16)
            outside = early("outside", [P, STEPS], BF16)
            r_in = early("r_in", [P, STEPS], BF16)
            iota_s = early("iota_s", [P, STEPS], F16)
            up_to(LOOP_BYTES, "qkv")
            qkv = early("qkv", [P, SLOTS, QKV + 1], F32)
            gout_all = early("gout_all", [P, DIM], F32)
            mix = qkv[:, :, HID:QKV]

        with ExitStack() as st:
            part2 = sb("part2", [P, 2, CH, W * HID], F16, st)
            post = sb("post", [P, W * HID], F32, st)
            aggT = sb("aggT", [P, W, P], F32, st)
            experts_from = st.pop_all()
            counts = sb("counts", [P, 2, KEYS, P], F16, st)
            hot_b = sb("hot_b", [P, 2, 2, P, GROUP], BF16, st)
            hot_k = sb("hot_k", [P, 2, 2, KEYS, GROUP], BF16, st)
            hs2 = sb("hs2", [P, SLOTS, 2, HID], F16, st)
            counts5 = counts[:, :, :, :].rearrange("p r (a d) s -> p r a d s", d=W)

        with ExitStack() as st:
            w_hi = sb("w_hi", [P, 2, EXPERTS, 2, DIM], F32R, st)
            with ExitStack() as raw:
                w_raw = sb("w_raw", [P, 2, EXPERTS, 2, DIM], F32, raw)
            w_lo = sb("w_lo", [P, 2, EXPERTS, 2, DIM], F32R, st)
            tok = sb("tok", [P, W, DIM], F32, st)
            tokT = sb("tokT", [P, 2, W * PT], F32, st)
            tokT_hi = sb("tokT_hi", [P, 2, SLOTS * PT], F32R, st)
            tokT_lo = sb("tokT_lo", [P, 2, SLOTS * PT], F32R, st)
        experts_from.close()

        with ExitStack() as st:
            g_sb = sb("g_sb", [P, 2, 2, 4 * PT], F32, st)
            h_hi = sb("h_hi", [P, 2, 2, 4 * PT], F32R, st)
            h_lo = sb("h_lo", [P, 2, 2, 4 * PT], F32R, st)
        with ExitStack() as st:
            logit = sb("logit", [P, SLOTS, EXPERTS], F32, st)
            top = sb("top", [P, SLOTS, 8], F32, st)
            topi = sb("topi", [P, SLOTS, 8], mybir.dt.uint32, st)
            pick = sb("pick", [P, 2, SLOTS, EXPERTS], F32, st)
            prob = sb("prob", [P, SLOTS, EXPERTS], F32, st)
            comb_hi = sb("comb_hi", [P, SLOTS, EXPERTS], F32R, st)
            comb3 = sb("comb3", [P, SLOTS, 3 * 32], F32, st)
            combT = sb("combT", [3 * 32, 2, 4 * PT], F32R, st)

        pads = sem("pads")
        consts = sem("consts")
        in_edges = sem("in_edges")
        in_x = sem("in_x")
        in_w = sem("in_w")
        in_w1, in_w2 = sem("in_w1"), sem("in_w2")
        v_ = sem("vector_steps")
        a_ = sem("scalar_steps")
        ident_ok = sem("ident_ok")
        q_ready = sem("q_ready")
        q_spread = sem("q_spread")
        q_used = sem("q_used")
        rhot_ok = sem("rhot_ok")
        sel_ok = sem("sel_ok")
        cnt_in = sem("cnt_in")
        cnt_ok = sem("cnt_ok")
        deg_in = sem("deg_in")
        deg_ok = sem("deg_ok")
        dsq_ok = sem("dsq_ok")
        dinv_ok = sem("dinv_ok")
        var_ok = sem("var_ok")
        std_ok = sem("std_ok")
        xn_ok = sem("xn_ok")
        ss_ok = sem("ss_ok")
        g16_ok = sem("g16_ok")
        wcat_ok = sem("wcat_ok")
        xt_in = sem("xt_in")
        xt_ok = sem("xt_ok")
        proj = sem("proj")
        proj_h = sem("proj_h")
        proj_q = sem("proj_q")
        km_ok = sem("km_ok")
        mixpe = sem("mixpe")
        mixdve = sem("mixdve")
        mixact = sem("mixact")
        q_sub = sem("q_sub")
        q_exp = sem("q_exp")
        q_done = sem("q_done")
        xn_free = sem("xn_free")
        norm_ok = sem("norm_ok")
        mix_scaled = sem("mix_scaled")
        qt_in = sem("qt_in")
        qt_ok = sem("qt_ok")
        mo_in = sem("mo_in")
        mo_ok = sem("mo_ok")
        mss_ok = sem("mss_ok")
        mixdone = sem("mixdone")
        xadd_ok = sem("xadd_ok")
        hot_ready = sem("hot_ready")
        built = sem("built")
        counts_ok = sem("counts_ok")
        summed = sem("summed")
        hi_ok = sem("hi_ok")
        sums_free = sem("sums_free")
        tok_ok = sem("tok_ok")
        tok_added = sem("tok_added")
        tt_hi = sem("tt_hi")
        tt_ok = sem("tt_ok")
        tt_lo = sem("tt_lo")
        w_hi_ok = sem("w_hi_ok")
        w_lo_ok = sem("w_lo_ok")
        g_ok = sem("g_ok")
        h_hi_ok = sem("h_hi_ok")
        h_lo_ok = sem("h_lo_ok")
        wr_in = sem("wr_in")
        wr_ok = sem("wr_ok")
        logit_in = sem("logit_in")
        lg_ok = sem("lg_ok")
        ex_ok = sem("ex_ok")
        comb_ok = sem("comb_ok")
        comb_made = sem("comb_made")
        eb_in = sem("eb_in")
        eb_ok = sem("eb_ok")
        tt_in = sem("tt_in")
        ct_in = sem("ct_in")
        ct_ok = sem("ct_ok")
        upped = sem("upped")
        down = sem("down")
        y_free = sem("y_free")
        merged = sem("merged")
        merge_used = sem("merge_used")
        hs_ok = sem("hs_ok")
        hs_hi = sem("hs_hi")
        hs_lo = sem("hs_lo")
        max_ok = sem("max_ok")
        max_in = sem("max_in")
        pow_ok = sem("pow_ok")
        pow_in = sem("pow_in")
        scale_ok = sem("scale_ok")
        post_ok = sem("post_ok")
        at_in = sem("at_in")
        at_ok = sem("at_ok")
        g2_in = sem("g2_in")
        g2_ok = sem("g2_ok")
        s_out = sem("s_out")
        s_dbg = sem("s_dbg")
        locals_ = dict(locals())

        block = ctx.enter_context(nc.Block())

        TOKEN_PARTS = ((0, 0, W, psA[:, 0:W * P]), (1, 0, 3, psA[:, W * P:8 * P]), (1, 3, W, psC[:, 512:512 + 2 * P]))

        x_v = x.rearrange("(c p m) f -> p c (m f)", p=PT, m=W)
        acc_v = acc[:, :, :].rearrange("p (c m) f -> p c (m f)", m=W)

        @block.sync
        def _(sp):
            full = (TCH - 1) * P
            n_last = EDGES // P - full
            tail = EDGES - (EDGES // P) * P
            sp.wait_ge(pads, 4)
            for e_sb, e in ((e_dst, dst), (e_src, src)):
                sp.dma_start(e_sb[:, 0:TCH - 1, :], e[0:full * P].rearrange("(c p e) -> p c e", p=P, e=P)).then_inc(in_edges, 16)
                sp.dma_start(e_sb[0:n_last, TCH - 1, :], e[full * P:(full + n_last) * P].rearrange("(p e) -> p e", e=P)).then_inc(in_edges, 16)
                sp.dma_start(e_sb[n_last:n_last + 1, TCH - 1, 0:tail], e[(full + n_last) * P:EDGES].rearrange("(p e) -> p e", p=1)).then_inc(in_edges, 16)
            ends = dst[0:(EDGES // P) * P].rearrange("(t e) -> t e", e=P)[:, P - 1:P]
            sp.dma_start(prev_dst[1:P, 0:1], ends[0:P - 1, :], allow_slow_non_contiguous=True).then_inc(in_edges, 16)
            for c in range(1, TCH):
                k = P if c < TCH - 1 else TLAST
                sp.dma_start(prev_dst[0:k, c:c + 1], ends[c * P - 1:c * P - 1 + k, :],
                             allow_slow_non_contiguous=True).then_inc(in_edges, 16)
            for lo, hi in ((0, 112), (112, PT)):
                sp.dma_start(acc_v[lo:hi], x_v[lo:hi]).then_inc(in_x, 16)
            loads = [
                (wcat[:, :, 0:HID], gnn_w1.rearrange("(k p) f -> p k f", p=P)),
                (wcat[:, :, HID:HID + QKV], w_qkv.rearrange("(k p) f -> p k f", p=P)),
                (mem_k[:, :], mem_kv[0].rearrange("h d m -> (h d) m")),
                (mem_v[:, :], mem_kv[1].rearrange("h d m -> (h d) m")),
                (wout[:, :], w_out),
                (w2g[:, :], gnn_w2),
                (b1_all[:, :], gnn_b1.rearrange("(a f) -> a f", a=1).to_broadcast([P, HID])),
                (b2_all[:, :], gnn_b2.rearrange("(a f) -> a f", a=1).to_broadcast([P, DIM])),
                (bout_all[:, :], b_out.rearrange("(a f) -> a f", a=1).to_broadcast([P, DIM])),
                (gout_all[:, :], g_out.rearrange("(a f) -> a f", a=1).to_broadcast([P, DIM])),
                (gpre[:, 0:1], g_pre[0:P].rearrange("(p a) -> p a", a=1)),
                (gpre[:, 1:2], g_pre[P:DIM].rearrange("(p a) -> p a", a=1)),
                (rw_nat[:, :], router_w),
                (eb2_raw[0:EXPERTS, :], moe_b2),
                (eb2_raw[32:32 + EXPERTS, :], moe_b2),
                (eb2_raw[64:64 + EXPERTS, :], moe_b2),
                (eb1_nat[:, :], moe_b1.rearrange("e (h p) -> (e h) p", p=P)),
            ]
            for to, frm in loads:
                sp.dma_start(to, frm).then_inc(in_w, 16)
            assert len(loads) == 17
            sp.wait_ge(summed, 2 * CH + 1)
            for i, w, loaded in ((0, moe_w1, in_w1), (1, moe_w2, in_w2)):
                sp.dma_start(w_raw[:, i, :, :, :].rearrange("p e k f -> p (e k) f"), w.rearrange("e (k p) f -> p (e k) f", p=P)).then_inc(loaded, 16)
            out_v = out.rearrange("(c p m) f -> p c (m f)", p=PT, m=W)
            for c in range(C):
                group = min((W * c + W - 1) // 4, 6)
                sp.wait_ge(y_free, 2 + EXPERTS * (group + 1))
                for lo, hi in ((0, 112), (112, PT)):
                    sp.dma_start(out_v[lo:hi, c], acc_v[lo:hi, c]).then_inc(s_out, 16)
            sp.wait_ge(s_out, 32 * C)
            if dbg:
                for n, (wait, ap, to) in enumerate(dbg(locals_)):
                    if n == 0:
                        sp.wait_ge(*wait)
                    sp.dma_start(to, ap).then_inc(s_dbg, 16)
                sp.wait_ge(s_dbg, 16 * (n + 1))
        IN_W = 16 * 17
        IN_EDGES = 16 * 10

        @block.gpsimd
        def _(pool):
            pool.memset(e_dst[:, TCH - 1, :], NO_NODE).then_inc(pads, 1)
            pool.memset(e_src[:, TCH - 1, :], 0).then_inc(pads, 1)
            pool.memset(prev_dst[:, :], 0).then_inc(pads, 1)
            pool.memset(eb2_raw[:, :], 0).then_inc(pads, 1)
            kw = dict(allow_small_or_imprecise_dtypes=True)
            pool.iota(t_of[:, :], [[P, TCH]], base=0, channel_multiplier=1, **kw).then_inc(consts, 1)
            pool.iota(iota_s[:, :], [[1, STEPS]], base=0, channel_multiplier=0, **kw).then_inc(consts, 1)
            pool.iota(t_of16[:, :], [[P, TCH]], base=0, channel_multiplier=1, **kw).then_inc(consts, 1)
            pool.iota(s_of[:, :], [[P, CH]], base=0, channel_multiplier=1, **kw).then_inc(consts, 1)
            pool.iota(ident_row[:, :], [[1, P]], base=0, channel_multiplier=0, **kw).then_inc(consts, 1)
            pool.iota(ident_col[:, :], [[0, 1]], base=0, channel_multiplier=1, **kw).then_inc(consts, 1)
            pool.iota(iota_j[:, :, :], [[1, P], [0, GROUP]], base=0, channel_multiplier=0, **kw).then_inc(consts, 1)
            pool.memset(ones16[:, :], 1.0).then_inc(consts, 1)
            pool.memset(ones_row[:, :], 1.0).then_inc(consts, 1)

            pool.wait_ge(xn_ok, SLOTS)
            pool.wait_ge(in_w, IN_W)
            pool.tensor_tensor(acc[0:PT], acc[0:PT], xn[0:PT], ALU.add).then_inc(xn_free, 1)
            pool.wait_ge(xn_free, 1)
            pool.tensor_tensor(acc[0:PT], acc[0:PT], b2_all[0:PT, :].unsqueeze(1).to_broadcast([PT, SLOTS, DIM]), ALU.add).then_inc(xadd_ok, 1)
            pool.wait_ge(norm_ok, 1)
            pool.wait_ge(xadd_ok, 1)
            m = mix[0:PT]
            pool.tensor_tensor(m, m, mnorm[0:PT, :].unsqueeze(2).to_broadcast([PT, SLOTS, DIM]), ALU.mult).then_inc(mix_scaled, 1)
            pool.wait_ge(mix_scaled, 1)
            pool.tensor_tensor(m, m, gout_all[0:PT, :].unsqueeze(1).to_broadcast([PT, SLOTS, DIM]), ALU.mult).then_inc(mix_scaled, 1)
            pool.wait_ge(mix_scaled, 2)
            pool.tensor_tensor(acc[0:PT], acc[0:PT], m, ALU.add).then_inc(mixdone, 1)

            for i in range(2):
                pool.wait_ge(w_hi_ok, i + 1)
                pool.tensor_tensor(w_lo[:, i], w_raw[:, i], w_hi[:, i].bitcast(F32), ALU.subtract).then_inc(w_lo_ok, 1)

        CONSTS = 9

        FIRST = 9
        assert FIRST + P // UNIT == SLOTS

        @block.vector
        def _(v):
            st = Steps(v, v_)

            v.wait_ge(in_edges, IN_EDGES)
            v.wait_ge(consts, CONSTS)
            st.did(v.tensor_scalar(dst_w[:], e_dst[:], 1.0 / W, -0.4, ALU.mult, ALU.add))
            st.did(v.tensor_scalar(src_w[:], e_src[:], 1.0 / W, -0.4, ALU.mult, ALU.add))
            st.did(v.tensor_scalar(prev_w[:], prev_dst[:], 1.0 / W, -0.4, ALU.mult, ALU.add))
            v.tensor_scalar(ident[:], ident_row[:], ident_col[:], None, ALU.is_equal).then_inc(ident_ok, 1)
            st.wait()
            st.did(v.scalar_tensor_tensor(q_r[:], dst_w[:], -float(W), e_dst[:], ALU.mult, ALU.add))
            st.did(v.tensor_tensor(q_wt[:], dst_w[:], t_of[:, :].unsqueeze(2).to_broadcast([P, TCH, P]), ALU.add))
            st.did(v.scalar_tensor_tensor(src_d[:], src_w[:], -float(W), e_src[:], ALU.mult, ALU.add))
            st.did(v.tensor_scalar(src_c[:], src_w[:], 1.0 / PT, 0.5 / PT - 0.5, ALU.mult, ALU.add))
            st.did(v.tensor_tensor(t_lo[:], prev_w[:], t_of[:], ALU.add))
            st.did(v.scalar_tensor_tensor(t_hi[:], dst_w[:, :, P - 1], 1.0, t_of[:], ALU.add, ALU.add))
            st.wait()
            st.did(v.scalar_tensor_tensor(q_b[:], src_c[:], -float(PT), src_w[:], ALU.mult, ALU.add))
            st.did(v.scalar_tensor_tensor(src_slot[:], src_c[:], float(W), src_d[:], ALU.mult, ALU.add))
            for c in range(TCH):
                st.did(v.tensor_scalar(past[:, c, :], iota_s[:], t_lo[:, c:c + 1], None, ALU.is_ge))
            st.wait()
            st.did(v.scalar_tensor_tensor(q_key[:], src_slot[:], float(W), q_r[:], ALU.mult, ALU.add))
            for c in range(TCH):
                st.did(v.scalar_tensor_tensor(tile_at[:, c, :], iota_s[:], t_hi[:, c:c + 1], past[:, c, :], ALU.is_lt, ALU.mult))
            st.wait()
            v.nop().then_inc(q_ready, 1)

            v.wait_ge(in_x, 32)
            for n in range(SLOTS):
                st.did(v.bn_stats(stats[0:PT, n, :], acc[0:PT, n, :]))

            v.wait_ge(q_spread, 1)
            v.tensor_tensor(outside[:], psA[:], iota_s[:], ALU.not_equal).then_inc(q_used, 1)
            v.wait_ge(q_used, 1)
            v.wait_ge(q_spread, 2)
            v.scalar_tensor_tensor(r_in[:], outside[:], NO_KEY, psB[:], ALU.mult, ALU.add).then_inc(q_used, 1)
            v.wait_ge(q_spread, 3)
            v.scalar_tensor_tensor(key[:, 0:STEPS], outside[:], NO_KEY, psC[:], ALU.mult, ALU.add).then_inc(q_used, 1)
            v.wait_ge(q_spread, 4)
            v.tensor_copy(brow[:, 0:STEPS], psD[:]).then_inc(q_used, 1)
            st.wait()
            for n in range(SLOTS):
                st.did(v.bn_aggr(mv[0:PT, n, :], stats[0:PT, n, :]))
            st.wait()
            v.tensor_scalar(small[0:PT, 2, :], mv[0:PT, :, 1], 1e-5, None, ALU.add).then_inc(var_ok, 1)
            v.wait_ge(std_ok, 1)
            st.did(v.reciprocal(rstd[0:PT, :], small[0:PT, 3, :]))
            st.wait()
            st.did(v.tensor_tensor(xnorm[0:PT, :], mv[0:PT, :, 1], rstd[0:PT, :], ALU.mult))
            st.wait()
            v.tensor_tensor(xnorm[0:PT, :], xnorm[0:PT, :], rstd[0:PT, :], ALU.mult).then_inc(ss_ok, 1)
            for n in range(SLOTS):
                v.tensor_scalar(xn[0:PT, n, :], acc[0:PT, n, :], mv[0:PT, n, 0:1], rstd[0:PT, n:n + 1],
                                ALU.subtract, ALU.mult).then_inc(xn_ok, 1)
                if n == 1:
                    v.wait_ge(in_w, IN_W)
                    for k in range(2):
                        v.tensor_scalar(wcat[:, k, HID:HID + QKV], wcat[:, k, HID:HID + QKV], gpre[:, k:k + 1], None,
                                        ALU.mult).then_inc(wcat_ok, 1)
                    v.wait_ge(std_ok, 2)
                    st.did(v.tensor_scalar(xnorm[0:PT, :], xnorm[0:PT, :], 1e-12 / DIM ** 0.5, None, ALU.max))
                    st.wait()
                    v.reciprocal(xnorm[0:PT, :], xnorm[0:PT, :]).then_inc(g16_ok, 1)

            v.wait_ge(q_used, 4)
            again = P + 2 * UNIT
            st.did(v.tensor_copy(key[:, STEPS:STEPS + again], key[:, 0:again]))
            st.did(v.tensor_copy(brow[:, STEPS:STEPS + again], brow[:, 0:again]))
            for d in range(W):
                v.tensor_scalar(r_hot[:, d, :], r_in[:], float(d), None, ALU.is_equal).then_inc(rhot_ok, 1)
            v.wait_ge(q_spread, 5)
            st.did(v.tensor_tensor(w_of_s[:], s_of[:], psA[:, 0:CH], ALU.subtract))
            st.wait()
            for k in range(CH):
                v.tensor_scalar(sel[:, k, :], iota_s[:, 0:WINDOWS], w_of_s[:, k:k + 1], None, ALU.is_equal).then_inc(sel_ok, 1)
            v.wait_ge(cnt_in, 1)
            v.tensor_copy(cnt[:], psA[:, 64:64 + CH * W]).then_inc(cnt_ok, 1)
            v.wait_ge(deg_in, 1)
            v.tensor_scalar(small[0:PT, 0, :], psA[0:PT, 128:128 + SLOTS], 1.0, None, ALU.add).then_inc(deg_ok, 1)
            v.wait_ge(dsq_ok, 1)
            v.reciprocal(dinv[0:PT, :], small[0:PT, 1, :]).then_inc(dinv_ok, 1)

            def hot_unit(slot, column):
                cols = bass.ds(column, UNIT)
                for hot, n, val in ((hot_b, P, brow), (hot_k, KEYS, key)):
                    v.tensor_tensor(hot[:, slot], iota_j[:, 0:n, :].unsqueeze(1).to_broadcast([P, 2, n, GROUP]),
                                    val[:, cols].rearrange("p (g s) -> p g s", g=2).unsqueeze(2).to_broadcast([P, 2, n, GROUP]),
                                    ALU.is_equal).then_inc(hot_ready, 1)

            qv = qkv[0:PT, :, 0:HID].rearrange("p n (h d) -> p n h d", h=HEADS)
            qr = qred[0:PT, :].rearrange("p (n h) -> p n h", h=HEADS)

            def q_block(c):
                sl = slice(W * c, W * c + W)
                return qv[:, sl], qr[:, sl], qr[:, sl].unsqueeze(3).to_broadcast([PT, W, HEADS, HEAD_DIM])

            def q_softmax_end(c):
                q, r, rb = q_block(c)
                v.wait_ge(q_exp, c + 1)
                st.did(v.tensor_reduce(r, q, AX.X, ALU.add))
                st.wait()
                st.did(v.reciprocal(r, r))
                st.wait()
                v.tensor_tensor(q, q, rb, ALU.mult).then_inc(q_done, 1)

            def block_done(c):
                q, r, rb = q_block(c)
                v.wait_ge(proj_q, W * c + W)
                h = hs[0:PT, W * c:W * c + W, :]
                v.tensor_tensor(h, h, dinv[0:PT, W * c:W * c + W].unsqueeze(2).to_broadcast([PT, W, HID]), ALU.mult).then_inc(hs_ok, 1)
                st.did(v.tensor_reduce(r, q, AX.X, ALU.max))
                st.wait()
                v.tensor_tensor(q, q, rb, ALU.subtract).then_inc(q_sub, 1)
                st.did(v.tensor_reduce(kmax_of[0:PT, c, :], qkv[0:PT, W * c:W * c + W, HID:2 * HID].rearrange("p n f -> p f n"), AX.X, ALU.max))
                v.wait_ge(hs_ok, c + 1)
                st.did(v.tensor_reduce(hs_max[0:PT, c + 1:c + 2], h.rearrange("p d f -> p (d f)"), AX.X, ALU.max, apply_absolute_value=True))

            v.wait_ge(dinv_ok, 1)
            for unit in range(P // UNIT + 2):
                n = FIRST + unit - 2
                v.wait_ge(built, 2 * unit + 2)
                hot_unit(unit % 2, UNIT * unit)
                if n == FIRST + 1:
                    block_done(0)
                if n > FIRST + 1 and n % W == W - 1 and n < SLOTS - 1:
                    block_done(n // W)
                if n == FIRST + 3:
                    block_done(1)
                if n > FIRST + 3 and n % W == 3:
                    q_softmax_end(n // W - 2)
            q_softmax_end(C - 2)
            block_done(C - 1)

            st.wait()
            v.tensor_reduce(kmax[0:PT, :], kmax_of[0:PT, :, :].rearrange("p c f -> p f c"), AX.X, ALU.max).then_inc(mixdve, 1)
            v.tensor_reduce(kmax_col[:, 1:2], mem_k[:], AX.X, ALU.max).then_inc(mixdve, 1)
            v.wait_ge(mixpe, 1)
            st.did(v.tensor_reduce(kmax_col[:, 0:1], psA[:, 0:PT], AX.X, ALU.max))
            v.wait_ge(mixdve, 2)
            st.wait()
            st.did(v.tensor_tensor(kmax_col[:, 0:1], kmax_col[:, 0:1], kmax_col[:, 1:2], ALU.max))
            st.wait()
            v.tensor_scalar(kmax_mat[:], ident[:], 0.0, kmax_col[:, 0:1], ALU.mult, ALU.add).then_inc(mixdve, 1)
            def make_scale(layer):
                st.did(v.tensor_reduce(hs_max[0:PT, 0:1], hs_max[0:PT, 1:C + 1], AX.X, ALU.max))
                st.wait()
                v.nop().then_inc(max_ok, 1)
                v.wait_ge(max_in, layer + 1)
                st.did(v.tensor_reduce(top_hs[:, 0:1], psD[0:1, 768:768 + PT], AX.X, ALU.max))
                st.wait()
                st.did(v.tensor_scalar(top_hs[:, 0:1], top_hs[:, 0:1], 2.0 ** -90, None, ALU.max))
                st.wait()
                bits = top_hs[:, :].bitcast(I32)
                st.did(v.tensor_scalar(bits[:, 1:2], bits[:, 0:1], 0xFF << 23, None, ALU.bitwise_and))
                st.wait()
                st.did(v.tensor_scalar(bits[:, 2:3], bits[:, 1:2], -1.0, float((2 * 127 + 14) << 23), ALU.mult, ALU.add))
                st.did(v.tensor_scalar(bits[:, 3:4], bits[:, 1:2], float((14 - 7) << 23), None, ALU.subtract))
                st.wait()
                v.nop().then_inc(pow_ok, 1)
                v.wait_ge(pow_in, layer + 1)
                st.did(v.tensor_copy(scale[:, :], psD[:, 896:898]))
                st.wait()
                v.nop().then_inc(scale_ok, 1)

            def hs_low(c, n):
                v.wait_ge(hs_hi, n + 1)
                v.scalar_tensor_tensor(hs2[0:PT, bass.ds(W * c, W), 1, :], hs[0:PT, bass.ds(W * c, W), :], scale[0:PT, 0:1],
                                       hs2[0:PT, bass.ds(W * c, W), 0, :], ALU.mult, ALU.subtract).then_inc(hs_lo, 1)

            v.wait_ge(mixpe, 2)
            kv_ = qkv[0:PT, :, HID:2 * HID]
            v.tensor_tensor(kv_, kv_, psA[0:PT, 256:256 + HID].unsqueeze(1).to_broadcast([PT, SLOTS, HID]),
                            ALU.subtract).then_inc(mixdve, 1)
            v.tensor_copy(memvT[:, 0:P], psB[0:MEM, 256:256 + P]).then_inc(mixdve, 1)
            st.did(v.tensor_copy(memkT[:], psB[0:MEM, 0:P]))
            st.wait()
            v.tensor_tensor(memkT[:], memkT[:], psA[0:MEM, 256:256 + HID], ALU.subtract).then_inc(mixdve, 1)
            v.memset(memvT[:, P:P + 1], 1.0).then_inc(mixdve, 1)
            v.memset(ctx_m[:], 0.0).then_inc(mixdve, 1)
            v.memset(qkv[0:PT, :, QKV:QKV + 1], 1.0).then_inc(mixdve, 1)
            make_scale(0)
            q_softmax_end(C - 1)
            with v.Fori(0, C) as c:
                hs_low(c, c)
            v.wait_ge(mixpe, 3)
            st.did(v.tensor_copy(ctx_sb[:], psB[:, 512:512 + P + 1]))
            st.wait()
            st.did(v.reciprocal(zinv[:], ctx_sb[:, P:P + 1]))
            st.wait()
            v.wait_ge(mixdve, 9)
            for h in range(HEADS):
                s = slice(h * HEAD_DIM, (h + 1) * HEAD_DIM)
                v.tensor_scalar(ctx_m[s, s], ctx_sb[s, s], zinv[s, :], HEAD_DIM ** -0.5, ALU.mult, ALU.mult).then_inc(mixdve, 1)
            v.wait_ge(mixpe, 4)
            v.tensor_copy(ctxT[:], psB[:, 0:P]).then_inc(mixdve, 1)
            v.wait_ge(wr_in, 1)
            v.tensor_copy(wr[:], psD[:, 0:2 * EXPERTS].rearrange("p (k e) -> p k e", k=2)).then_inc(wr_ok, 1)
            v.tensor_copy(eb1[:], psD[:, 128:128 + 2 * EXPERTS]).then_inc(wr_ok, 1)
            st.did(v.tensor_copy(eb2[:], eb2_raw[:]))
            st.wait()
            st.did(v.tensor_tensor(eb2[32:64, :], eb2_raw[32:64, :], eb2[32:64, :].bitcast(F32), ALU.subtract))
            v.wait_ge(mixpe, 5)
            v.tensor_copy(wmix[:], psB[:, 256:256 + DIM]).then_inc(mixdve, 1)
            for g, (n0, tiles) in enumerate(TILE_GROUPS):
                v.wait_ge(mo_in, g + 1)
                v.tensor_tensor(mix[0:PT, n0:n0 + tiles, :], (psC, psB)[g % 2][0:PT, 0:DIM * tiles].rearrange("p (t f) -> p t f", f=DIM),
                                bout_all[0:PT, :].unsqueeze(1).to_broadcast([PT, tiles, DIM]), ALU.add).then_inc(mo_ok, 1)
            v.wait_ge(mss_ok, 1)
            st.did(v.tensor_scalar(small[0:PT, 3, :], small[0:PT, 3, :], 1e-12, 1.0 / DIM ** 0.5, ALU.max, ALU.mult))
            st.wait()
            v.reciprocal(mnorm[0:PT, :], small[0:PT, 3, :]).then_inc(norm_ok, 1)

            v.nop().then_inc(sums_free, 2)
            v.nop().then_inc(merge_used, 1)
            v.nop().then_inc(hs_ok, 1)
            v.nop().then_inc(g2_ok, 2)
            v.wait_ge(norm_ok, 1)
            v.wait_ge(proj_h, SLOTS)
            st.wait()
            def hot_units(count, chunk, first, g):
                with v.Fori(0, count) as i:
                    for u in range(2):
                        v.wait_ge(built, 4 * i + 2 * (first + u + 1) + g)
                        hot_unit(u, 2 * UNIT * i + P * chunk + UNIT * (first + u))

            for layer in range(2):
                k0, g0 = CH * layer, GROUPS * (1 + CH * layer)
                def two_chunks(kp, last):
                    for par in range(2):
                        if not (last and par):
                            hot_units(7 if last else 8, 2 * kp + par + 1, 2, 2 * GROUPS * kp + (g0 + GROUPS * par))
                        v.wait_ge(hi_ok, 2 * kp + (k0 + par + 1))
                        hi_p, lo_p = (part2[:, part, bass.ds(2 * kp + par, 1), :].rearrange("p a f -> p (a f)") for part in range(2))
                        v.scalar_tensor_tensor(lo_p, (psB, psC)[par][:, 0:W * HID], 1.0 / P, hi_p, ALU.mult, ALU.subtract).then_inc(sums_free, 1)

                with v.Fori(0, CH // 2 - layer) as kp:
                    two_chunks(kp, False)
                if layer:
                    two_chunks(CH // 2 - 1, True)
                def post_of(c, ps=psD):
                    dv = dinv[0:PT, bass.ds(W * c, W)].unsqueeze(2).to_broadcast([PT, W, HID])
                    v.wait_ge(merged, c + (C * layer + 1))
                    v.scalar_tensor_tensor(post_v, ps[0:PT, 0:W * HID].rearrange("p (d f) -> p d f", d=W), scale[0:PT, 1:2],
                                           hs[0:PT, bass.ds(W * c, W), :], ALU.mult, ALU.add).then_inc(merge_used, 1)
                    v.wait_ge(merge_used, c + (C * layer + 2))
                    return dv

                post_v = post[0:PT, :].rearrange("p (d f) -> p d f", d=W)
                if layer == 0:
                    for c in range(C):
                        v.wait_ge(hs_ok, c + (C + 1))
                        dv = post_of(c, (psD, psA)[c % 2])
                        st.did(v.tensor_tensor(post_v, post_v, dv, ALU.mult))
                        st.wait()
                        st.did(v.tensor_tensor(post_v, post_v, b1_all[0:PT, :].unsqueeze(1).to_broadcast([PT, W, HID]), ALU.add))
                        st.wait()
                        v.scalar_tensor_tensor(hs[0:PT, bass.ds(W * c, W), :], post_v, 0.0, dv, ALU.max, ALU.mult).then_inc(hs_ok, 1)
                        v.wait_ge(hs_ok, c + (C + 2))
                        st.did(v.tensor_reduce(hs_max[0:PT, bass.ds(c + 1, 1)], hs[0:PT, bass.ds(W * c, W), :].rearrange("p d f -> p (d f)"),
                                               AX.X, ALU.max))
                    st.wait()
                    make_scale(1)
                    with v.Fori(0, C) as c:
                        hs_low(c, c + C)

            def token_low(c):
                v.wait_ge(tt_hi, c + 1)
                cols = slice(W * PT * c, W * PT * (c + 1))
                v.tensor_tensor(tokT_lo[:, :, cols], tokT[:], tokT_hi[:, :, cols].bitcast(F32), ALU.subtract).then_inc(tt_lo, 1)

            def post2(c):
                if c:
                    v.wait_ge(at_in, c + 1)
                dv = post_of(c)
                v.tensor_tensor(post_v, post_v, dv, ALU.mult).then_inc(post_ok, 1)

            layer = 1
            post2(0)
            for c in range(C):
                a = acc[0:PT, W * c:W * c + W, :]
                if c == 0:
                    v.wait_ge(mixdone, 1)
                v.wait_ge(g2_in, c + 2)
                v.tensor_tensor(a[:, 0:4, :], psB[0:PT, :].rearrange("p (d f) -> p d f", d=4), a[:, 0:4, :], ALU.add).then_inc(g2_ok, 1)
                v.tensor_tensor(a[:, 4:5, :], psC[0:PT, 0:DIM].rearrange("p (d f) -> p d f", d=1), a[:, 4:5, :], ALU.add).then_inc(g2_ok, 1)
                v.wait_ge(g2_ok, 2 * c + 4)
                for d in range(W):
                    st.did(v.bn_stats(stats[0:PT, d, :], a[:, d, :]))
                st.wait()
                for d in range(W):
                    st.did(v.bn_aggr(mv[0:PT, d, :], stats[0:PT, d, :]))
                st.wait()
                v.tensor_scalar(small[0:PT, 2, 0:W], mv[0:PT, 0:W, 1], 1e-5, None, ALU.add).then_inc(var_ok, 1)
                if c < C - 1:
                    post2(c + 1)
                if c:
                    v.wait_ge(tok_ok, c)
                    b = acc[0:PT, W * (c - 1):W * c, :]
                    v.tensor_tensor(b, b, tok[0:PT], ALU.add).then_inc(tok_added, 1)
                v.wait_ge(std_ok, c + 3)
                st.did(v.reciprocal(rstd[0:PT, 0:W], small[0:PT, 3, 0:W]))
                st.wait()
                if c:
                    v.wait_ge(tok_added, c)
                    v.wait_ge(tt_in, c)
                for d in range(W):
                    ins = v.tensor_scalar(tok[0:PT, d, :], a[:, d, :], mv[0:PT, d, 0:1], rstd[0:PT, d:d + 1], ALU.subtract, ALU.mult)
                    if d < W - 1:
                        st.did(ins)
                ins.then_inc(tok_ok, 1)
                if c:
                    token_low(c - 1)
            v.wait_ge(tok_ok, C)
            st.did(v.tensor_tensor(acc[0:PT, W * (C - 1):SLOTS, :], acc[0:PT, W * (C - 1):SLOTS, :], tok[0:PT], ALU.add))
            token_low(C - 1)

            st.did(v.memset(comb3[0:PT], 0.0))
            v.wait_ge(logit_in, C)
            st.did(v.tensor_copy(logit[0:PT], psC[0:PT, 768:768 + SLOTS * EXPERTS].rearrange("p (n e) -> p n e", e=EXPERTS)))
            st.wait()
            for n in range(SLOTS):
                st.did(v.max(top[0:PT, n, :], logit[0:PT, n, :]))
            st.wait()
            for n in range(SLOTS):
                st.did(v.max_index(topi[0:PT, n, :], top[0:PT, n, :], logit[0:PT, n, :]))
            v.tensor_tensor(prob[0:PT], logit[0:PT], top[0:PT, :, 0:1].to_broadcast([PT, SLOTS, EXPERTS]), ALU.subtract).then_inc(lg_ok, 1)
            st.wait()
            for j in range(2):
                st.did(v.tensor_tensor(pick[0:PT, j], ident_row[0:PT, 0:EXPERTS].unsqueeze(1).to_broadcast([PT, SLOTS, EXPERTS]),
                                       topi[0:PT, :, j:j + 1].to_broadcast([PT, SLOTS, EXPERTS]), ALU.is_equal))
            st.wait()
            st.did(v.tensor_tensor(pick[0:PT, 0], pick[0:PT, 0], pick[0:PT, 1], ALU.add))
            v.wait_ge(ex_ok, 1)
            st.did(v.tensor_reduce(small[0:PT, 0, :], prob[0:PT], AX.X, ALU.add))
            st.wait()
            st.did(v.reciprocal(small[0:PT, 1, :], small[0:PT, 0, :]))
            st.wait()
            st.did(v.tensor_tensor(prob[0:PT], prob[0:PT], small[0:PT, 1, :].unsqueeze(2).to_broadcast([PT, SLOTS, EXPERTS]), ALU.mult))
            st.wait()
            st.did(v.tensor_tensor(prob[0:PT], prob[0:PT], pick[0:PT, 0], ALU.mult))
            st.wait()
            st.did(v.tensor_reduce(small[0:PT, 0, :], prob[0:PT], AX.X, ALU.add))
            st.wait()
            st.did(v.tensor_scalar(small[0:PT, 0, :], small[0:PT, 0, :], 1e-12, None, ALU.max))
            st.wait()
            st.did(v.reciprocal(small[0:PT, 1, :], small[0:PT, 0, :]))
            st.wait()
            v.tensor_tensor(comb[0:PT], prob[0:PT], small[0:PT, 1, :].unsqueeze(2).to_broadcast([PT, SLOTS, EXPERTS]), ALU.mult).then_inc(comb_made, 1)
            v.wait_ge(comb_made, 1)
            st.did(v.tensor_copy(comb_hi[0:PT], comb[0:PT]))
            st.wait()
            st.did(v.tensor_copy(comb3[0:PT, :, 0:EXPERTS], comb_hi[0:PT].bitcast(F32)))
            st.did(v.tensor_copy(comb3[0:PT, :, 32:32 + EXPERTS], comb_hi[0:PT].bitcast(F32)))
            st.did(v.tensor_tensor(comb3[0:PT, :, 64:64 + EXPERTS], comb[0:PT], comb_hi[0:PT].bitcast(F32), ALU.subtract))
            st.wait()
            v.nop().then_inc(comb_ok, 1)
            def add_bias2(g, n0, tiles):
                v.wait_ge(eb_in, g + 1)
                a = acc[0:PT, bass.ds(n0, tiles), :]
                v.tensor_tensor(a, a, (psC, psD)[g % 2][0:PT, 0:DIM * tiles].rearrange("p (t f) -> p t f", f=DIM), ALU.add).then_inc(eb_ok, 1)

            st.wait()
            for g in range(7):
                add_bias2(g, 4 * g, 4 if g < 6 else 1)
            v.wait_ge(eb_ok, 7)

            def take(base, n0, tiles, f):
                v.wait_ge(down, base + (f + 3))
                v.wait_ge(y_free, base + (f + 2))
                for t in range(tiles):
                    a = acc[0:PT, bass.ds(n0 + t, 1), :].rearrange("p a f -> p (a f)")
                    cw = comb[0:PT, bass.ds(n0 + t, 1), f:f + 1].rearrange("p a e -> p (a e)")
                    y = v.scalar_tensor_tensor(a, (psC, psD)[f % 2][0:PT, DIM * t:DIM * t + DIM], cw, a, ALU.mult, ALU.add)
                y.then_inc(y_free, 1)

            def expert_group(base, n0, tiles, size):
                for e in range(EXPERTS + 1):
                    if e < EXPERTS:
                        v.wait_ge(down, base + (e + 1))
                        for h in range(2):
                            v.wait_ge(h_hi_ok, 2 * base + (2 * e + h + 1))
                            v.tensor_tensor(h_lo[:, e % 2, h, 0:size], g_sb[:, e % 2, h, 0:size], h_hi[:, e % 2, h, 0:size].bitcast(F32),
                                            ALU.subtract).then_inc(h_lo_ok, 1)
                    if e:
                        take(base, n0, tiles, e - 1)

            v.nop().then_inc(y_free, 2)
            v.nop().then_inc(h_lo_ok, 4)
            with v.Fori(0, 6) as g:
                expert_group(EXPERTS * g, 4 * g, 4, 4 * PT)
            expert_group(6 * EXPERTS, 24, 1, PT + 1)

        @block.tensor
        def _(pe):
            pe.wait_ge(q_ready, 1)
            for q, ps in ((q_wt, psA), (q_r, psB), (q_key, psC), (q_b, psD)):
                for half in range(2):
                    for c in range(TCH):
                        k = P if c < TCH - 1 else TLAST
                        m = pe.matmul(ps[:, 512 * half:512 * half + 512], q[0:k, c, :], tile_at[0:k, c, 512 * half:512 * half + 512],
                                      start=(c == 0), stop=(c == TCH - 1))
                m.then_inc(q_spread, 1)
            pe.wait_ge(q_used, 1)
            for k in range(CH):
                for c in range(TCH):
                    n = P if c < TCH - 1 else TLAST
                    m = pe.matmul(psA[:, k:k + 1], tile_at[0:n, c, P * k:P * k + P], t_of16[0:n, c:c + 1], start=(c == 0), stop=(c == TCH - 1))
            m.then_inc(q_spread, 1)
            def degrees():
                pe.wait_ge(rhot_ok, W)
                pe.wait_ge(sel_ok, CH)
                for k in range(CH):
                    for d in range(W):
                        m = pe.matmul(psA[:, 64 + W * k + d:65 + W * k + d], r_hot[:, d, P * k:P * k + P], ones16[:, 0:1], start=True, stop=True)
                m.then_inc(cnt_in, 1)
                pe.wait_ge(cnt_ok, 1)
                for c in range(C):
                    for k in range(CH):
                        m = pe.matmul(psA[0:PT, 128 + W * c:128 + W * c + W], sel[:, k, PT * c:PT * c + PT], cnt[:, W * k:W * k + W],
                                      start=(k == 0), stop=(k == CH - 1))
                m.then_inc(deg_in, 1)

            pe.wait_ge(ident_ok, 1)
            pe.wait_ge(q_used, 4)

            def transposes(n):
                pe.wait_ge(xn_ok, n + 1)
                if n >= 2:
                    pe.wait_ge(xt_ok, n - 1)
                for k in range(2):
                    m = pe.transpose(psB[:, 512 * (n % 2) + P * k:512 * (n % 2) + P * k + PT], xn[0:PT, n, P * k:P * k + P], ident[0:PT, 0:PT])
                m.then_inc(xt_in, 1)

            def project(n):
                if n == 0:
                    pe.wait_ge(wcat_ok, 2)
                pe.wait_ge(xt_ok, n + 1)
                if n >= 2:
                    pe.wait_ge(proj_h, n - 1)
                    pe.wait_ge(proj_q, n - 1)
                for k in range(2):
                    m = pe.matmul(psC[0:PT, 512 * (n % 2):512 * (n % 2) + 512], xnT[:, n % 2, k, :], wcat[:, k, :], start=(k == 0), stop=(k == 1))
                m.then_inc(proj, 1)

            def build(g, j, slot):
                if j % 2 == 0:
                    pe.wait_ge(hot_ready, g + 2)
                bank = 512 * (j % 2)
                for q in range(GROUP):
                    m = pe.matmul(psA[:, bank + KEYS * q:bank + KEYS * q + KEYS], hot_b[:, slot, j % 2, :, q], hot_k[:, slot, j % 2, :, q],
                                  start=True, stop=True)
                m.then_inc(built, 1)

            pe.nop().then_inc(built, 4)
            transposes(0)
            for n in range(SLOTS):
                if n + 1 < SLOTS:
                    transposes(n + 1)
                project(n)
                if n == FIRST - 3:
                    degrees()
                if n >= FIRST:
                    for j in range(2):
                        g = 2 * (n - FIRST) + j
                        pe.wait_ge(counts_ok, g + 1)
                        build(g, j, (n - FIRST) % 2)

            def spread_scale(layer):
                pe.wait_ge(max_ok, layer + 1)
                pe.transpose(psD[0:1, 768:768 + PT], hs_max[0:PT, 0:1], ident[0:PT, 0:PT]).then_inc(max_in, 1)
                pe.wait_ge(pow_ok, layer + 1)
                pe.matmul(psD[:, 896:898], ones_row[:, :], top_hs[:, 2:4], start=True, stop=True).then_inc(pow_in, 1)

            pe.wait_ge(mixdve, 1)
            pe.wait_ge(counts_ok, GROUPS + 2)
            pe.transpose(psA[:, 0:PT], kmax[0:PT, :], ident[0:PT, 0:PT]).then_inc(mixpe, 1)
            pe.wait_ge(mixdve, 3)
            pe.wait_ge(proj_q, SLOTS)
            pe.transpose(psB[0:MEM, 0:P], mem_k[:], ident[:, :])
            pe.transpose(psB[0:MEM, 256:256 + P], mem_v[:], ident[:, :])
            pe.matmul(psA[:, 256:256 + P], kmax_mat[:], ident[:, :], start=True, stop=True).then_inc(mixpe, 1)
            spread_scale(0)
            pe.wait_ge(mixact, 2)
            pe.wait_ge(mixdve, 9)
            for n in range(SLOTS):
                pe.matmul(psB[:, 512:512 + P + 1], qkv[0:PT, n, HID:2 * HID], qkv[0:PT, n, 2 * HID:3 * HID + 1], start=(n == 0), stop=False)
            pe.matmul(psB[:, 512:512 + P + 1], memkT[:], memvT[:], start=False, stop=True).then_inc(mixpe, 1)
            pe.wait_ge(mixdve, 13)
            pe.transpose(psB[:, 0:P], ctx_m[:], ident[:, :]).then_inc(mixpe, 1)
            pe.wait_ge(mixdve, 14)
            pe.matmul(psB[:, 256:256 + DIM], ctxT[:], wout[:], start=True, stop=True).then_inc(mixpe, 1)
            pe.wait_ge(q_done, C)

            def q_transposes(g):
                if g >= 2:
                    pe.wait_ge(qt_ok, g - 1)
                n0, tiles = TILE_GROUPS[g]
                for t in range(tiles):
                    m = pe.transpose(psD[:, 512 * (g % 2) + PT * t:512 * (g % 2) + PT * t + PT], qkv[0:PT, n0 + t, 0:HID], ident[0:PT, 0:PT])
                m.then_inc(qt_in, 1)

            for k in range(2):
                pe.transpose(psD[:, EXPERTS * k:EXPERTS * k + EXPERTS], rw_nat[:, P * k:P * k + P], ident[0:EXPERTS, 0:EXPERTS])
            pe.transpose(psD[:, 128:128 + 2 * EXPERTS], eb1_nat[:], ident[0:2 * EXPERTS, 0:2 * EXPERTS]).then_inc(wr_in, 1)
            pe.wait_ge(mixpe, 5)
            pe.wait_ge(mixdve, 15)
            pe.wait_ge(wr_ok, 2)
            q_transposes(0)
            for g, (n0, tiles) in enumerate(TILE_GROUPS):
                if g + 1 < len(TILE_GROUPS):
                    q_transposes(g + 1)
                pe.wait_ge(qt_ok, g + 1)
                if g >= 2:
                    pe.wait_ge(mo_ok, g - 1)
                for t in range(tiles):
                    m = pe.matmul((psC, psB)[g % 2][0:PT, DIM * t:DIM * t + DIM], qT[:, g % 2, PT * t:PT * t + PT], wmix[:], start=True, stop=True)
                m.then_inc(mo_in, 1)

            def add_slot(par, a, start):
                ca = counts5[0:PT, par, a, :, :]
                ha = hs2[0:PT, a, :, :]
                for d in range(W):
                    for part in range(2):
                        m = pe.matmul((psB, psC)[par][:, HID * d:HID * d + HID], ca[:, d, :], ha[:, part, :],
                                      start=start and part == 0 and d % 4 == 0, stop=part == 1, skip_group_check=True)
                return m

            def merge(c, used, ps=psD):
                pe.wait_ge(merge_used, used)
                for lo, hi in ((0, 512), (512, W * HID)):
                    for k in range(CH):
                        for part in range(2):
                            m = pe.matmul(ps[0:PT, lo:hi], sel[:, k, bass.ds(PT * c, PT)], part2[:, part, k, lo:hi],
                                          start=(k == 0 and part == 0), stop=(k == CH - 1 and part == 1))
                m.then_inc(merged, 1)

            pe.nop().then_inc(down, 2)
            pe.wait_ge(consts, 9)
            pe.nop().then_inc(at_in, 1)
            pe.nop().then_inc(g2_in, 1)
            pe.nop().then_inc(summed, 1)
            pe.wait_ge(mo_ok, len(TILE_GROUPS))
            for layer in range(2):
                k0, g0 = CH * layer, GROUPS * (1 + CH * layer)
                if layer:
                    spread_scale(layer)
                def two_chunks(kp, last):
                    for par in range(2):
                        pe.wait_ge(counts_ok, 2 * GROUPS * kp + (g0 + GROUPS * par + 2))
                        pe.wait_ge(sums_free, 2 * kp + (k0 + par + 1))
                        pe.wait_ge(hs_lo, C * layer + 1)
                        add_slot(par, 0, True)
                        due = 1
                        for j in range(0 if last and par else GROUPS):
                            g = 2 * GROUPS * kp + (g0 + GROUPS * par + j)
                            pe.wait_ge(counts_ok, g + 1)
                            build(g, j, j // 2 % 2)
                            while GROUPS * due < (SLOTS - 2) * (j + 1):
                                if due % W == 0:
                                    pe.wait_ge(hs_lo, C * layer + due // W + 1)
                                add_slot(par, due, False)
                                due += 1
                        for a in range(due, SLOTS):
                            m = add_slot(par, a, False)
                        m.then_inc(summed, 1)

                with pe.Fori(0, CH // 2 - layer) as kp:
                    two_chunks(kp, False)
                if layer:
                    two_chunks(CH // 2 - 1, True)
                pe.wait_ge(sums_free, k0 + CH + 2)
                if layer == 0:
                    pe.wait_ge(counts_ok, GROUPS * (CH + 1) + 2)
                    for c in range(C):
                        merge(c, max(c, 1), (psD, psA)[c % 2])

            def post_transposes(c):
                pe.wait_ge(post_ok, c + 1)
                if c:
                    pe.wait_ge(tt_ok, 3 * c)
                for d in range(W):
                    m = pe.transpose(psA[:, P * d:P * d + PT], post[0:PT, HID * d:HID * d + HID], ident[0:PT, 0:PT])
                m.then_inc(at_in, 1)

            def times_w2(c):
                pe.wait_ge(at_ok, c + 1)
                pe.wait_ge(g2_ok, 2 * c + 2)
                for d in range(W):
                    o = psB[0:PT, DIM * d:DIM * d + DIM] if d < 4 else psC[0:PT, 0:DIM]
                    m = pe.matmul(o, aggT[:, d, 0:PT], w2g[:], start=True, stop=True)
                m.then_inc(g2_in, 1)

            def token_transposes(c):
                pe.wait_ge(tok_ok, c + 1)
                pe.wait_ge(tt_ok, 3 * c + 3)
                for j in range(2 * W):
                    o = psA[:, P * j:P * j + PT] if j < 8 else psC[:, 512 + P * (j - 8):512 + P * (j - 8) + PT]
                    m = pe.transpose(o, tok[0:PT, j % W, P * (j // W):P * (j // W) + P], ident[0:PT, 0:PT])
                m.then_inc(tt_in, 1)

            THREE = ((0, 0), (0, 1), (1, 0))

            def logits(c):
                pe.wait_ge(tt_ok, 3 * c + 6)
                for d in range(W):
                    out_cols = psC[0:PT, bass.ds(768 + EXPERTS * W * c + EXPERTS * d, EXPERTS)]
                    for k in range(2):
                        m = pe.matmul(out_cols, tokT[:, k, PT * d:PT * d + PT], wr[:, k, :], start=(k == 0), stop=(k == 1))
                m.then_inc(logit_in, 1)

            merge(0, C + 1)
            for c in range(C):
                post_transposes(c)
                times_w2(c)
                if c < C - 1:
                    merge(c + 1, C + c + 2)
                if c >= 2:
                    logits(c - 2)
                if c >= 1:
                    token_transposes(c - 1)
            logits(C - 2)
            token_transposes(C - 1)
            logits(C - 1)

            def comb_transposes(g, tiles):
                if g == 0:
                    pe.wait_ge(comb_ok, 1)
                if g >= 2:
                    pe.wait_ge(ct_ok, g - 1)
                for t in range(tiles):
                    m = pe.transpose(psA[0:96, 512 * (g % 2) + PT * t:512 * (g % 2) + PT * t + PT], comb3[0:PT, 4 * g + t, :], ident[0:PT, 0:PT])
                m.then_inc(ct_in, 1)

            def bias2(g, tiles):
                pe.wait_ge(ct_ok, g + 1)
                if g >= 2:
                    pe.wait_ge(eb_ok, g - 1)
                for t in range(tiles):
                    m = pe.matmul((psC, psD)[g % 2][0:PT, DIM * t:DIM * t + DIM], combT[:, g % 2, PT * t:PT * t + PT], eb2[:], start=True, stop=True)
                m.then_inc(eb_in, 1)

            comb_transposes(0, 4)
            for g in range(7):
                if g < 6:
                    comb_transposes(g + 1, 4 if g < 5 else 1)
                bias2(g, 4 if g < 6 else 1)

            def up(E, cols, size, e):
                pe.wait_ge(g_ok, 2 * E + 2)
                for h in range(2):
                    for i, (a, b) in enumerate(THREE):
                        for k in range(2):
                            m = pe.matmul((psA, psB)[e % 2][:, 512 * h:512 * h + size], (w_hi, w_lo)[a][:, 0, e, k, P * h:P * h + P],
                                          (tokT_hi, tokT_lo)[b][:, k, bass.ds(cols, size)], start=(i == 0 and k == 0), stop=(i == 2 and k == 1))
                    m.then_inc(upped, 1)

            def group(base, cols, size, tiles):
                for e in range(EXPERTS + 1):
                    if e < EXPERTS:
                        up(base + e, cols, size, e)
                    if e:
                        f = e - 1
                        pe.wait_ge(h_lo_ok, 2 * base + (2 * f + 6))
                        pe.wait_ge(y_free, base + (f + 1))
                        for t in range(tiles):
                            q = size - tiles * PT + PT * t
                            for i, (a, b) in enumerate(THREE):
                                for k in range(2):
                                    m = pe.matmul((psC, psD)[f % 2][0:PT, DIM * t:DIM * t + DIM], (h_hi, h_lo)[a][:, f % 2, k, q:q + PT],
                                                  (w_hi, w_lo)[b][:, 1, f, k, :], start=(i == 0 and k == 0), stop=(i == 2 and k == 1))
                        m.then_inc(down, 1)

            pe.wait_ge(w_lo_ok, 2)
            pe.wait_ge(eb_ok, 7)
            with pe.Fori(0, 6) as g:
                group(EXPERTS * g, 4 * PT * g, 4 * PT, 4)
            group(6 * EXPERTS, 24 * PT - 1, PT + 1, 1)

        @block.scalar
        def _(act):
            sa = Steps(act, a_)
            act.wait_ge(var_ok, 1)
            act.activation(small[0:PT, 3, :], small[0:PT, 2, :], ACT.Sqrt).then_inc(std_ok, 1)
            act.wait_ge(ss_ok, 1)
            act.activation(xnorm[0:PT, :], xnorm[0:PT, :], ACT.Sqrt).then_inc(std_ok, 1)
            act.wait_ge(g16_ok, 1)
            act.nop().then_inc(counts_ok, 2)

            def xn_copy(n):
                act.wait_ge(xt_in, n + 1)
                if n >= 2:
                    act.wait_ge(proj, n - 1)
                act.copy(xnT[:, n % 2, :, :], psB[:, 512 * (n % 2):512 * (n % 2) + 256].rearrange("p (k q) -> p k q", k=2)[:, :, 0:PT]).then_inc(xt_ok, 1)

            def q_exponential(c):
                act.wait_ge(q_sub, c + 1)
                act.activation(qkv[0:PT, W * c:W * c + W, 0:HID], qkv[0:PT, W * c:W * c + W, 0:HID], ACT.Exp).then_inc(q_exp, 1)

            def take_counts(g, par, j, col):
                act.wait_ge(built, g + 5)
                act.copy(counts[:, par, :, bass.ds(col, GROUP)].rearrange("p j s -> p s j"),
                         psA[:, 512 * (j % 2):512 * (j % 2) + GROUP * KEYS].rearrange("p (s j) -> p s j", s=GROUP)).then_inc(counts_ok, 1)

            xn_copy(0)
            for n in range(SLOTS):
                if n + 1 < SLOTS:
                    xn_copy(n + 1)
                act.wait_ge(proj, n + 1)
                act.copy(hs[0:PT, n, :], psC[0:PT, 512 * (n % 2):512 * (n % 2) + HID]).then_inc(proj_h, 1)
                act.activation(qkv[0:PT, n, 0:QKV], psC[0:PT, 512 * (n % 2) + HID:512 * (n % 2) + 512], ACT.Copy,
                               scale=xnorm[0:PT, n:n + 1]).then_inc(proj_q, 1)
                if n == FIRST - 2:
                    act.wait_ge(deg_ok, 1)
                    act.activation(small[0:PT, 1, :], small[0:PT, 0, :], ACT.Sqrt).then_inc(dsq_ok, 1)
                if n >= FIRST:
                    for j in range(2):
                        g = 2 * (n - FIRST) + j
                        take_counts(g, 0, j, GROUP * g)
                if n > FIRST + 2 and n % W == 2:
                    q_exponential(n // W - 2)
            q_exponential(C - 2)
            q_exponential(C - 1)
            act.wait_ge(mixdve, 4)
            act.activation(qkv[0:PT, :, HID:2 * HID], qkv[0:PT, :, HID:2 * HID], ACT.Exp).then_inc(mixact, 1)
            act.wait_ge(mixdve, 6)
            act.activation(memkT[:], memkT[:], ACT.Exp).then_inc(mixact, 1)
            def hs_high(layer):
                act.wait_ge(scale_ok, layer + 1)
                with act.Fori(0, C) as c:
                    act.activation(hs2[0:PT, bass.ds(W * c, W), 0, :], hs[0:PT, bass.ds(W * c, W), :], ACT.Copy, scale=scale[0:PT, 0:1]).then_inc(hs_hi, 1)

            hs_high(0)

            def squares(g):
                act.wait_ge(mo_ok, g + 1)
                for n in range(4 * g, min(4 * g + 4, SLOTS)):
                    sa.did(act.activation(xn[0:PT, n, :], mix[0:PT, n, :], ACT.Square, accum_out=small[0:PT, 2, n:n + 1]))

            act.wait_ge(xn_free, 1)
            for g, (n0, tiles) in enumerate(TILE_GROUPS):
                act.wait_ge(qt_in, g + 1)
                if g >= 2:
                    act.wait_ge(mo_in, g - 1)
                act.copy(qT[:, g % 2, 0:PT * tiles], psD[:, 512 * (g % 2):512 * (g % 2) + PT * tiles]).then_inc(qt_ok, 1)
                if g:
                    squares(g - 1)
            squares(len(TILE_GROUPS) - 1)
            sa.wait()
            act.activation(small[0:PT, 3, :], small[0:PT, 2, :], ACT.Sqrt).then_inc(mss_ok, 1)

            act.nop().then_inc(g_ok, 4)
            act.nop().then_inc(tt_ok, 3)
            act.preload_act_table(ACT.Copy)

            act.wait_ge(xadd_ok, 1)
            for layer in range(2):
                k0, g0 = CH * layer, GROUPS * (1 + CH * layer)
                if layer:
                    act.wait_ge(merged, C)
                def two_chunks(kp, last):
                    for par in range(2):
                        if not (last and par):
                            act.wait_ge(summed, 2 * kp + (k0 + par + 1))
                            with act.Fori(0, 8) as i:
                                for j in range(4):
                                    take_counts(2 * GROUPS * kp + 4 * i + (g0 + GROUPS * par + j), 1 - par, j, 4 * GROUP * i + GROUP * j)
                        act.wait_ge(summed, 2 * kp + (k0 + par + 2))
                        act.activation(part2[:, 0, bass.ds(2 * kp + par, 1), :].rearrange("p a f -> p (a f)"), (psB, psC)[par][:, 0:W * HID],
                                       ACT.Copy, scale=1.0 / P).then_inc(hi_ok, 1)

                with act.Fori(0, CH // 2 - layer) as kp:
                    two_chunks(kp, False)
                if layer:
                    two_chunks(CH // 2 - 1, True)
                if layer == 0:
                    hs_high(1)

            def agg_copy(c):
                act.wait_ge(at_in, c + 2)
                act.wait_ge(g2_in, c + 1)
                act.copy(aggT[:, :, 0:PT], psA[:, 0:W * P].rearrange("p (d q) -> p d q", d=W)[:, :, 0:PT]).then_inc(at_ok, 1)

            def std(c):
                act.wait_ge(var_ok, c + 2)
                act.activation(small[0:PT, 3, 0:W], small[0:PT, 2, 0:W], ACT.Sqrt).then_inc(std_ok, 1)

            def token_high(c):
                act.wait_ge(tt_in, c + 1)
                if c:
                    act.wait_ge(logit_in, c)
                    act.wait_ge(tt_lo, c)
                for k, d0, d1, ps in TOKEN_PARTS:
                    act.copy(tokT[:, k, PT * d0:PT * d1].rearrange("p (d q) -> p d q", q=PT),
                             ps.rearrange("p (d q) -> p d q", q=P)[:, :, 0:PT]).then_inc(tt_ok, 1)
                act.wait_ge(tt_ok, 3 * c + 6)
                act.copy(tokT_hi[:, :, W * PT * c:W * PT * (c + 1)], tokT[:]).then_inc(tt_hi, 1)

            def weights_high(i):
                act.wait_ge((in_w1, in_w2)[i], 16)
                act.copy(w_hi[:, i], w_raw[:, i]).then_inc(w_hi_ok, 1)

            for c in range(C):
                agg_copy(c)
                std(c)
                if c:
                    token_high(c - 1)
                if c in (1, 3):
                    weights_high(c // 2)
            token_high(C - 1)

            act.wait_ge(lg_ok, 1)
            act.activation(prob[0:PT], prob[0:PT], ACT.Exp).then_inc(ex_ok, 1)
            for g in range(7):
                size = PT * (4 if g < 6 else 1)
                act.wait_ge(ct_in, g + 1)
                if g >= 2:
                    act.wait_ge(eb_in, g - 1)
                act.copy(combT[:, g % 2, 0:size], psA[0:96, 512 * (g % 2):512 * (g % 2) + size]).then_inc(ct_ok, 1)
            act.preload_act_table(ACT.Gelu)
            act.wait_ge(wr_ok, 2)

            def hidden(base, size):
                for e in range(EXPERTS):
                    act.wait_ge(down, base + (e + 1))
                    for h in range(2):
                        E = 2 * base + (2 * e + h + 1)
                        act.wait_ge(upped, E)
                        act.wait_ge(h_lo_ok, E)
                        act.activation(g_sb[:, e % 2, h, 0:size], (psA, psB)[e % 2][:, 512 * h:512 * h + size], ACT.Gelu,
                                       bias=eb1[:, 2 * e + h:2 * e + h + 1]).then_inc(g_ok, 1)
                    for h in range(2):
                        act.wait_ge(g_ok, 2 * base + (2 * e + h + 5))
                        act.copy(h_hi[:, e % 2, h, 0:size], g_sb[:, e % 2, h, 0:size]).then_inc(h_hi_ok, 1)

            with act.Fori(0, 6) as g:
                hidden(EXPERTS * g, 4 * PT)
            hidden(6 * EXPERTS, PT + 1)


_INS = ['x', 'src', 'dst', 'L0_gnn_W1', 'L0_gnn_b1', 'L0_gnn_W2', 'L0_gnn_b2', 'L0_mix_w_qkv', 'L0_mix_mem_kv', 'L0_mix_w_out',
        'L0_mix_b_out', 'L0_mix_g_out', 'L0_mix_g_pre', 'L0_ffn_router_w', 'L0_ffn_w1', 'L0_ffn_b1', 'L0_ffn_w2', 'L0_ffn_b2']
_OUTS = [((NODES, DIM), 'float32')]


def kernel(**inputs):
    import numpy as _np
    import concourse.bacc as _bacc
    from concourse import mybir as _mybir
    from concourse.bass_utils import run_bass_kernel_spmd as _run

    nc = _bacc.Bacc("TRN2", target_bir_lowering=False, num_devices=1)
    arrays, args = {}, []
    for name in _INS:
        a = _np.ascontiguousarray(inputs[name])
        arrays[f"in_{name}_dram"] = a
        args.append(nc.dram_tensor(f"in_{name}_dram", a.shape, _mybir.dt.from_np(a.dtype), kind="ExternalInput").ap())
    for i, (shape, dtype) in enumerate(_OUTS):
        dt = _mybir.dt.from_np(_np.dtype(dtype))
        args.append(nc.dram_tensor(f"out_{i}_dram", shape, dt, kind="ExternalOutput").ap())
    gps_layer(nc, *args)
    r = _run(nc, [arrays], core_ids=[0])
    got = tuple(r.results[0][f"out_{i}_dram"] for i in range(len(_OUTS)))
    return got[0]
```

```python
from contextlib import ExitStack

import concourse.bass as bass
from concourse import mybir

ALU = mybir.AluOpType
ACT = mybir.ActivationFunctionType
AX = mybir.AxisListType
F32 = mybir.dt.float32
BF16 = mybir.dt.bfloat16
F16 = mybir.dt.float16
F32R = mybir.dt.float32r
I32 = mybir.dt.int32

P = 128
NODES, DIM, HID, EDGES = 3125, 256, 128, 50000
HEADS, HEAD_DIM, MEM = 4, 32, 4
EXPERTS = 8
W = 5
PT = 125
C = 5
SLOTS = C * W
WINDOWS = NODES // W
EDGE_TILES = -(-EDGES // P)
TCH = -(-EDGE_TILES // P)
TLAST = EDGE_TILES - (TCH - 1) * P
STEPS = 1024
CH = STEPS // P
KEYS = SLOTS * W
NO_NODE = 4000
NO_KEY = 1000.0
UNIT = 8
GROUP = 4
GROUPS = P // GROUP
QKV = 3 * HID
assert EDGE_TILES + WINDOWS - 1 <= STEPS and SLOTS * PT == NODES


TILE_GROUPS = [(n, min(4, SLOTS - n)) for n in range(0, SLOTS, 4)]


class Steps:

    def __init__(self, eng, sem):
        self.eng, self.sem, self.n, self.base = eng, sem, 0, 0

    def did(self, ins):
        ins.then_inc(self.sem, 1)
        self.n += 1

    def wait(self):
        self.eng.wait_ge(self.sem, self.base + self.n)

    def enter(self, i, per):
        self.start, self.per, self.base = self.n, per, i * per

    def leave(self, count):
        assert self.n - self.start == self.per, (self.n - self.start, self.per)
        self.n, self.base = self.start + count * self.per, 0


def gps_layer(nc, x, src, dst, gnn_w1, gnn_b1, gnn_w2, gnn_b2, w_qkv, mem_kv, w_out, b_out, g_out,
              g_pre, router_w, moe_w1, moe_b1, moe_w2, moe_b2, out):
    ctx = ExitStack()
    with ctx:
        def sb(name, shape, dt, scope=ctx):
            return scope.enter_context(nc.sbuf_tensor(name, shape, dt))

        def sem(name):
            return ctx.enter_context(nc.semaphore(name))

        psA, psB, psC, psD = (ctx.enter_context(nc.psum_tensor(f"ps{n}", [P, 1024], F32)) for n in "ABCD")

        ident = sb("ident", [P, P], F32)
        ident_row = sb("ident_row", [P, P], F32)
        diag = sb("diag", [P, P], F16)
        second_scale = sb("second_scale", [P, SLOTS], F32)
        ident_col = sb("ident_col", [P, 1], F32)
        iota_j = sb("iota_j", [P, P, GROUP], BF16)
        acc = sb("acc", [P, SLOTS, DIM], F32)
        hs = sb("hs", [P, SLOTS, HID], F32)
        dinv = sb("dinv", [P, SLOTS], F32)
        key = sb("key", [P, STEPS + P + 2 * UNIT], BF16)
        brow = sb("brow", [P, STEPS + P + 2 * UNIT], BF16)
        ones_row = sb("ones_row", [1, P], F32)
        hs_max = sb("hs_max", [P, C + 1], F32)
        top_hs = sb("top_hs", [1, 4], F32)
        scale = sb("scale", [P, 2], F32)
        sel = sb("sel", [P, CH, WINDOWS], F16)
        b1_all = sb("b1_all", [P, HID], F32)
        w2g = sb("w2g", [P, DIM], F32)
        stats = sb("stats", [P, SLOTS, 6], F32)
        mv = sb("mv", [P, SLOTS, 2], F32)
        rstd = sb("rstd", [P, SLOTS], F32)
        small = sb("small", [P, 4, SLOTS], F32)
        mnorm = sb("mnorm", [P, SLOTS], F32)
        xnorm = sb("xnorm", [P, SLOTS], F32)
        wr = sb("wr", [P, 2, EXPERTS], F32)
        eb2 = sb("eb2", [3 * 32, DIM], F32R)
        eb1 = sb("eb1", [P, 2 * EXPERTS], F32)
        comb = sb("comb", [P, SLOTS, EXPERTS], F32)

        SUMS_BYTES = (2 * CH * W * HID * 2 + W * HID * 4 + W * P * 4)
        COUNTS_BYTES = KEYS * P * 2
        HOT_BYTES = 2 * UNIT * (P + KEYS) * 2
        HS2_BYTES = SLOTS * 2 * HID * 2
        LOOP_BYTES = SUMS_BYTES + HS2_BYTES + 2 * COUNTS_BYTES + HOT_BYTES
        with ExitStack() as st:
            used = 0

            def early(name, shape, dt):
                nonlocal used
                size = {F32: 4, I32: 4, F16: 2, BF16: 2}[dt]
                for n in shape[1:]:
                    size *= n
                used += size
                return sb(name, shape, dt, st)

            def up_to(offset, name):
                nonlocal used
                assert used <= offset, (name, used, offset)
                if used < offset:
                    sb(f"before_{name}", [P, (offset - used) // 2], F16, st)
                used = offset

            t_of = early("t_of", [P, TCH], F32)
            s_of = early("s_of", [P, CH], F32)
            t_of16 = early("t_of16", [P, TCH], F16)
            ones16 = early("ones16", [P, 2], BF16)
            t_lo = early("t_lo", [P, TCH], F32)
            t_hi = early("t_hi", [P, TCH], F32)
            prev_dst = early("prev_dst", [P, TCH], I32)
            prev_w = early("prev_w", [P, TCH], I32)
            w_of_s = early("w_of_s", [P, CH], F32)
            cnt = early("cnt", [P, CH * W], F16)
            b2_all = early("b2_all", [P, DIM], F32)
            bout_all = early("bout_all", [P, DIM], F32)
            eb2_raw = early("eb2_raw", [3 * 32, DIM], F32)
            rw_nat = early("rw_nat", [EXPERTS, DIM], F32)
            eb1_nat = early("eb1_nat", [2 * EXPERTS, P], F32)
            xnT = early("xnT", [P, 2, 2, PT], F32)
            wcat = early("wcat", [P, 2, HID + QKV], F32)
            gpre = early("gpre", [P, 2], F32)
            mem_v = early("mem_v", [P, MEM], F32)
            mem_k = early("mem_k", [P, MEM], F32)
            memkT = early("memkT", [MEM, P], F32)
            memvT = early("memvT", [MEM, P + 1], F32)
            kmax_of = early("kmax_of", [P, C, HID], F32)
            kmax = early("kmax", [P, HID], F32)
            kmax_col = early("kmax_col", [P, 2], F32)
            kmax_mat = early("kmax_mat", [P, P], F32)
            qred = early("qred", [P, SLOTS * HEADS], F32)
            ctx_sb = early("ctx_sb", [P, P + 1], F32)
            ctx_m = early("ctx_m", [P, P], F32)
            ctxT = early("ctxT", [P, P], F32)
            wmix = early("wmix", [P, DIM], F32)
            zinv = early("zinv", [P, 1], F32)
            wout = early("wout", [P, DIM], F32)
            qT = early("qT", [P, 2, 4 * PT], F32)
            up_to(SUMS_BYTES, "hs2")
            src_slot = early("src_slot", [P, TCH, P], F32)
            q_r = early("q_r", [P, TCH, P], F16)
            q_wt = early("q_wt", [P, TCH, P], F16)
            q_b = early("q_b", [P, TCH, P], F16)
            q_key = early("q_key", [P, TCH, P], F16)
            outside = early("outside", [P, STEPS], BF16)
            r_in = early("r_in", [P, STEPS], BF16)
            iota_s = early("iota_s", [P, STEPS], F16)
            up_to(SUMS_BYTES + HS2_BYTES, "counts")
            e_dst = early("e_dst", [P, TCH, P], I32)
            e_src = early("e_src", [P, TCH, P], I32)
            dst_w = early("dst_w", [P, TCH, P], I32)
            src_w = early("src_w", [P, TCH, P], I32)
            src_c = early("src_c", [P, TCH, P], I32)
            src_d = early("src_d", [P, TCH, P], F32)
            past = early("past", [P, TCH, STEPS], F16)
            r_hot = early("r_hot", [P, W, STEPS], BF16)
            up_to(SUMS_BYTES + HS2_BYTES + COUNTS_BYTES, "second_counts")
            xn = early("xn", [P, SLOTS, DIM], F32)
            tile_at = early("tile_at", [P, TCH, STEPS], F16)
            up_to(LOOP_BYTES, "qkv")
            qkv = early("qkv", [P, SLOTS, QKV + 1], F32)
            gout_all = early("gout_all", [P, DIM], F32)
            mix = qkv[:, :, HID:QKV]

        with ExitStack() as st:
            part2 = sb("part2", [P, 2, CH, W * HID], F16, st)
            post = sb("post", [P, W * HID], F32, st)
            aggT = sb("aggT", [P, W, P], F32, st)
            experts_from = st.pop_all()
            hs2 = sb("hs2", [P, SLOTS, 2, HID], F16, st)
            counts = sb("counts", [P, 2, KEYS, P], F16, st)
            hot_b = sb("hot_b", [P, 2, 2, P, GROUP], BF16, st)
            hot_k = sb("hot_k", [P, 2, 2, KEYS, GROUP], BF16, st)
            counts5 = counts[:, :, :, :].rearrange("p r (a d) s -> p r a d s", d=W)

        with ExitStack() as st:
            w_hi = sb("w_hi", [P, 2, EXPERTS, 2, DIM], F32R, st)
            with ExitStack() as raw:
                w_raw = sb("w_raw", [P, 2, EXPERTS, 2, DIM], F32, raw)
            w_lo = sb("w_lo", [P, 2, EXPERTS, 2, DIM], F32R, st)
            tok = sb("tok", [P, W, DIM], F32, st)
            tokT = sb("tokT", [P, 2, W * PT], F32, st)
            tokT_hi = sb("tokT_hi", [P, 2, SLOTS * PT], F32R, st)
            tokT_lo = sb("tokT_lo", [P, 2, SLOTS * PT], F32R, st)
        experts_from.close()

        with ExitStack() as st:
            g_sb = sb("g_sb", [P, 2, W * PT], F32, st)
            h_hi = sb("h_hi", [P, 2, 2, W * PT], F32R, st)
            h_lo = sb("h_lo", [P, 2, 2, W * PT], F32R, st)
        with ExitStack() as st:
            logit = sb("logit", [P, SLOTS, EXPERTS], F32, st)
            top = sb("top", [P, SLOTS, 8], F32, st)
            topi = sb("topi", [P, SLOTS, 8], mybir.dt.uint32, st)
            pick = sb("pick", [P, 2, SLOTS, EXPERTS], F32, st)
            prob = sb("prob", [P, SLOTS, EXPERTS], F32, st)
            comb_hi = sb("comb_hi", [P, SLOTS, EXPERTS], F32R, st)
            comb3 = sb("comb3", [P, SLOTS, 3 * 32], F32, st)
            combT = sb("combT", [3 * 32, 2, 4 * PT], F32R, st)

        pads = sem("pads")
        consts = sem("consts")
        in_edges = sem("in_edges")
        in_x = sem("in_x")
        in_w = sem("in_w")
        in_w1, in_w2 = sem("in_w1"), sem("in_w2")
        vector_done = sem("vector_done")
        scalar_done = sem("scalar_done")
        ident_ok = sem("ident_ok")
        q_ready = sem("q_ready")
        q_spread = sem("q_spread")
        q_used = sem("q_used")
        window_node_hot_ok = sem("window_node_hot_ok")
        sel_ok = sem("sel_ok")
        step_degree_in = sem("step_degree_in")
        step_degree_ok = sem("step_degree_ok")
        degree_in = sem("degree_in")
        degree_ok = sem("degree_ok")
        degree_root_ok = sem("degree_root_ok")
        dinv_ok = sem("dinv_ok")
        var_ok = sem("var_ok")
        std_ok = sem("std_ok")
        xn_ok = sem("xn_ok")
        xn_square_ok = sem("xn_square_ok")
        xnorm_ok = sem("xnorm_ok")
        wcat_ok = sem("wcat_ok")
        xn_transposed = sem("xn_transposed")
        xn_transposed_ok = sem("xn_transposed_ok")
        projected = sem("projected")
        projected_h_ok = sem("projected_h_ok")
        projected_qkv_ok = sem("projected_qkv_ok")
        attention_pe = sem("attention_pe")
        attention_dve = sem("attention_dve")
        q_sub = sem("q_sub")
        q_exp = sem("q_exp")
        k_sub = sem("k_sub")
        k_exp = sem("k_exp")
        q_done = sem("q_done")
        xn_free = sem("xn_free")
        norm_ok = sem("norm_ok")
        mix_scaled = sem("mix_scaled")
        q_transposed = sem("q_transposed")
        q_transposed_ok = sem("q_transposed_ok")
        attended = sem("attended")
        attended_ok = sem("attended_ok")
        attended_norm_ok = sem("attended_norm_ok")
        acc_mixed = sem("acc_mixed")
        acc_xn_ok = sem("acc_xn_ok")
        hot_ready = sem("hot_ready")
        built = sem("built")
        counts_ok = sem("counts_ok")
        summed = sem("summed")
        sums_high_ok = sem("sums_high_ok")
        sums_low_ok = sem("sums_low_ok")
        tok_ok = sem("tok_ok")
        tok_added = sem("tok_added")
        token_high_ok = sem("token_high_ok")
        token_full_ok = sem("token_full_ok")
        token_low_ok = sem("token_low_ok")
        w_hi_ok = sem("w_hi_ok")
        w_lo_ok = sem("w_lo_ok")
        hidden_ok = sem("hidden_ok")
        hidden_high_ok = sem("hidden_high_ok")
        hidden_low_ok = sem("hidden_low_ok")
        router_in = sem("router_in")
        router_ok = sem("router_ok")
        logit_in = sem("logit_in")
        logit_ok = sem("logit_ok")
        prob_exp = sem("prob_exp")
        comb3_ok = sem("comb3_ok")
        comb_ok = sem("comb_ok")
        comb3_clear = sem("comb3_clear")
        bias2_in = sem("bias2_in")
        bias2_ok = sem("bias2_ok")
        tok_transposed = sem("tok_transposed")
        comb_transposed = sem("comb_transposed")
        comb_transposed_ok = sem("comb_transposed_ok")
        upped = sem("upped")
        down = sem("down")
        weighted = sem("weighted")
        merged = sem("merged")
        merge_used = sem("merge_used")
        hs_ok = sem("hs_ok")
        hs_high_ok = sem("hs_high_ok")
        hs_low_ok = sem("hs_low_ok")
        max_ok = sem("max_ok")
        max_in = sem("max_in")
        pow_ok = sem("pow_ok")
        pow_in = sem("pow_in")
        scale_ok = sem("scale_ok")
        second_sums_ok = sem("second_sums_ok")
        second_in = sem("second_in")
        second_ok = sem("second_ok")
        stored = sem("stored")

        block = ctx.enter_context(nc.Block())

        HALVES = ((0, 312, 0), (311, 314, 1))
        assert HALVES[1][0] + HALVES[1][1] == W * PT

        def out_place(f, d):
            bank = (3 * f + d // 2) % 4
            at = 512 * (bank % 2) + DIM * (d % 2)
            return (psC, psD)[bank // 2][0:PT, at:at + DIM]

        TOKEN_PARTS = ((0, 0, W, psA[:, 0:W * P]), (1, 0, 3, psA[:, W * P:8 * P]), (1, 3, W, psC[:, 512:512 + 2 * P]))

        x_v = x.rearrange("(c p m) f -> p c (m f)", p=PT, m=W)
        acc_v = acc[:, :, :].rearrange("p (c m) f -> p c (m f)", m=W)

        @block.sync
        def _(sp):
            full = (TCH - 1) * P
            n_last = EDGES // P - full
            tail = EDGES - (EDGES // P) * P
            sp.wait_ge(pads, 4)
            for e_sb, e in ((e_dst, dst), (e_src, src)):
                sp.dma_start(e_sb[:, 0:TCH - 1, :], e[0:full * P].rearrange("(c p e) -> p c e", p=P, e=P)).then_inc(in_edges, 16)
                sp.dma_start(e_sb[0:n_last, TCH - 1, :], e[full * P:(full + n_last) * P].rearrange("(p e) -> p e", e=P)).then_inc(in_edges, 16)
                sp.dma_start(e_sb[n_last:n_last + 1, TCH - 1, 0:tail], e[(full + n_last) * P:EDGES].rearrange("(p e) -> p e", p=1)).then_inc(in_edges, 16)
            ends = dst[0:(EDGES // P) * P].rearrange("(t e) -> t e", e=P)[:, P - 1:P]
            sp.dma_start(prev_dst[1:P, 0:1], ends[0:P - 1, :], allow_slow_non_contiguous=True).then_inc(in_edges, 16)
            for c in range(1, TCH):
                k = P if c < TCH - 1 else TLAST
                sp.dma_start(prev_dst[0:k, c:c + 1], ends[c * P - 1:c * P - 1 + k, :],
                             allow_slow_non_contiguous=True).then_inc(in_edges, 16)
            for lo, hi in ((0, 112), (112, PT)):
                sp.dma_start(acc_v[lo:hi], x_v[lo:hi]).then_inc(in_x, 16)
            loads = [
                (wcat[:, :, 0:HID], gnn_w1.rearrange("(k p) f -> p k f", p=P)),
                (wcat[:, :, HID:HID + QKV], w_qkv.rearrange("(k p) f -> p k f", p=P)),
                (mem_k[:, :], mem_kv[0].rearrange("h d m -> (h d) m")),
                (mem_v[:, :], mem_kv[1].rearrange("h d m -> (h d) m")),
                (wout[:, :], w_out),
                (w2g[:, :], gnn_w2),
                (b1_all[:, :], gnn_b1.rearrange("(a f) -> a f", a=1).to_broadcast([P, HID])),
                (b2_all[:, :], gnn_b2.rearrange("(a f) -> a f", a=1).to_broadcast([P, DIM])),
                (bout_all[:, :], b_out.rearrange("(a f) -> a f", a=1).to_broadcast([P, DIM])),
                (gout_all[:, :], g_out.rearrange("(a f) -> a f", a=1).to_broadcast([P, DIM])),
                (gpre[:, 0:1], g_pre[0:P].rearrange("(p a) -> p a", a=1)),
                (gpre[:, 1:2], g_pre[P:DIM].rearrange("(p a) -> p a", a=1)),
                (rw_nat[:, :], router_w),
                (eb2_raw[0:EXPERTS, :], moe_b2),
                (eb2_raw[32:32 + EXPERTS, :], moe_b2),
                (eb2_raw[64:64 + EXPERTS, :], moe_b2),
                (eb1_nat[:, :], moe_b1.rearrange("e (h p) -> (e h) p", p=P)),
            ]
            for to, frm in loads:
                sp.dma_start(to, frm).then_inc(in_w, 16)
            assert len(loads) == 17
            sp.wait_ge(summed, 2 * CH + 1)
            for i, w, loaded in ((0, moe_w1, in_w1), (1, moe_w2, in_w2)):
                sp.dma_start(w_raw[:, i, :, :, :].rearrange("p e k f -> p (e k) f"), w.rearrange("e (k p) f -> p (e k) f", p=P)).then_inc(loaded, 16)
            out_v = out.rearrange("(c p m) f -> p c (m f)", p=PT, m=W)
            for c in range(C):
                sp.wait_ge(weighted, 4 + 3 * EXPERTS * (c + 1))
                for lo, hi in ((0, 112), (112, PT)):
                    sp.dma_start(out_v[lo:hi, c], acc_v[lo:hi, c]).then_inc(stored, 16)
            sp.wait_ge(stored, 32 * C)
        IN_W = 16 * 17
        IN_EDGES = 16 * 10

        @block.gpsimd
        def _(pool):
            pool.memset(e_dst[:, TCH - 1, :], NO_NODE).then_inc(pads, 1)
            pool.memset(e_src[:, TCH - 1, :], 0).then_inc(pads, 1)
            pool.memset(prev_dst[:, :], 0).then_inc(pads, 1)
            pool.memset(eb2_raw[:, :], 0).then_inc(pads, 1)
            kw = dict(allow_small_or_imprecise_dtypes=True)
            pool.iota(t_of[:, :], [[P, TCH]], base=0, channel_multiplier=1, **kw).then_inc(consts, 1)
            pool.iota(iota_s[:, :], [[1, STEPS]], base=0, channel_multiplier=0, **kw).then_inc(consts, 1)
            pool.iota(t_of16[:, :], [[P, TCH]], base=0, channel_multiplier=1, **kw).then_inc(consts, 1)
            pool.iota(s_of[:, :], [[P, CH]], base=0, channel_multiplier=1, **kw).then_inc(consts, 1)
            pool.iota(ident_row[:, :], [[1, P]], base=0, channel_multiplier=0, **kw).then_inc(consts, 1)
            pool.iota(ident_col[:, :], [[0, 1]], base=0, channel_multiplier=1, **kw).then_inc(consts, 1)
            pool.iota(iota_j[:, :, :], [[1, P], [0, GROUP]], base=0, channel_multiplier=0, **kw).then_inc(consts, 1)
            pool.memset(ones16[:, :], 1.0).then_inc(consts, 1)
            pool.memset(ones_row[:, :], 1.0).then_inc(consts, 1)

            pool.wait_ge(xn_ok, SLOTS)
            pool.wait_ge(in_w, IN_W)
            pool.tensor_tensor(acc[0:PT], acc[0:PT], xn[0:PT], ALU.add).then_inc(xn_free, 1)
            pool.wait_ge(xn_free, 1)
            pool.tensor_tensor(acc[0:PT], acc[0:PT], b2_all[0:PT, :].unsqueeze(1).to_broadcast([PT, SLOTS, DIM]), ALU.add).then_inc(acc_xn_ok, 1)
            pool.wait_ge(norm_ok, 1)
            pool.wait_ge(acc_xn_ok, 1)
            m = mix[0:PT]
            pool.tensor_tensor(m, m, mnorm[0:PT, :].unsqueeze(2).to_broadcast([PT, SLOTS, DIM]), ALU.mult).then_inc(mix_scaled, 1)
            pool.wait_ge(mix_scaled, 1)
            pool.tensor_tensor(m, m, gout_all[0:PT, :].unsqueeze(1).to_broadcast([PT, SLOTS, DIM]), ALU.mult).then_inc(mix_scaled, 1)
            pool.wait_ge(mix_scaled, 2)
            pool.tensor_tensor(acc[0:PT], acc[0:PT], m, ALU.add).then_inc(acc_mixed, 1)

            for n, i in enumerate((1, 0)):
                if n:
                    pool.wait_ge(merged, 2 * C)
                    pool.memset(comb3[:], 0.0).then_inc(comb3_clear, 1)
                pool.wait_ge(w_hi_ok, n + 1)
                pool.tensor_tensor(w_lo[:, i], w_raw[:, i], w_hi[:, i].bitcast(F32), ALU.subtract).then_inc(w_lo_ok, 1)

        CONSTS = 9

        FIRST = 9
        assert FIRST + P // UNIT == SLOTS

        @block.vector
        def _(v):
            st = Steps(v, vector_done)

            v.wait_ge(in_edges, IN_EDGES)
            v.wait_ge(consts, CONSTS)
            st.did(v.tensor_scalar(dst_w[:], e_dst[:], 1.0 / W, -0.4, ALU.mult, ALU.add))
            st.did(v.tensor_scalar(src_w[:], e_src[:], 1.0 / W, -0.4, ALU.mult, ALU.add))
            st.did(v.tensor_scalar(prev_w[:], prev_dst[:], 1.0 / W, -0.4, ALU.mult, ALU.add))
            v.tensor_scalar(ident[:], ident_row[:], ident_col[:], None, ALU.is_equal).then_inc(ident_ok, 1)
            st.did(v.tensor_scalar(diag[:], ident_row[:], ident_col[:], 1.0 / P, ALU.is_equal, ALU.mult))
            st.wait()
            st.did(v.scalar_tensor_tensor(q_r[:], dst_w[:], -float(W), e_dst[:], ALU.mult, ALU.add))
            st.did(v.tensor_tensor(q_wt[:], dst_w[:], t_of[:, :].unsqueeze(2).to_broadcast([P, TCH, P]), ALU.add))
            st.did(v.scalar_tensor_tensor(src_d[:], src_w[:], -float(W), e_src[:], ALU.mult, ALU.add))
            st.did(v.tensor_scalar(src_c[:], src_w[:], 1.0 / PT, 0.5 / PT - 0.5, ALU.mult, ALU.add))
            st.did(v.tensor_tensor(t_lo[:], prev_w[:], t_of[:], ALU.add))
            st.did(v.scalar_tensor_tensor(t_hi[:], dst_w[:, :, P - 1], 1.0, t_of[:], ALU.add, ALU.add))
            st.wait()
            st.did(v.scalar_tensor_tensor(q_b[:], src_c[:], -float(PT), src_w[:], ALU.mult, ALU.add))
            st.did(v.scalar_tensor_tensor(src_slot[:], src_c[:], float(W), src_d[:], ALU.mult, ALU.add))
            for c in range(TCH):
                st.did(v.tensor_scalar(past[:, c, :], iota_s[:], t_lo[:, c:c + 1], None, ALU.is_ge))
            st.wait()
            st.did(v.scalar_tensor_tensor(q_key[:], src_slot[:], float(W), q_r[:], ALU.mult, ALU.add))
            for c in range(TCH):
                st.did(v.scalar_tensor_tensor(tile_at[:, c, :], iota_s[:], t_hi[:, c:c + 1], past[:, c, :], ALU.is_lt, ALU.mult))
            st.wait()
            v.nop().then_inc(q_ready, 1)

            v.wait_ge(in_x, 32)
            for n in range(SLOTS):
                st.did(v.bn_stats(stats[0:PT, n, :], acc[0:PT, n, :]))

            v.wait_ge(q_spread, 1)
            v.tensor_tensor(outside[:], psA[:], iota_s[:], ALU.not_equal).then_inc(q_used, 1)
            v.wait_ge(q_used, 1)
            v.wait_ge(q_spread, 2)
            v.scalar_tensor_tensor(r_in[:], outside[:], NO_KEY, psB[:], ALU.mult, ALU.add).then_inc(q_used, 1)
            v.wait_ge(q_spread, 3)
            v.scalar_tensor_tensor(key[:, 0:STEPS], outside[:], NO_KEY, psC[:], ALU.mult, ALU.add).then_inc(q_used, 1)
            v.wait_ge(q_spread, 4)
            v.tensor_copy(brow[:, 0:STEPS], psD[:]).then_inc(q_used, 1)
            st.wait()
            for n in range(SLOTS):
                st.did(v.bn_aggr(mv[0:PT, n, :], stats[0:PT, n, :]))
            st.wait()
            v.tensor_scalar(small[0:PT, 2, :], mv[0:PT, :, 1], 1e-5, None, ALU.add).then_inc(var_ok, 1)
            v.wait_ge(std_ok, 1)
            st.did(v.reciprocal(rstd[0:PT, :], small[0:PT, 3, :]))
            st.wait()
            st.did(v.tensor_tensor(xnorm[0:PT, :], mv[0:PT, :, 1], rstd[0:PT, :], ALU.mult))
            st.wait()
            v.tensor_tensor(xnorm[0:PT, :], xnorm[0:PT, :], rstd[0:PT, :], ALU.mult).then_inc(xn_square_ok, 1)
            for n in range(SLOTS):
                v.tensor_scalar(xn[0:PT, n, :], acc[0:PT, n, :], mv[0:PT, n, 0:1], rstd[0:PT, n:n + 1],
                                ALU.subtract, ALU.mult).then_inc(xn_ok, 1)
                if n == 1:
                    v.wait_ge(in_w, IN_W)
                    for k in range(2):
                        v.tensor_scalar(wcat[:, k, HID:HID + QKV], wcat[:, k, HID:HID + QKV], gpre[:, k:k + 1], None,
                                        ALU.mult).then_inc(wcat_ok, 1)
                    v.wait_ge(std_ok, 2)
                    st.did(v.tensor_scalar(xnorm[0:PT, :], xnorm[0:PT, :], 1e-12 / DIM ** 0.5, None, ALU.max))
                    st.wait()
                    v.reciprocal(xnorm[0:PT, :], xnorm[0:PT, :]).then_inc(xnorm_ok, 1)

            v.wait_ge(q_used, 4)
            again = P + 2 * UNIT
            st.did(v.tensor_copy(key[:, STEPS:STEPS + again], key[:, 0:again]))
            st.did(v.tensor_copy(brow[:, STEPS:STEPS + again], brow[:, 0:again]))
            for d in range(W):
                v.tensor_scalar(r_hot[:, d, :], r_in[:], float(d), None, ALU.is_equal).then_inc(window_node_hot_ok, 1)
            v.wait_ge(q_spread, 5)
            st.did(v.tensor_tensor(w_of_s[:], s_of[:], psA[:, 0:CH], ALU.subtract))
            st.wait()
            for k in range(CH):
                v.tensor_scalar(sel[:, k, :], iota_s[:, 0:WINDOWS], w_of_s[:, k:k + 1], None, ALU.is_equal).then_inc(sel_ok, 1)
            v.wait_ge(step_degree_in, 1)
            v.tensor_copy(cnt[:], psA[:, 64:64 + CH * W]).then_inc(step_degree_ok, 1)
            v.wait_ge(degree_in, 1)
            v.tensor_scalar(small[0:PT, 0, :], psA[0:PT, 128:128 + SLOTS], 1.0, None, ALU.add).then_inc(degree_ok, 1)
            v.wait_ge(degree_root_ok, 1)
            v.reciprocal(dinv[0:PT, :], small[0:PT, 1, :]).then_inc(dinv_ok, 1)

            def hot_unit(slot, column):
                cols = bass.ds(column, UNIT)
                for hot, n, val in ((hot_b, P, brow), (hot_k, KEYS, key)):
                    v.tensor_tensor(hot[:, slot], iota_j[:, 0:n, :].unsqueeze(1).to_broadcast([P, 2, n, GROUP]),
                                    val[:, cols].rearrange("p (g s) -> p g s", g=2).unsqueeze(2).to_broadcast([P, 2, n, GROUP]),
                                    ALU.is_equal).then_inc(hot_ready, 1)

            qv = qkv[0:PT, :, 0:HID].rearrange("p n (h d) -> p n h d", h=HEADS)
            qr = qred[0:PT, :].rearrange("p (n h) -> p n h", h=HEADS)

            def q_block(c):
                sl = slice(W * c, W * c + W)
                return qv[:, sl], qr[:, sl], qr[:, sl].unsqueeze(3).to_broadcast([PT, W, HEADS, HEAD_DIM])

            def q_softmax_end(c):
                q, r, rb = q_block(c)
                v.wait_ge(q_exp, c + 1)
                st.did(v.tensor_reduce(r, q, AX.X, ALU.add))
                st.wait()
                st.did(v.reciprocal(r, r))
                st.wait()
                v.tensor_tensor(q, q, rb, ALU.mult).then_inc(q_done, 1)

            def block_done(c):
                q, r, rb = q_block(c)
                v.wait_ge(projected_qkv_ok, W * c + W)
                h = hs[0:PT, W * c:W * c + W, :]
                v.tensor_tensor(h, h, dinv[0:PT, W * c:W * c + W].unsqueeze(2).to_broadcast([PT, W, HID]), ALU.mult).then_inc(hs_ok, 1)
                st.did(v.tensor_reduce(r, q, AX.X, ALU.max))
                st.wait()
                v.tensor_tensor(q, q, rb, ALU.subtract).then_inc(q_sub, 1)
                st.did(v.tensor_reduce(kmax_of[0:PT, c, :], qkv[0:PT, W * c:W * c + W, HID:2 * HID].rearrange("p n f -> p f n"), AX.X, ALU.max))
                v.wait_ge(hs_ok, c + 1)
                st.did(v.tensor_reduce(hs_max[0:PT, c + 1:c + 2], h.rearrange("p d f -> p (d f)"), AX.X, ALU.max, apply_absolute_value=True))

            v.wait_ge(dinv_ok, 1)
            for unit in range(P // UNIT + 2):
                n = FIRST + unit - 2
                v.wait_ge(built, 2 * unit + 2)
                hot_unit(unit % 2, UNIT * unit)
                if n == FIRST + 1:
                    block_done(0)
                if n > FIRST + 1 and n % W == W - 1 and n < SLOTS - 1:
                    block_done(n // W)
                if n == FIRST + 3:
                    block_done(1)
                if n > FIRST + 3 and n % W == 3:
                    q_softmax_end(n // W - 2)
            q_softmax_end(C - 2)
            block_done(C - 1)

            st.wait()
            v.tensor_reduce(kmax[0:PT, :], kmax_of[0:PT, :, :].rearrange("p c f -> p f c"), AX.X, ALU.max).then_inc(attention_dve, 1)
            v.tensor_reduce(kmax_col[:, 1:2], mem_k[:], AX.X, ALU.max).then_inc(attention_dve, 1)
            v.wait_ge(attention_pe, 1)
            st.did(v.tensor_reduce(kmax_col[:, 0:1], psA[:, 0:PT], AX.X, ALU.max))
            v.wait_ge(attention_dve, 2)
            st.wait()
            st.did(v.tensor_tensor(kmax_col[:, 0:1], kmax_col[:, 0:1], kmax_col[:, 1:2], ALU.max))
            st.wait()
            v.tensor_scalar(kmax_mat[:], ident[:], 0.0, kmax_col[:, 0:1], ALU.mult, ALU.add).then_inc(attention_dve, 1)
            def make_scale(layer):
                st.did(v.tensor_reduce(hs_max[0:PT, 0:1], hs_max[0:PT, 1:C + 1], AX.X, ALU.max))
                st.wait()
                v.nop().then_inc(max_ok, 1)
                v.wait_ge(max_in, layer + 1)
                st.did(v.tensor_reduce(top_hs[:, 0:1], psD[0:1, 768:768 + PT], AX.X, ALU.max))
                st.wait()
                st.did(v.tensor_scalar(top_hs[:, 0:1], top_hs[:, 0:1], 2.0 ** -90, None, ALU.max))
                st.wait()
                bits = top_hs[:, :].bitcast(I32)
                st.did(v.tensor_scalar(bits[:, 1:2], bits[:, 0:1], 0xFF << 23, None, ALU.bitwise_and))
                st.wait()
                st.did(v.tensor_scalar(bits[:, 2:3], bits[:, 1:2], -1.0, float((2 * 127 + 14) << 23), ALU.mult, ALU.add))
                st.did(v.tensor_scalar(bits[:, 3:4], bits[:, 1:2], float((14 - 7) << 23), None, ALU.subtract))
                st.wait()
                v.nop().then_inc(pow_ok, 1)
                v.wait_ge(pow_in, layer + 1)
                st.did(v.tensor_copy(scale[:, :], psD[:, 896:898]))
                st.wait()
                v.nop().then_inc(scale_ok, 1)

            def hs_low(c, n):
                v.wait_ge(hs_high_ok, n + 1)
                v.scalar_tensor_tensor(hs2[0:PT, bass.ds(W * c, W), 1, :], hs[0:PT, bass.ds(W * c, W), :], scale[0:PT, 0:1],
                                       hs2[0:PT, bass.ds(W * c, W), 0, :], ALU.mult, ALU.subtract).then_inc(hs_low_ok, 1)

            v.wait_ge(attention_pe, 2)
            kv_ = qkv[0:PT, :, HID:2 * HID]
            for c in range(C):
                kc = kv_[:, W * c:W * c + W, :]
                v.tensor_tensor(kc, kc, psA[0:PT, 256:256 + HID].unsqueeze(1).to_broadcast([PT, W, HID]), ALU.subtract).then_inc(k_sub, 1)
            v.nop().then_inc(attention_dve, 1)
            v.tensor_copy(memvT[:, 0:P], psB[0:MEM, 256:256 + P]).then_inc(attention_dve, 1)
            st.did(v.tensor_copy(memkT[:], psB[0:MEM, 0:P]))
            st.wait()
            v.tensor_tensor(memkT[:], memkT[:], psA[0:MEM, 256:256 + HID], ALU.subtract).then_inc(attention_dve, 1)
            v.memset(memvT[:, P:P + 1], 1.0).then_inc(attention_dve, 1)
            v.memset(ctx_m[:], 0.0).then_inc(attention_dve, 1)
            v.memset(qkv[0:PT, :, QKV:QKV + 1], 1.0).then_inc(attention_dve, 1)
            make_scale(0)
            q_softmax_end(C - 1)
            with v.Fori(0, C) as c:
                hs_low(c, c)
            v.wait_ge(attention_pe, 3)
            st.did(v.tensor_copy(ctx_sb[:], psB[:, 512:512 + P + 1]))
            st.wait()
            st.did(v.reciprocal(zinv[:], ctx_sb[:, P:P + 1]))
            st.wait()
            v.wait_ge(attention_dve, 9)
            for h in range(HEADS):
                s = slice(h * HEAD_DIM, (h + 1) * HEAD_DIM)
                v.tensor_scalar(ctx_m[s, s], ctx_sb[s, s], zinv[s, :], HEAD_DIM ** -0.5, ALU.mult, ALU.mult).then_inc(attention_dve, 1)
            v.wait_ge(attention_pe, 4)
            v.tensor_copy(ctxT[:], psB[:, 0:P]).then_inc(attention_dve, 1)
            v.wait_ge(router_in, 1)
            v.tensor_copy(wr[:], psD[:, 0:2 * EXPERTS].rearrange("p (k e) -> p k e", k=2)).then_inc(router_ok, 1)
            v.tensor_copy(eb1[:], psD[:, 128:128 + 2 * EXPERTS]).then_inc(router_ok, 1)
            st.did(v.tensor_copy(eb2[:], eb2_raw[:]))
            st.wait()
            st.did(v.tensor_tensor(eb2[32:64, :], eb2_raw[32:64, :], eb2[32:64, :].bitcast(F32), ALU.subtract))
            v.wait_ge(attention_pe, 5)
            v.tensor_copy(wmix[:], psB[:, 256:256 + DIM]).then_inc(attention_dve, 1)
            for g, (n0, tiles) in enumerate(TILE_GROUPS):
                v.wait_ge(attended, g + 1)
                v.tensor_tensor(mix[0:PT, n0:n0 + tiles, :], (psC, psB)[g % 2][0:PT, 0:DIM * tiles].rearrange("p (t f) -> p t f", f=DIM),
                                bout_all[0:PT, :].unsqueeze(1).to_broadcast([PT, tiles, DIM]), ALU.add).then_inc(attended_ok, 1)
            v.wait_ge(attended_norm_ok, 1)
            st.did(v.tensor_scalar(small[0:PT, 3, :], small[0:PT, 3, :], 1e-12, 1.0 / DIM ** 0.5, ALU.max, ALU.mult))
            st.wait()
            v.reciprocal(mnorm[0:PT, :], small[0:PT, 3, :]).then_inc(norm_ok, 1)

            v.nop().then_inc(sums_low_ok, 2)
            v.nop().then_inc(merge_used, 1)
            v.nop().then_inc(hs_ok, 1)
            v.nop().then_inc(second_ok, 2)
            v.wait_ge(norm_ok, 1)
            v.wait_ge(projected_h_ok, SLOTS)
            st.wait()
            def hot_units(count, chunk, first, g):
                with v.Fori(0, count) as i:
                    for u in range(2):
                        v.wait_ge(built, 4 * i + 2 * (first + u + 1) + g)
                        hot_unit(u, 2 * UNIT * i + P * chunk + UNIT * (first + u))

            for layer in range(2):
                k0, g0 = CH * layer, GROUPS * (1 + CH * layer)
                def two_chunks(kp, last):
                    for par in range(2):
                        if not (last and par):
                            hot_units(7 if last else 8, 2 * kp + par + 1, 2, 2 * GROUPS * kp + (g0 + GROUPS * par))
                        v.wait_ge(sums_high_ok, 2 * kp + (k0 + par + 1))
                        hi_p, lo_p = (part2[:, part, bass.ds(2 * kp + par, 1), :].rearrange("p a f -> p (a f)") for part in range(2))
                        v.scalar_tensor_tensor(lo_p, (psB, psC)[par][:, 0:W * HID], 1.0 / P, hi_p, ALU.mult, ALU.subtract).then_inc(sums_low_ok, 1)

                with v.Fori(0, CH // 2 - layer) as kp:
                    two_chunks(kp, False)
                if layer:
                    two_chunks(CH // 2 - 1, True)
                post_v = post[0:PT, :].rearrange("p (d f) -> p d f", d=W)
                if layer == 0:
                    for c in range(C):
                        v.wait_ge(hs_ok, c + (C + 1))
                        dv = dinv[0:PT, W * c:W * c + W].unsqueeze(2).to_broadcast([PT, W, HID])
                        v.wait_ge(merged, c + 1)
                        v.scalar_tensor_tensor(post_v, (psD, psA)[c % 2][0:PT, 0:W * HID].rearrange("p (d f) -> p d f", d=W), scale[0:PT, 1:2],
                                               hs[0:PT, W * c:W * c + W, :], ALU.mult, ALU.add).then_inc(merge_used, 1)
                        v.wait_ge(merge_used, c + 2)
                        st.did(v.tensor_tensor(post_v, post_v, dv, ALU.mult))
                        st.wait()
                        st.did(v.tensor_tensor(post_v, post_v, b1_all[0:PT, :].unsqueeze(1).to_broadcast([PT, W, HID]), ALU.add))
                        st.wait()
                        v.scalar_tensor_tensor(hs[0:PT, bass.ds(W * c, W), :], post_v, 0.0, dv, ALU.max, ALU.mult).then_inc(hs_ok, 1)
                        v.wait_ge(hs_ok, c + (C + 2))
                        st.did(v.tensor_reduce(hs_max[0:PT, bass.ds(c + 1, 1)], hs[0:PT, bass.ds(W * c, W), :].rearrange("p d f -> p (d f)"),
                                               AX.X, ALU.max))
                    st.wait()
                    make_scale(1)
                    st.did(v.tensor_scalar(second_scale[0:PT, :], dinv[0:PT, :], scale[0:PT, 1:2], None, ALU.mult))
                    with v.Fori(0, C) as c:
                        hs_low(c, c + C)

            def token_low(c):
                v.wait_ge(token_high_ok, c + 1)
                cols = slice(W * PT * c, W * PT * (c + 1))
                v.tensor_tensor(tokT_lo[:, :, cols], tokT[:], tokT_hi[:, :, cols].bitcast(F32), ALU.subtract).then_inc(token_low_ok, 1)

            st.wait()
            for c in range(C):
                a = acc[0:PT, W * c:W * c + W, :]
                if c == 0:
                    v.wait_ge(acc_mixed, 1)
                v.wait_ge(second_in, c + 2)
                for d in range(W):
                    ins = v.scalar_tensor_tensor(a[:, d, :], psB[0:PT, DIM * d:DIM * d + DIM] if d < 4 else psC[0:PT, 0:DIM],
                                                 second_scale[0:PT, W * c + d:W * c + d + 1], a[:, d, :], ALU.mult, ALU.add)
                    if d >= 3:
                        ins.then_inc(second_ok, 1)
                v.wait_ge(second_ok, 2 * c + 4)
                for d in range(W):
                    st.did(v.bn_stats(stats[0:PT, d, :], a[:, d, :]))
                st.wait()
                for d in range(W):
                    st.did(v.bn_aggr(mv[0:PT, d, :], stats[0:PT, d, :]))
                st.wait()
                v.tensor_scalar(small[0:PT, 2, 0:W], mv[0:PT, 0:W, 1], 1e-5, None, ALU.add).then_inc(var_ok, 1)
                if c:
                    v.wait_ge(tok_ok, c)
                    b = acc[0:PT, W * (c - 1):W * c, :]
                    v.tensor_tensor(b, b, tok[0:PT], ALU.add).then_inc(tok_added, 1)
                v.wait_ge(std_ok, c + 3)
                st.did(v.reciprocal(rstd[0:PT, 0:W], small[0:PT, 3, 0:W]))
                st.wait()
                if c:
                    v.wait_ge(tok_added, c)
                    v.wait_ge(tok_transposed, c)
                for d in range(W):
                    ins = v.tensor_scalar(tok[0:PT, d, :], a[:, d, :], mv[0:PT, d, 0:1], rstd[0:PT, d:d + 1], ALU.subtract, ALU.mult)
                    if d < W - 1:
                        st.did(ins)
                ins.then_inc(tok_ok, 1)
                if c:
                    token_low(c - 1)
            v.wait_ge(tok_ok, C)
            st.did(v.tensor_tensor(acc[0:PT, W * (C - 1):SLOTS, :], acc[0:PT, W * (C - 1):SLOTS, :], tok[0:PT], ALU.add))
            token_low(C - 1)

            v.wait_ge(logit_in, C)
            st.did(v.tensor_copy(logit[0:PT], psC[0:PT, 768:768 + SLOTS * EXPERTS].rearrange("p (n e) -> p n e", e=EXPERTS)))
            st.wait()
            for n in range(SLOTS):
                st.did(v.max(top[0:PT, n, :], logit[0:PT, n, :]))
            st.wait()
            for n in range(SLOTS):
                st.did(v.max_index(topi[0:PT, n, :], top[0:PT, n, :], logit[0:PT, n, :]))
            v.tensor_tensor(prob[0:PT], logit[0:PT], top[0:PT, :, 0:1].to_broadcast([PT, SLOTS, EXPERTS]), ALU.subtract).then_inc(logit_ok, 1)
            st.wait()
            for j in range(2):
                st.did(v.tensor_tensor(pick[0:PT, j], ident_row[0:PT, 0:EXPERTS].unsqueeze(1).to_broadcast([PT, SLOTS, EXPERTS]),
                                       topi[0:PT, :, j:j + 1].to_broadcast([PT, SLOTS, EXPERTS]), ALU.is_equal))
            st.wait()
            st.did(v.tensor_tensor(pick[0:PT, 0], pick[0:PT, 0], pick[0:PT, 1], ALU.add))
            v.wait_ge(prob_exp, 1)
            st.did(v.tensor_reduce(small[0:PT, 0, :], prob[0:PT], AX.X, ALU.add))
            st.wait()
            st.did(v.reciprocal(small[0:PT, 1, :], small[0:PT, 0, :]))
            st.wait()
            st.did(v.tensor_tensor(prob[0:PT], prob[0:PT], small[0:PT, 1, :].unsqueeze(2).to_broadcast([PT, SLOTS, EXPERTS]), ALU.mult))
            st.wait()
            st.did(v.tensor_tensor(prob[0:PT], prob[0:PT], pick[0:PT, 0], ALU.mult))
            st.wait()
            st.did(v.tensor_reduce(small[0:PT, 0, :], prob[0:PT], AX.X, ALU.add))
            st.wait()
            st.did(v.tensor_scalar(small[0:PT, 0, :], small[0:PT, 0, :], 1e-12, None, ALU.max))
            st.wait()
            st.did(v.reciprocal(small[0:PT, 1, :], small[0:PT, 0, :]))
            st.wait()
            v.tensor_tensor(comb[0:PT], prob[0:PT], small[0:PT, 1, :].unsqueeze(2).to_broadcast([PT, SLOTS, EXPERTS]), ALU.mult).then_inc(comb_ok, 1)
            v.wait_ge(comb_ok, 1)
            st.did(v.tensor_copy(comb_hi[0:PT], comb[0:PT]))
            v.wait_ge(comb3_clear, 1)
            st.wait()
            st.did(v.tensor_copy(comb3[0:PT, :, 0:EXPERTS], comb_hi[0:PT].bitcast(F32)))
            st.did(v.tensor_copy(comb3[0:PT, :, 32:32 + EXPERTS], comb_hi[0:PT].bitcast(F32)))
            st.did(v.tensor_tensor(comb3[0:PT, :, 64:64 + EXPERTS], comb[0:PT], comb_hi[0:PT].bitcast(F32), ALU.subtract))
            st.wait()
            v.nop().then_inc(comb3_ok, 1)
            def add_bias2(g, n0, tiles):
                v.wait_ge(bias2_in, g + 1)
                a = acc[0:PT, bass.ds(n0, tiles), :]
                v.tensor_tensor(a, a, (psC, psD)[g % 2][0:PT, 0:DIM * tiles].rearrange("p (t f) -> p t f", f=DIM), ALU.add).then_inc(bias2_ok, 1)

            st.wait()
            for g in range(7):
                add_bias2(g, 4 * g, 4 if g < 6 else 1)
            v.wait_ge(bias2_ok, 7)

            def take(base, c, f):
                v.wait_ge(down, base + (f + 3))
                v.wait_ge(weighted, 3 * base + (3 * f + 4))
                for d in range(W):
                    a = acc[0:PT, bass.ds(W * c + d, 1), :].rearrange("p a f -> p (a f)")
                    cw = comb[0:PT, bass.ds(W * c + d, 1), f:f + 1].rearrange("p a e -> p (a e)")
                    y = v.scalar_tensor_tensor(a, out_place(f, d), cw, a, ALU.mult, ALU.add)
                    if d % 2 or d == W - 1:
                        y.then_inc(weighted, 1)

            v.nop().then_inc(weighted, 4)
            v.nop().then_inc(hidden_low_ok, 4)
            with v.Fori(0, C) as c:
                base = EXPERTS * c
                for e in range(EXPERTS + 1):
                    if e < EXPERTS:
                        v.wait_ge(down, base + (e + 1))
                        for h in range(2):
                            v.wait_ge(hidden_high_ok, 2 * base + (2 * e + h + 1))
                            v.tensor_tensor(h_lo[:, e % 2, h, :], g_sb[:, h, :], h_hi[:, e % 2, h, :].bitcast(F32), ALU.subtract).then_inc(hidden_low_ok, 1)
                    if e:
                        take(base, c, e - 1)

        @block.tensor
        def _(pe):
            pe.wait_ge(q_ready, 1)
            for q, ps in ((q_wt, psA), (q_r, psB), (q_key, psC), (q_b, psD)):
                for half in range(2):
                    for c in range(TCH):
                        k = P if c < TCH - 1 else TLAST
                        m = pe.matmul(ps[:, 512 * half:512 * half + 512], q[0:k, c, :], tile_at[0:k, c, 512 * half:512 * half + 512],
                                      start=(c == 0), stop=(c == TCH - 1))
                m.then_inc(q_spread, 1)
            pe.wait_ge(q_used, 1)
            for k in range(CH):
                for c in range(TCH):
                    n = P if c < TCH - 1 else TLAST
                    m = pe.matmul(psA[:, k:k + 1], tile_at[0:n, c, P * k:P * k + P], t_of16[0:n, c:c + 1], start=(c == 0), stop=(c == TCH - 1))
            m.then_inc(q_spread, 1)
            def degrees():
                pe.wait_ge(window_node_hot_ok, W)
                pe.wait_ge(sel_ok, CH)
                for k in range(CH):
                    for d in range(W):
                        m = pe.matmul(psA[:, 64 + W * k + d:65 + W * k + d], r_hot[:, d, P * k:P * k + P], ones16[:, 0:1], start=True, stop=True)
                m.then_inc(step_degree_in, 1)
                pe.wait_ge(step_degree_ok, 1)
                for c in range(C):
                    for k in range(CH):
                        m = pe.matmul(psA[0:PT, 128 + W * c:128 + W * c + W], sel[:, k, PT * c:PT * c + PT], cnt[:, W * k:W * k + W],
                                      start=(k == 0), stop=(k == CH - 1))
                m.then_inc(degree_in, 1)

            pe.wait_ge(ident_ok, 1)
            pe.wait_ge(q_used, 4)

            def transposes(n):
                pe.wait_ge(xn_ok, n + 1)
                if n >= 2:
                    pe.wait_ge(xn_transposed_ok, n - 1)
                for k in range(2):
                    m = pe.transpose(psB[:, 512 * (n % 2) + P * k:512 * (n % 2) + P * k + PT], xn[0:PT, n, P * k:P * k + P], ident[0:PT, 0:PT])
                m.then_inc(xn_transposed, 1)

            def project(n):
                if n == 0:
                    pe.wait_ge(wcat_ok, 2)
                pe.wait_ge(xn_transposed_ok, n + 1)
                if n >= 2:
                    pe.wait_ge(projected_h_ok, n - 1)
                    pe.wait_ge(projected_qkv_ok, n - 1)
                for k in range(2):
                    m = pe.matmul(psC[0:PT, 512 * (n % 2):512 * (n % 2) + 512], xnT[:, n % 2, k, :], wcat[:, k, :], start=(k == 0), stop=(k == 1))
                m.then_inc(projected, 1)

            def build(g, j, slot, ps=psA):
                if j % 2 == 0:
                    pe.wait_ge(hot_ready, g + 2)
                bank = 512 * (j % 2)
                for q in range(GROUP):
                    m = pe.matmul(ps[:, bank + KEYS * q:bank + KEYS * q + KEYS], hot_b[:, slot, j % 2, :, q], hot_k[:, slot, j % 2, :, q],
                                  start=True, stop=True)
                m.then_inc(built, 1)

            pe.nop().then_inc(built, 4)
            transposes(0)
            for n in range(SLOTS):
                if n + 1 < SLOTS:
                    transposes(n + 1)
                project(n)
                if n == FIRST - 5:
                    degrees()
                if n >= FIRST:
                    for j in range(2):
                        g = 2 * (n - FIRST) + j
                        pe.wait_ge(counts_ok, g + 1)
                        build(g, j, (n - FIRST) % 2)

            def spread_scale(layer):
                pe.wait_ge(max_ok, layer + 1)
                pe.transpose(psD[0:1, 768:768 + PT], hs_max[0:PT, 0:1], ident[0:PT, 0:PT]).then_inc(max_in, 1)
                pe.wait_ge(pow_ok, layer + 1)
                pe.matmul(psD[:, 896:898], ones_row[:, :], top_hs[:, 2:4], start=True, stop=True).then_inc(pow_in, 1)

            pe.wait_ge(attention_dve, 1)
            pe.wait_ge(counts_ok, GROUPS + 2)
            pe.transpose(psA[:, 0:PT], kmax[0:PT, :], ident[0:PT, 0:PT]).then_inc(attention_pe, 1)
            pe.wait_ge(attention_dve, 3)
            pe.wait_ge(projected_qkv_ok, SLOTS)
            pe.transpose(psB[0:MEM, 0:P], mem_k[:], ident[:, :])
            pe.transpose(psB[0:MEM, 256:256 + P], mem_v[:], ident[:, :])
            pe.matmul(psA[:, 256:256 + P], kmax_mat[:], ident[:, :], start=True, stop=True).then_inc(attention_pe, 1)
            spread_scale(0)
            pe.wait_ge(attention_dve, 9)
            for n in range(SLOTS):
                if n % W == 0:
                    pe.wait_ge(k_exp, n // W + 1)
                pe.matmul(psB[:, 512:512 + P + 1], qkv[0:PT, n, HID:2 * HID], qkv[0:PT, n, 2 * HID:3 * HID + 1], start=(n == 0), stop=False)
            pe.wait_ge(k_exp, C + 1)
            pe.matmul(psB[:, 512:512 + P + 1], memkT[:], memvT[:], start=False, stop=True).then_inc(attention_pe, 1)
            pe.wait_ge(attention_dve, 13)
            pe.transpose(psB[:, 0:P], ctx_m[:], ident[:, :]).then_inc(attention_pe, 1)
            pe.wait_ge(attention_dve, 14)
            pe.matmul(psB[:, 256:256 + DIM], ctxT[:], wout[:], start=True, stop=True).then_inc(attention_pe, 1)
            pe.wait_ge(q_done, C)

            def q_transposes(g):
                if g >= 2:
                    pe.wait_ge(q_transposed_ok, g - 1)
                n0, tiles = TILE_GROUPS[g]
                for t in range(tiles):
                    m = pe.transpose(psD[:, 512 * (g % 2) + PT * t:512 * (g % 2) + PT * t + PT], qkv[0:PT, n0 + t, 0:HID], ident[0:PT, 0:PT])
                m.then_inc(q_transposed, 1)

            for k in range(2):
                pe.transpose(psD[:, EXPERTS * k:EXPERTS * k + EXPERTS], rw_nat[:, P * k:P * k + P], ident[0:EXPERTS, 0:EXPERTS])
            pe.transpose(psD[:, 128:128 + 2 * EXPERTS], eb1_nat[:], ident[0:2 * EXPERTS, 0:2 * EXPERTS]).then_inc(router_in, 1)
            pe.wait_ge(attention_pe, 5)
            pe.wait_ge(attention_dve, 15)
            pe.wait_ge(router_ok, 2)
            q_transposes(0)
            for g, (n0, tiles) in enumerate(TILE_GROUPS):
                if g + 1 < len(TILE_GROUPS):
                    q_transposes(g + 1)
                pe.wait_ge(q_transposed_ok, g + 1)
                if g >= 2:
                    pe.wait_ge(attended_ok, g - 1)
                for t in range(tiles):
                    m = pe.matmul((psC, psB)[g % 2][0:PT, DIM * t:DIM * t + DIM], qT[:, g % 2, PT * t:PT * t + PT], wmix[:], start=True, stop=True)
                m.then_inc(attended, 1)

            def add_slot(par, a, start):
                ca = counts5[0:PT, par, a, :, :]
                ha = hs2[0:PT, a, :, :]
                for d in range(W):
                    for part in range(2):
                        m = pe.matmul((psB, psC)[par][:, HID * d:HID * d + HID], ca[:, d, :], ha[:, part, :],
                                      start=start and part == 0 and d % 4 == 0, stop=part == 1, skip_group_check=True)
                return m

            def merge(c, used, ps=psD):
                pe.wait_ge(merge_used, used)
                for lo, hi in ((0, 512), (512, W * HID)):
                    for k in range(CH):
                        for part in range(2):
                            m = pe.matmul(ps[0:PT, lo:hi], sel[:, k, bass.ds(PT * c, PT)], part2[:, part, k, lo:hi],
                                          start=(k == 0 and part == 0), stop=(k == CH - 1 and part == 1))
                m.then_inc(merged, 1)

            pe.nop().then_inc(down, 2)
            pe.wait_ge(consts, 9)
            pe.nop().then_inc(second_in, 1)
            pe.nop().then_inc(summed, 1)
            pe.wait_ge(attended_ok, len(TILE_GROUPS))
            for layer in range(2):
                k0, g0 = CH * layer, GROUPS * (1 + CH * layer)
                if layer:
                    spread_scale(layer)
                def two_chunks(kp, last):
                    for par in range(2):
                        pe.wait_ge(counts_ok, 2 * GROUPS * kp + (g0 + GROUPS * par + 2))
                        pe.wait_ge(sums_low_ok, 2 * kp + (k0 + par + 1))
                        pe.wait_ge(hs_low_ok, C * layer + 1)
                        add_slot(par, 0, True)
                        due = 1
                        for j in range(0 if last and par else GROUPS):
                            g = 2 * GROUPS * kp + (g0 + GROUPS * par + j)
                            pe.wait_ge(counts_ok, g - 1)
                            build(g, j, j // 2 % 2, (psA, psD)[j // 2 % 2])
                            while GROUPS * due < (SLOTS - 3) * (j + 1):
                                if due % W == 0:
                                    pe.wait_ge(hs_low_ok, C * layer + due // W + 1)
                                add_slot(par, due, False)
                                due += 1
                        for a in range(due, SLOTS):
                            m = add_slot(par, a, False)
                        m.then_inc(summed, 1)

                with pe.Fori(0, CH // 2 - layer) as kp:
                    two_chunks(kp, False)
                if layer:
                    two_chunks(CH // 2 - 1, True)
                pe.wait_ge(sums_low_ok, k0 + CH + 1 + (1 - layer))
                if layer == 0:
                    pe.wait_ge(counts_ok, GROUPS * (CH + 1) + 2)
                    for c in range(C):
                        merge(c, max(c, 1), (psD, psA)[c % 2])

            def merge_transposed(c):
                if c:
                    pe.wait_ge(second_sums_ok, 2 * c)
                for d in range(W):
                    o = psD[:, PT * d:PT * d + PT] if d < 4 else psD[:, 512:512 + PT]
                    for part in range(2):
                        pe.matmul(o, hs2[0:PT, W * c + d, part, :], diag[0:PT, 0:PT], start=part == 0, stop=False)
                    for k in range(CH):
                        if k == CH - 1 and c == 0 and d == 0:
                            pe.wait_ge(sums_low_ok, 2 * CH + 2)
                        for part in range(2):
                            m = pe.matmul(o, part2[:, part, k, HID * d:HID * d + HID], sel[:, k, PT * c:PT * c + PT],
                                          start=False, stop=(k == CH - 1 and part == 1))
                m.then_inc(merged, 1)

            def times_w2(c):
                pe.wait_ge(second_sums_ok, 2 * c + 2)
                pe.wait_ge(second_ok, 2 * c + 2)
                for d in range(W):
                    o = psB[0:PT, DIM * d:DIM * d + DIM] if d < 4 else psC[0:PT, 0:DIM]
                    m = pe.matmul(o, aggT[:, d, 0:PT], w2g[:], start=True, stop=True)
                m.then_inc(second_in, 1)

            def token_transposes(c):
                pe.wait_ge(tok_ok, c + 1)
                pe.wait_ge(token_full_ok, 3 * c + 3)
                for j in range(2 * W):
                    o = psA[:, P * j:P * j + PT] if j < 8 else psC[:, 512 + P * (j - 8):512 + P * (j - 8) + PT]
                    m = pe.transpose(o, tok[0:PT, j % W, P * (j // W):P * (j // W) + P], ident[0:PT, 0:PT])
                m.then_inc(tok_transposed, 1)

            THREE = ((0, 0), (0, 1), (1, 0))

            def logits(c):
                pe.wait_ge(token_full_ok, 3 * c + 6)
                for d in range(W):
                    out_cols = psC[0:PT, bass.ds(768 + EXPERTS * W * c + EXPERTS * d, EXPERTS)]
                    for k in range(2):
                        m = pe.matmul(out_cols, tokT[:, k, PT * d:PT * d + PT], wr[:, k, :], start=(k == 0), stop=(k == 1))
                m.then_inc(logit_in, 1)

            merge_transposed(0)
            for c in range(C):
                times_w2(c)
                if c < C - 1:
                    merge_transposed(c + 1)
                if c >= 2:
                    logits(c - 2)
                if c >= 1:
                    token_transposes(c - 1)
            logits(C - 2)
            token_transposes(C - 1)
            logits(C - 1)

            def comb_transposes(g, tiles):
                if g == 0:
                    pe.wait_ge(comb3_ok, 1)
                if g >= 2:
                    pe.wait_ge(comb_transposed_ok, g - 1)
                for t in range(tiles):
                    m = pe.transpose(psA[0:96, 512 * (g % 2) + PT * t:512 * (g % 2) + PT * t + PT], comb3[0:PT, 4 * g + t, :], ident[0:PT, 0:PT])
                m.then_inc(comb_transposed, 1)

            def bias2(g, tiles):
                pe.wait_ge(comb_transposed_ok, g + 1)
                if g >= 2:
                    pe.wait_ge(bias2_ok, g - 1)
                for t in range(tiles):
                    m = pe.matmul((psC, psD)[g % 2][0:PT, DIM * t:DIM * t + DIM], combT[:, g % 2, PT * t:PT * t + PT], eb2[:], start=True, stop=True)
                m.then_inc(bias2_in, 1)

            comb_transposes(0, 4)
            for g in range(7):
                if g < 6:
                    comb_transposes(g + 1, 4 if g < 5 else 1)
                bias2(g, 4 if g < 6 else 1)

            def up(E, c, e):
                for h in range(2):
                    pe.wait_ge(hidden_ok, 2 * E + (h + 3))
                    for n, (at, size, _) in enumerate(HALVES):
                        for i, (a, b) in enumerate(THREE):
                            for k in range(2):
                                m = pe.matmul((psA, psB)[h][:, 512 * n:512 * n + size], (w_hi, w_lo)[a][:, 0, e, k, P * h:P * h + P],
                                              (tokT_hi, tokT_lo)[b][:, k, bass.ds(W * PT * c + at, size)],
                                              start=(i == 0 and k == 0), stop=(i == 2 and k == 1))
                    m.then_inc(upped, 1)

            pe.wait_ge(w_lo_ok, 2)
            pe.wait_ge(bias2_ok, 7)
            with pe.Fori(0, C) as c:
                base = EXPERTS * c
                for e in range(EXPERTS + 1):
                    if e < EXPERTS:
                        up(base + e, c, e)
                    if e:
                        f = e - 1
                        pe.wait_ge(hidden_low_ok, 2 * base + (2 * f + 6))
                        for d in range(W):
                            if d % 2 == 0:
                                pe.wait_ge(weighted, 3 * base + (3 * f + d // 2 + 1))
                            for i, (a, b) in enumerate(THREE):
                                for k in range(2):
                                    m = pe.matmul(out_place(f, d),
                                                  (h_hi, h_lo)[a][:, f % 2, k, PT * d:PT * d + PT], (w_hi, w_lo)[b][:, 1, f, k, :],
                                                  start=(i == 0 and k == 0), stop=(i == 2 and k == 1))
                        m.then_inc(down, 1)

        @block.scalar
        def _(act):
            sa = Steps(act, scalar_done)
            act.wait_ge(var_ok, 1)
            act.activation(small[0:PT, 3, :], small[0:PT, 2, :], ACT.Sqrt).then_inc(std_ok, 1)
            act.wait_ge(xn_square_ok, 1)
            act.activation(xnorm[0:PT, :], xnorm[0:PT, :], ACT.Sqrt).then_inc(std_ok, 1)
            act.wait_ge(xnorm_ok, 1)
            act.nop().then_inc(counts_ok, 2)

            def xn_copy(n):
                act.wait_ge(xn_transposed, n + 1)
                if n >= 2:
                    act.wait_ge(projected, n - 1)
                act.copy(xnT[:, n % 2, :, :], psB[:, 512 * (n % 2):512 * (n % 2) + 256].rearrange("p (k q) -> p k q", k=2)[:, :, 0:PT]).then_inc(xn_transposed_ok, 1)

            def q_exponential(c):
                act.wait_ge(q_sub, c + 1)
                act.activation(qkv[0:PT, W * c:W * c + W, 0:HID], qkv[0:PT, W * c:W * c + W, 0:HID], ACT.Exp).then_inc(q_exp, 1)

            def take_counts(g, par, j, col, ps=psA):
                act.wait_ge(built, g + 5)
                act.copy(counts[:, par, :, bass.ds(col, GROUP)].rearrange("p j s -> p s j"),
                         ps[:, 512 * (j % 2):512 * (j % 2) + GROUP * KEYS].rearrange("p (s j) -> p s j", s=GROUP)).then_inc(counts_ok, 1)

            xn_copy(0)
            for n in range(SLOTS):
                if n + 1 < SLOTS:
                    xn_copy(n + 1)
                act.wait_ge(projected, n + 1)
                act.copy(hs[0:PT, n, :], psC[0:PT, 512 * (n % 2):512 * (n % 2) + HID]).then_inc(projected_h_ok, 1)
                act.activation(qkv[0:PT, n, 0:QKV], psC[0:PT, 512 * (n % 2) + HID:512 * (n % 2) + 512], ACT.Copy,
                               scale=xnorm[0:PT, n:n + 1]).then_inc(projected_qkv_ok, 1)
                if n == FIRST - 4:
                    act.wait_ge(degree_ok, 1)
                    act.activation(small[0:PT, 1, :], small[0:PT, 0, :], ACT.Sqrt).then_inc(degree_root_ok, 1)
                if n >= FIRST:
                    for j in range(2):
                        g = 2 * (n - FIRST) + j
                        take_counts(g, 0, j, GROUP * g)
                if n > FIRST + 2 and n % W == 2:
                    q_exponential(n // W - 2)
            q_exponential(C - 2)
            q_exponential(C - 1)
            for c in range(C):
                act.wait_ge(k_sub, c + 1)
                act.activation(qkv[0:PT, W * c:W * c + W, HID:2 * HID], qkv[0:PT, W * c:W * c + W, HID:2 * HID], ACT.Exp).then_inc(k_exp, 1)
            act.wait_ge(attention_dve, 6)
            act.activation(memkT[:], memkT[:], ACT.Exp).then_inc(k_exp, 1)
            def hs_high(layer):
                act.wait_ge(scale_ok, layer + 1)
                with act.Fori(0, C) as c:
                    act.activation(hs2[0:PT, bass.ds(W * c, W), 0, :], hs[0:PT, bass.ds(W * c, W), :], ACT.Copy, scale=scale[0:PT, 0:1]).then_inc(hs_high_ok, 1)

            hs_high(0)

            def squares(g):
                act.wait_ge(attended_ok, g + 1)
                for n in range(4 * g, min(4 * g + 4, SLOTS)):
                    sa.did(act.activation(xn[0:PT, n, :], mix[0:PT, n, :], ACT.Square, accum_out=small[0:PT, 2, n:n + 1]))

            act.wait_ge(xn_free, 1)
            for g, (n0, tiles) in enumerate(TILE_GROUPS):
                act.wait_ge(q_transposed, g + 1)
                if g >= 2:
                    act.wait_ge(attended, g - 1)
                act.copy(qT[:, g % 2, 0:PT * tiles], psD[:, 512 * (g % 2):512 * (g % 2) + PT * tiles]).then_inc(q_transposed_ok, 1)
                if g >= 2:
                    squares(g - 2)
            squares(len(TILE_GROUPS) - 2)
            squares(len(TILE_GROUPS) - 1)
            sa.wait()
            act.activation(small[0:PT, 3, :], small[0:PT, 2, :], ACT.Sqrt).then_inc(attended_norm_ok, 1)

            act.nop().then_inc(hidden_ok, 4)
            act.nop().then_inc(token_full_ok, 3)
            act.preload_act_table(ACT.Copy)

            act.wait_ge(acc_xn_ok, 1)
            for layer in range(2):
                k0, g0 = CH * layer, GROUPS * (1 + CH * layer)
                if layer:
                    act.wait_ge(merged, C)
                def two_chunks(kp, last):
                    for par in range(2):
                        if not (last and par):
                            act.wait_ge(summed, 2 * kp + (k0 + par + 1))
                            with act.Fori(0, 8) as i:
                                for j in range(4):
                                    take_counts(2 * GROUPS * kp + 4 * i + (g0 + GROUPS * par + j), 1 - par, j, 4 * GROUP * i + GROUP * j,
                                                (psA, psD)[j // 2])
                        act.wait_ge(summed, 2 * kp + (k0 + par + 2))
                        act.activation(part2[:, 0, bass.ds(2 * kp + par, 1), :].rearrange("p a f -> p (a f)"), (psB, psC)[par][:, 0:W * HID],
                                       ACT.Copy, scale=1.0 / P).then_inc(sums_high_ok, 1)

                with act.Fori(0, CH // 2 - layer) as kp:
                    two_chunks(kp, False)
                if layer:
                    two_chunks(CH // 2 - 1, True)
                if layer == 0:
                    hs_high(1)

            def agg_copy(c):
                act.wait_ge(merged, C + c + 1)
                act.wait_ge(second_in, c + 1)
                act.copy(aggT[:, 0:4, 0:PT], psD[:, 0:4 * PT].rearrange("p (d q) -> p d q", d=4)).then_inc(second_sums_ok, 1)
                act.copy(aggT[:, 4, 0:PT], psD[:, 512:512 + PT]).then_inc(second_sums_ok, 1)

            def std(c):
                act.wait_ge(var_ok, c + 2)
                act.activation(small[0:PT, 3, 0:W], small[0:PT, 2, 0:W], ACT.Sqrt).then_inc(std_ok, 1)

            def token_high(c):
                act.wait_ge(tok_transposed, c + 1)
                if c:
                    act.wait_ge(logit_in, c)
                    act.wait_ge(token_low_ok, c)
                for k, d0, d1, ps in TOKEN_PARTS:
                    act.copy(tokT[:, k, PT * d0:PT * d1].rearrange("p (d q) -> p d q", q=PT),
                             ps.rearrange("p (d q) -> p d q", q=P)[:, :, 0:PT]).then_inc(token_full_ok, 1)
                act.wait_ge(token_full_ok, 3 * c + 6)
                act.copy(tokT_hi[:, :, W * PT * c:W * PT * (c + 1)], tokT[:]).then_inc(token_high_ok, 1)

            def weights_high(i):
                act.wait_ge((in_w1, in_w2)[i], 16)
                act.copy(w_hi[:, i], w_raw[:, i]).then_inc(w_hi_ok, 1)

            agg_copy(0)
            for c in range(C):
                std(c)
                if c < C - 1:
                    agg_copy(c + 1)
                if c:
                    token_high(c - 1)
                if c == 1:
                    weights_high(1)
                if c == C - 2:
                    act.wait_ge(merged, 2 * C)
                    weights_high(0)
            token_high(C - 1)

            act.wait_ge(logit_ok, 1)
            act.activation(prob[0:PT], prob[0:PT], ACT.Exp).then_inc(prob_exp, 1)
            for g in range(7):
                size = PT * (4 if g < 6 else 1)
                act.wait_ge(comb_transposed, g + 1)
                if g >= 2:
                    act.wait_ge(bias2_in, g - 1)
                act.copy(combT[:, g % 2, 0:size], psA[0:96, 512 * (g % 2):512 * (g % 2) + size]).then_inc(comb_transposed_ok, 1)
            act.preload_act_table(ACT.Gelu)
            act.wait_ge(router_ok, 2)

            with act.Fori(0, C) as c:
                base = EXPERTS * c
                for e in range(EXPERTS):
                    act.wait_ge(down, base + (e + 1))
                    for h in range(2):
                        act.wait_ge(upped, 2 * base + (2 * e + h + 1))
                        act.wait_ge(hidden_low_ok, 2 * base + (2 * e + h + 3))
                        for n, (at, size, had) in enumerate(HALVES):
                            g = act.activation(g_sb[:, h, at + had:at + size], (psA, psB)[h][:, 512 * n + had:512 * n + size], ACT.Gelu,
                                               bias=eb1[:, 2 * e + h:2 * e + h + 1])
                        g.then_inc(hidden_ok, 1)
                    for h in range(2):
                        act.wait_ge(hidden_ok, 2 * base + (2 * e + h + 5))
                        act.copy(h_hi[:, e % 2, h, :], g_sb[:, h, :]).then_inc(hidden_high_ok, 1)


_INS = ['x', 'src', 'dst', 'L0_gnn_W1', 'L0_gnn_b1', 'L0_gnn_W2', 'L0_gnn_b2', 'L0_mix_w_qkv', 'L0_mix_mem_kv', 'L0_mix_w_out',
        'L0_mix_b_out', 'L0_mix_g_out', 'L0_mix_g_pre', 'L0_ffn_router_w', 'L0_ffn_w1', 'L0_ffn_b1', 'L0_ffn_w2', 'L0_ffn_b2']
_OUTS = [((NODES, DIM), 'float32')]


def kernel(**inputs):
    import numpy as _np
    import concourse.bacc as _bacc
    from concourse import mybir as _mybir
    from concourse.bass_utils import run_bass_kernel_spmd as _run

    nc = _bacc.Bacc("TRN2", target_bir_lowering=False, num_devices=1)
    arrays, args = {}, []
    for name in _INS:
        a = _np.ascontiguousarray(inputs[name])
        arrays[f"in_{name}_dram"] = a
        args.append(nc.dram_tensor(f"in_{name}_dram", a.shape, _mybir.dt.from_np(a.dtype), kind="ExternalInput").ap())
    for i, (shape, dtype) in enumerate(_OUTS):
        dt = _mybir.dt.from_np(_np.dtype(dtype))
        args.append(nc.dram_tensor(f"out_{i}_dram", shape, dt, kind="ExternalOutput").ap())
    gps_layer(nc, *args)
    r = _run(nc, [arrays], core_ids=[0])
    got = tuple(r.results[0][f"out_{i}_dram"] for i in range(len(_OUTS)))
    return got[0]
```
